# Optimizing a Trainium2 kernel written in Bass

```python
import numpy as np
import jax
import jax.numpy as jnp

def _softmax(x, axis=-1):
    return jax.nn.softmax(x, axis=axis)

def _gelu(x):
    return jax.nn.gelu(x, approximate=True)

def _silu(x):
    return jax.nn.silu(x)

def _sigmoid(x):
    return jax.nn.sigmoid(x)

def _layernorm(x, axis=-1, eps=1e-05):
    m = jnp.mean(x, axis=axis, keepdims=True)
    v = jnp.var(x, axis=axis, keepdims=True)
    return (x - m) / jnp.sqrt(v + eps)

def _scatter_add(tgt, idx, src, axis=0):
    return tgt.at[idx].add(src)

def _segment_sum(src, seg, n):
    return jax.ops.segment_sum(src, seg, n)
kernel_name = 'mk_prb_d4_jaxref_r8_d00b11'

def setup_inputs(seed: int=0):
    np.random.seed(seed)
    _w = jnp.asarray

    def _L0_attn_setup():
        import jax, jax.numpy as jnp
        import numpy as np
        B, T, D = (2, 256, 256)
        H, LAT, RD = (16, 64, 64)
        HD = D // H

        def _rope_tables(rd, max_t, theta=10000.0):
            freqs = 1.0 / theta ** (np.arange(0, rd, 2, dtype=np.float32) / rd)
            t = np.arange(max_t, dtype=np.float32)
            ang = np.outer(t, freqs)
            cos = np.tile(np.cos(ang), (1, 2))
            sin = np.tile(np.sin(ang), (1, 2))
            return (jnp.asarray(cos), jnp.asarray(sin))

        def _rotate_half(x):
            d = x.shape[-1] // 2
            return jnp.concatenate([-x[..., d:], x[..., :d]], axis=-1)

        def _apply_rope(x, cos, sin):
            t = x.shape[2]
            return x * cos[:t][None, None] + _rotate_half(x) * sin[:t][None, None]
        key = jax.random.key(seed)
        ks = jax.random.split(key, 9)
        s = 0.02
        return {'x': jax.random.normal(ks[0], (B, T, D), jnp.float32), 'Wqd': jax.random.normal(ks[1], (D, LAT), jnp.float32) * s, 'Wqu': jax.random.normal(ks[2], (LAT, D), jnp.float32) * s, 'Wqr': jax.random.normal(ks[3], (LAT, H * RD), jnp.float32) * s, 'Wkvd': jax.random.normal(ks[4], (D, LAT), jnp.float32) * s, 'Wku': jax.random.normal(ks[5], (LAT, D), jnp.float32) * s, 'Wvu': jax.random.normal(ks[6], (LAT, D), jnp.float32) * s, 'Wkr': jax.random.normal(ks[7], (D, RD), jnp.float32) * s, 'Wo': jax.random.normal(ks[8], (D, D), jnp.float32) * s}
    _L0_attn_in = _L0_attn_setup()

    def _L0_ffn_setup():
        import jax, jax.numpy as jnp
        import numpy as np
        import math
        N_EMBD = 256
        N_HEAD = 16
        HEAD_DIM = N_EMBD // N_HEAD
        B, T = (2, 256)
        key = jax.random.key(seed)
        k1, k2, k3 = jax.random.split(key, 3)
        x = jax.random.normal(k1, (B, T, N_EMBD), dtype=jnp.float32)
        W_gate = jax.random.normal(k2, (N_HEAD, N_EMBD), dtype=jnp.float32) * 0.02
        W_qkv = jax.random.normal(k3, (3 * N_EMBD, N_EMBD), dtype=jnp.float32) * 0.02
        return {'x': x, 'W_gate': W_gate, 'W_qkv': W_qkv}
    _L0_ffn_in = _L0_ffn_setup()

    def _L1_attn_setup():
        import jax, jax.numpy as jnp
        import numpy as np
        H = 256
        Q_RANK = 32
        SCALE = float(np.sqrt(Q_RANK))
        key = jax.random.key(seed)
        k_x, k_s, k_a, k_o, k_b = jax.random.split(key, 5)
        B, L = (4, 512)
        x = jax.random.normal(k_x, (B, L, H), dtype=jnp.float32)
        Ws = jax.random.normal(k_s, (H, Q_RANK), dtype=jnp.float32) / np.sqrt(H)
        Wa = jax.random.normal(k_a, (H, Q_RANK), dtype=jnp.float32) / np.sqrt(H)
        Wo = jax.random.normal(k_o, (H, H), dtype=jnp.float32) / np.sqrt(H)
        bo = jax.random.normal(k_b, (H,), dtype=jnp.float32) * 0.01
        return {'x': x, 'Ws': Ws, 'Wa': Wa, 'Wo': Wo, 'bo': bo}
    _L1_attn_in = _L1_attn_setup()

    def _L1_ffn_setup():
        import jax, jax.numpy as jnp
        import numpy as np
        HIDDEN = 256
        INTER = 1024
        SCALE = 64.0

        def fwht(x):
            orig_shape = x.shape
            n = orig_shape[-1]
            x = x.reshape(-1, n)
            h = 1
            while h < n:
                x = x.reshape(-1, n // (2 * h), 2, h)
                a, b = (x[:, :, 0, :], x[:, :, 1, :])
                x = jnp.stack([a + b, a - b], axis=2).reshape(-1, n)
                h *= 2
            return (x / jnp.sqrt(jnp.asarray(n, x.dtype))).reshape(orig_shape)
        key = jax.random.key(seed)
        ks = jax.random.split(key, 8)
        inp = jax.random.normal(ks[0], (4, 256, HIDDEN), dtype=jnp.float32)
        SU_ug = jnp.where(jax.random.bernoulli(ks[1], 0.5, (HIDDEN,)), 1.0, -1.0).astype(jnp.float32)
        SU_dp = jnp.where(jax.random.bernoulli(ks[2], 0.5, (INTER,)), 1.0, -1.0).astype(jnp.float32)
        Wscale_ug = jax.random.uniform(ks[3], (2 * INTER,), jnp.float32, 0.5, 1.5)
        Wscale_dp = jax.random.uniform(ks[4], (HIDDEN,), jnp.float32, 0.5, 1.5)
        W_up = jax.random.normal(ks[5], (INTER, HIDDEN), dtype=jnp.float32) * 0.02
        W_gate = jax.random.normal(ks[6], (INTER, HIDDEN), dtype=jnp.float32) * 0.02
        W_down = jax.random.normal(ks[7], (HIDDEN, INTER), dtype=jnp.float32) * 0.02
        return {'input': inp, 'SU_ug': SU_ug, 'SU_dp': SU_dp, 'Wscale_ug': Wscale_ug, 'Wscale_dp': Wscale_dp, 'W_up': W_up, 'W_gate': W_gate, 'W_down': W_down}
    _L1_ffn_in = _L1_ffn_setup()

    def _L2_attn_setup():
        import jax, jax.numpy as jnp
        import numpy as np
        HIDDEN = 256
        NUM_HEADS = 16
        HEAD_DIM = HIDDEN // NUM_HEADS
        BATCH = 4
        SEQ = 256
        key = jax.random.key(seed)
        k1, k2, k3 = jax.random.split(key, 3)
        x = jax.random.normal(k1, (BATCH, SEQ, HIDDEN), dtype=jnp.float32)
        w_qkv = jax.random.normal(k2, (3 * HIDDEN, HIDDEN), dtype=jnp.float32) * HIDDEN ** (-0.5)
        w_out = jax.random.normal(k3, (HIDDEN, HIDDEN), dtype=jnp.float32) * HIDDEN ** (-0.5)
        return {'x': x, 'w_qkv': w_qkv, 'w_out': w_out}
    _L2_attn_in = _L2_attn_setup()

    def _L2_ffn_setup():
        import jax, jax.numpy as jnp
        import numpy as np
        N_EXPERTS = 8
        TOP_K = 2
        C = 256
        H = 128
        HS = 256
        B, T = (1, 64)
        SCALE = 0.02
        key = jax.random.key(seed)
        ks = jax.random.split(key, 10)
        x = jax.random.normal(ks[0], (B, T, C), dtype=jnp.float32)
        gate_w = jax.random.normal(ks[1], (N_EXPERTS, C), dtype=jnp.float32) * SCALE
        w_gate = jax.random.normal(ks[2], (N_EXPERTS, H, C), dtype=jnp.float32) * SCALE
        w_up = jax.random.normal(ks[3], (N_EXPERTS, H, C), dtype=jnp.float32) * SCALE
        w_down = jax.random.normal(ks[4], (N_EXPERTS, C, H), dtype=jnp.float32) * SCALE
        sh_gate = jax.random.normal(ks[5], (HS, C), dtype=jnp.float32) * SCALE
        sh_up = jax.random.normal(ks[6], (HS, C), dtype=jnp.float32) * SCALE
        sh_down = jax.random.normal(ks[7], (C, HS), dtype=jnp.float32) * SCALE
        se_gate_w = jax.random.normal(ks[8], (1, C), dtype=jnp.float32) * SCALE
        return {'x': x, 'gate_w': gate_w, 'w_gate': w_gate, 'w_up': w_up, 'w_down': w_down, 'sh_gate': sh_gate, 'sh_up': sh_up, 'sh_down': sh_down, 'se_gate_w': se_gate_w}
    _L2_ffn_in = _L2_ffn_setup()

    def _L3_attn_setup():
        import jax, jax.numpy as jnp
        import numpy as np
        DIM = 256
        key = jax.random.key(seed)
        ks = jax.random.split(key, 9)
        scale = 1.0 / np.sqrt(DIM)
        x = jax.random.normal(ks[0], (4, 512, DIM), dtype=jnp.float32)

        def lin(kw, kb):
            W = jax.random.uniform(kw, (DIM, DIM), jnp.float32, -scale, scale)
            b = jax.random.uniform(kb, (DIM,), jnp.float32, -scale, scale)
            return (W, b)
        Wq, bq = lin(ks[1], ks[2])
        Wk, bk = lin(ks[3], ks[4])
        Wv, bv = lin(ks[5], ks[6])
        Wg, bg = lin(ks[7], ks[8])
        return {'x': x, 'Wq': Wq, 'bq': bq, 'Wk': Wk, 'bk': bk, 'Wv': Wv, 'bv': bv, 'Wg': Wg, 'bg': bg}
    _L3_attn_in = _L3_attn_setup()

    def _L3_ffn_setup():
        import jax, jax.numpy as jnp
        import numpy as np
        EPS = 1e-08

        def _quantize(w):
            gamma = jnp.mean(jnp.abs(w))
            return jnp.clip(jnp.round(w / (gamma + EPS)), -1.0, 1.0)

        def _bitlinear(x, w):
            return jnp.matmul(x, _quantize(w).T)
        key = jax.random.key(seed)
        k1, k2, k3, k4 = jax.random.split(key, 4)
        d, h = (256, 704)
        x = jax.random.normal(k1, (4, 256, d), dtype=jnp.float32)
        w1 = jax.random.normal(k2, (h, d), dtype=jnp.float32)
        w2 = jax.random.normal(k3, (h, d), dtype=jnp.float32)
        w3 = jax.random.normal(k4, (d, h), dtype=jnp.float32)
        return {'x': x, 'w1': w1, 'w2': w2, 'w3': w3}
    _L3_ffn_in = _L3_ffn_setup()
    _d = {'L0_attn_x': _L0_attn_in['x'], 'L0_attn_Wqd': _L0_attn_in['Wqd'], 'L0_attn_Wqu': _L0_attn_in['Wqu'], 'L0_attn_Wqr': _L0_attn_in['Wqr'], 'L0_attn_Wkvd': _L0_attn_in['Wkvd'], 'L0_attn_Wku': _L0_attn_in['Wku'], 'L0_attn_Wvu': _L0_attn_in['Wvu'], 'L0_attn_Wkr': _L0_attn_in['Wkr'], 'L0_attn_Wo': _L0_attn_in['Wo'], 'L0_ffn_W_gate': _L0_ffn_in['W_gate'], 'L0_ffn_W_qkv': _L0_ffn_in['W_qkv'], 'L1_attn_Ws': _L1_attn_in['Ws'], 'L1_attn_Wa': _L1_attn_in['Wa'], 'L1_attn_Wo': _L1_attn_in['Wo'], 'L1_attn_bo': _L1_attn_in['bo'], 'L1_ffn_SU_ug': _L1_ffn_in['SU_ug'], 'L1_ffn_SU_dp': _L1_ffn_in['SU_dp'], 'L1_ffn_Wscale_ug': _L1_ffn_in['Wscale_ug'], 'L1_ffn_Wscale_dp': _L1_ffn_in['Wscale_dp'], 'L1_ffn_W_up': _L1_ffn_in['W_up'], 'L1_ffn_W_gate': _L1_ffn_in['W_gate'], 'L1_ffn_W_down': _L1_ffn_in['W_down'], 'L2_attn_w_qkv': _L2_attn_in['w_qkv'], 'L2_attn_w_out': _L2_attn_in['w_out'], 'L2_ffn_gate_w': _L2_ffn_in['gate_w'], 'L2_ffn_w_gate': _L2_ffn_in['w_gate'], 'L2_ffn_w_up': _L2_ffn_in['w_up'], 'L2_ffn_w_down': _L2_ffn_in['w_down'], 'L2_ffn_sh_gate': _L2_ffn_in['sh_gate'], 'L2_ffn_sh_up': _L2_ffn_in['sh_up'], 'L2_ffn_sh_down': _L2_ffn_in['sh_down'], 'L2_ffn_se_gate_w': _L2_ffn_in['se_gate_w'], 'L3_attn_Wq': _L3_attn_in['Wq'], 'L3_attn_bq': _L3_attn_in['bq'], 'L3_attn_Wk': _L3_attn_in['Wk'], 'L3_attn_bk': _L3_attn_in['bk'], 'L3_attn_Wv': _L3_attn_in['Wv'], 'L3_attn_bv': _L3_attn_in['bv'], 'L3_attn_Wg': _L3_attn_in['Wg'], 'L3_attn_bg': _L3_attn_in['bg'], 'L3_ffn_w1': _L3_ffn_in['w1'], 'L3_ffn_w2': _L3_ffn_in['w2'], 'L3_ffn_w3': _L3_ffn_in['w3']}
    _x0 = _d['L0_attn_x']
    _d['L0_attn_x'] = jax.random.normal(jax.random.fold_in(jax.random.key(seed), 1), (1, 1024, 256), dtype=_x0.dtype)
    del _x0
    return _d

def reference(L0_attn_x, L0_attn_Wqd, L0_attn_Wqu, L0_attn_Wqr, L0_attn_Wkvd, L0_attn_Wku, L0_attn_Wvu, L0_attn_Wkr, L0_attn_Wo, L0_ffn_W_gate, L0_ffn_W_qkv, L1_attn_Ws, L1_attn_Wa, L1_attn_Wo, L1_attn_bo, L1_ffn_SU_ug, L1_ffn_SU_dp, L1_ffn_Wscale_ug, L1_ffn_Wscale_dp, L1_ffn_W_up, L1_ffn_W_gate, L1_ffn_W_down, L2_attn_w_qkv, L2_attn_w_out, L2_ffn_gate_w, L2_ffn_w_gate, L2_ffn_w_up, L2_ffn_w_down, L2_ffn_sh_gate, L2_ffn_sh_up, L2_ffn_sh_down, L2_ffn_se_gate_w, L3_attn_Wq, L3_attn_bq, L3_attn_Wk, L3_attn_bk, L3_attn_Wv, L3_attn_bv, L3_attn_Wg, L3_attn_bg, L3_ffn_w1, L3_ffn_w2, L3_ffn_w3):

    def _L0_attn_ref(x, Wqd, Wqu, Wqr, Wkvd, Wku, Wvu, Wkr, Wo):
        import jax, jax.numpy as jnp
        import numpy as np
        B, T, D = (2, 256, 256)
        H, LAT, RD = (16, 64, 64)
        HD = D // H

        def _rope_tables(rd, max_t, theta=10000.0):
            freqs = 1.0 / theta ** (np.arange(0, rd, 2, dtype=np.float32) / rd)
            t = np.arange(max_t, dtype=np.float32)
            ang = np.outer(t, freqs)
            cos = np.tile(np.cos(ang), (1, 2))
            sin = np.tile(np.sin(ang), (1, 2))
            return (jnp.asarray(cos), jnp.asarray(sin))

        def _rotate_half(x):
            d = x.shape[-1] // 2
            return jnp.concatenate([-x[..., d:], x[..., :d]], axis=-1)

        def _apply_rope(x, cos, sin):
            t = x.shape[2]
            return x * cos[:t][None, None] + _rotate_half(x) * sin[:t][None, None]
        b, t, d = x.shape
        cos, sin = _rope_tables(RD, t)
        ql = x @ Wqd
        q = (ql @ Wqu).reshape(b, t, H, HD).transpose(0, 2, 1, 3)
        qr = (ql @ Wqr).reshape(b, t, H, RD).transpose(0, 2, 1, 3)
        qr = _apply_rope(qr, cos, sin)
        ckv = x @ Wkvd
        k = (ckv @ Wku).reshape(b, t, H, HD).transpose(0, 2, 1, 3)
        v = (ckv @ Wvu).reshape(b, t, H, HD).transpose(0, 2, 1, 3)
        kr = _apply_rope((x @ Wkr)[:, None], cos, sin)[:, 0]
        scale = 1.0 / jnp.sqrt(jnp.float32(HD + RD))
        scores = (jnp.einsum('bhtd,bhsd->bhts', q, k) + jnp.einsum('bhtd,bsd->bhts', qr, kr)) * scale
        causal = jnp.tril(jnp.ones((t, t), dtype=bool))
        scores = jnp.where(causal[None, None], scores, jnp.float32(-jnp.inf))
        attn = jax.nn.softmax(scores, axis=-1)
        out = jnp.einsum('bhts,bhsd->bhtd', attn, v)
        out = out.transpose(0, 2, 1, 3).reshape(b, t, d)
        return out @ Wo

    def _L0_ffn_ref(x, W_gate, W_qkv):
        import jax, jax.numpy as jnp
        import numpy as np
        import math
        N_EMBD = 256
        N_HEAD = 16
        HEAD_DIM = N_EMBD // N_HEAD
        B, T = (2, 256)
        Bb, Tt, C = x.shape
        H, hd = (N_HEAD, HEAD_DIM)
        gating = jax.nn.softmax(x @ W_gate.T, axis=-1)
        idx = jnp.argmax(gating, axis=-1)
        indicator = jax.nn.one_hot(idx, H, dtype=gating.dtype)
        top1_val = jnp.max(gating, axis=-1, keepdims=True)
        gating_top1 = indicator * top1_val
        qkv = x @ W_qkv.T
        q, k, v = jnp.split(qkv, 3, axis=-1)
        k = k.reshape(Bb, Tt, H, hd)
        v = v.reshape(Bb, Tt, H, hd)
        k_shared = jnp.einsum('bth,bthd->btd', indicator, k)
        v_shared = jnp.einsum('bth,bthd->btd', gating_top1, v)
        q = q.reshape(Bb, Tt, H, hd).transpose(0, 2, 1, 3)
        att = jnp.einsum('bhqd,bkd->bhqk', q, k_shared) * (1.0 / math.sqrt(hd))
        causal = jnp.tril(jnp.ones((Tt, Tt), dtype=bool))
        att = jnp.where(causal[None, None, :, :], att, -jnp.inf)
        att = jax.nn.softmax(att, axis=-1)
        y = jnp.einsum('bhqk,bkd->bhqd', att, v_shared)
        y = y.transpose(0, 2, 1, 3).reshape(Bb, Tt, C)
        return y

    def _L1_attn_ref(x, Ws, Wa, Wo, bo):
        import jax, jax.numpy as jnp
        import numpy as np
        H = 256
        Q_RANK = 32
        SCALE = float(np.sqrt(Q_RANK))
        B, L, _ = x.shape
        state = jnp.einsum('blh,hr->blr', x, Ws)
        action = jnp.einsum('blh,hr->blr', x, Wa)
        q_values = jnp.einsum('bir,bjr->bij', state, action) / SCALE
        causal = jnp.tril(jnp.ones((L, L), dtype=bool))
        q_values = jnp.where(causal, q_values, -jnp.inf)
        weights = jax.nn.softmax(q_values, axis=-1)
        out = jnp.einsum('bij,bjh->bih', weights, x)
        return jnp.einsum('bih,ho->bio', out, Wo.T) + bo

    def _L1_ffn_ref(input, SU_ug, SU_dp, Wscale_ug, Wscale_dp, W_up, W_gate, W_down):
        import jax, jax.numpy as jnp
        import numpy as np
        HIDDEN = 256
        INTER = 1024
        SCALE = 64.0

        def fwht(x):
            orig_shape = x.shape
            n = orig_shape[-1]
            x = x.reshape(-1, n)
            h = 1
            while h < n:
                x = x.reshape(-1, n // (2 * h), 2, h)
                a, b = (x[:, :, 0, :], x[:, :, 1, :])
                x = jnp.stack([a + b, a - b], axis=2).reshape(-1, n)
                h *= 2
            return (x / jnp.sqrt(jnp.asarray(n, x.dtype))).reshape(orig_shape)
        n = SU_ug.shape[0]
        x = input.reshape(-1, n)
        x = fwht(x * SU_ug) / SCALE
        x_up = x @ W_up.T * (Wscale_ug[:INTER] * SCALE)
        x_gate = x @ W_gate.T * (Wscale_ug[INTER:] * SCALE)
        x = jax.nn.silu(x_gate) * x_up
        x = fwht(x * SU_dp) / SCALE
        x = x @ W_down.T * (Wscale_dp * SCALE)
        return x.reshape(input.shape)

    def _L2_attn_ref(x, w_qkv, w_out):
        import jax, jax.numpy as jnp
        import numpy as np
        HIDDEN = 256
        NUM_HEADS = 16
        HEAD_DIM = HIDDEN // NUM_HEADS
        BATCH = 4
        SEQ = 256
        B, S, H = x.shape
        nh, hd = (NUM_HEADS, HEAD_DIM)
        qkv = jnp.einsum('bsh,oh->bso', x, w_qkv)
        q, k, v = jnp.split(qkv, 3, axis=-1)
        q = q.reshape(B, S, nh, hd).transpose(0, 2, 1, 3)
        k = k.reshape(B, S, nh, hd).transpose(0, 2, 1, 3)
        v = v.reshape(B, S, nh, hd).transpose(0, 2, 1, 3)
        scale = hd ** (-0.5)
        scores = jnp.einsum('bhqd,bhkd->bhqk', q, k) * scale
        causal = jnp.tril(jnp.ones((S, S), dtype=bool))
        scores = jnp.where(causal, scores, jnp.finfo(scores.dtype).min)
        attn = jax.nn.softmax(scores, axis=-1)
        out = jnp.einsum('bhqk,bhkd->bhqd', attn, v)
        out = out.transpose(0, 2, 1, 3).reshape(B, S, H)
        return jnp.einsum('bsh,oh->bso', out, w_out)

    def _L2_ffn_ref(x, gate_w, w_gate, w_up, w_down, sh_gate, sh_up, sh_down, se_gate_w):
        import jax, jax.numpy as jnp
        import numpy as np
        N_EXPERTS = 8
        TOP_K = 2
        C = 256
        H = 128
        HS = 256
        B, T = (1, 64)
        SCALE = 0.02
        Bb, Tt, Cc = x.shape
        xf = x.reshape(-1, Cc)
        scores = xf @ gate_w.T
        ew, ei = jax.lax.top_k(scores, TOP_K)
        ew = jax.nn.softmax(ew, axis=-1)
        x1 = jax.nn.silu(jnp.einsum('td,ehd->teh', xf, w_gate))
        x3 = jnp.einsum('td,ehd->teh', xf, w_up)
        expert_out = jnp.einsum('teh,edh->ted', x1 * x3, w_down)
        onehot = jax.nn.one_hot(ei, N_EXPERTS, dtype=ew.dtype)
        comb = jnp.einsum('ta,tae->te', ew, onehot)
        routed = jnp.einsum('te,ted->td', comb, expert_out)
        shared = jax.nn.silu(xf @ sh_gate.T) * (xf @ sh_up.T) @ sh_down.T
        sgate = jax.nn.sigmoid(xf @ se_gate_w.T)
        return (routed + sgate * shared).reshape(Bb, Tt, Cc)

    def _L3_attn_ref(x, Wq, bq, Wk, bk, Wv, bv, Wg, bg):
        import jax, jax.numpy as jnp
        import numpy as np
        DIM = 256
        q = jnp.einsum('bsd,ed->bse', x, Wq) + bq
        k = jnp.einsum('bsd,ed->bse', x, Wk) + bk
        v = jnp.einsum('bsd,ed->bse', x, Wv) + bv
        g = jax.nn.sigmoid(jnp.einsum('bsd,ed->bse', x, Wg) + bg)
        kv_state = jnp.cumsum(k * v, axis=1)
        return q * kv_state * g

    def _L3_ffn_ref(x, w1, w2, w3):
        import jax, jax.numpy as jnp
        import numpy as np
        EPS = 1e-08

        def _quantize(w):
            gamma = jnp.mean(jnp.abs(w))
            return jnp.clip(jnp.round(w / (gamma + EPS)), -1.0, 1.0)

        def _bitlinear(x, w):
            return jnp.matmul(x, _quantize(w).T)
        x1 = _bitlinear(x, w1)
        x2 = _bitlinear(x, w2)
        hidden = jax.nn.sigmoid(x1) * x2
        return _bitlinear(hidden, w3)
    x = L0_attn_x
    xn = _layernorm(x, axis=-1)
    x = x + _L0_attn_ref(xn, L0_attn_Wqd, L0_attn_Wqu, L0_attn_Wqr, L0_attn_Wkvd, L0_attn_Wku, L0_attn_Wvu, L0_attn_Wkr, L0_attn_Wo) + _L0_ffn_ref(xn, L0_ffn_W_gate, L0_ffn_W_qkv)
    xn = _layernorm(x, axis=-1)
    x = x + _L1_attn_ref(xn, L1_attn_Ws, L1_attn_Wa, L1_attn_Wo, L1_attn_bo) + _L1_ffn_ref(xn, L1_ffn_SU_ug, L1_ffn_SU_dp, L1_ffn_Wscale_ug, L1_ffn_Wscale_dp, L1_ffn_W_up, L1_ffn_W_gate, L1_ffn_W_down)
    xn = _layernorm(x, axis=-1)
    x = x + _L2_attn_ref(xn, L2_attn_w_qkv, L2_attn_w_out) + _L2_ffn_ref(xn, L2_ffn_gate_w, L2_ffn_w_gate, L2_ffn_w_up, L2_ffn_w_down, L2_ffn_sh_gate, L2_ffn_sh_up, L2_ffn_sh_down, L2_ffn_se_gate_w)
    xn = _layernorm(x, axis=-1)
    x = x + _L3_attn_ref(xn, L3_attn_Wq, L3_attn_bq, L3_attn_Wk, L3_attn_bk, L3_attn_Wv, L3_attn_bv, L3_attn_Wg, L3_attn_bg) + _L3_ffn_ref(xn, L3_ffn_w1, L3_ffn_w2, L3_ffn_w3)
    return x

_drawn_inputs = setup_inputs


def setup_inputs(seed=0):
    import zlib

    import numpy as np

    out = dict(_drawn_inputs(seed))
    spreads = {}
    factors = {'L0_attn_Wqd': 8.0,
     'L0_attn_Wqu': 8.0,
     'L0_attn_Wqr': 8.0,
     'L0_attn_Wkvd': 8.0,
     'L0_attn_Wku': 8.0,
     'L0_attn_Wvu': 8.0,
     'L0_attn_Wkr': 8.0,
     'L0_attn_Wo': 8.0,
     'L1_ffn_Wscale_dp': 15.01,
     'L2_ffn_gate_w': 4.928,
     'L2_ffn_w_gate': 4.368,
     'L2_ffn_w_up': 4.309,
     'L2_ffn_w_down': 4.309,
     'L2_ffn_sh_gate': 4.374,
     'L2_ffn_sh_up': 4.34,
     'L2_ffn_sh_down': 4.339,
     'L2_ffn_se_gate_w': 8.0,
     'L3_attn_bq': 8.0,
     'L3_attn_bk': 8.0,
     'L3_attn_bv': 8.0,
     'L3_attn_Wg': 8.0,
     'L3_attn_bg': 64.0,
     'L0_ffn_W_gate': 8.0,
     'L0_ffn_W_qkv': 8.0,
     'L1_attn_bo': 43.554,
     'L1_ffn_Wscale_ug': 4.315,
     'L1_attn_Ws': 3.733,
     'L1_attn_Wa': 3.692,
     'L2_attn_w_qkv': 2.706,
     'L2_attn_w_out': 2.837}
    for name, (base, spread) in spreads.items():
        noise = np.random.default_rng([zlib.crc32(name.encode()), seed]).standard_normal(out[name].shape)
        drawn = base * np.exp(spread * noise) if base else spread * noise
        out[name] = jnp.asarray(drawn.astype(out[name].dtype))
    for name, factor in factors.items():
        out[name] = (out[name] * factor).astype(out[name].dtype)
    return out
```

```python
from contextlib import ExitStack

import numpy as np
import concourse.bass as bass
from concourse import mybir

F32, BF16 = mybir.dt.float32, mybir.dt.bfloat16
ALU = mybir.AluOpType
ACT = mybir.ActivationFunctionType
AX = mybir.AxisListType.X

P = 128
T, D = 1024, 256
NT, DC = T // P, D // P
HALF = 512
H, HD, RD, LAT = 16, 16, 64, 64
GH = 4
NG = H // GH
HV, VW = HD + 1, 32
RANK = 32
INTER, E, TOP, F3 = 1024, 8, 2, 704
FC = INTER // P
F3C = (F3 + P - 1) // P
EPS_LN, EPS_Q = 1e-5, 1e-8
LOWEST = -3.0e38
Q_PARTS = (0, 0, 0, 1, 1, 2)
K_PARTS = (0, 1, 2, 0, 1, 0)
STACK = len(Q_PARTS) * HD
MLA = RD + HD


def f3_rows(m):
    return min(P, F3 - m * P)


def max_units():
    for j in range(NT):
        for part in range(1 + (j >= NT // 2)):
            w = min(HALF, (j + 1) * P) if part == 0 else (j + 1) * P - HALF
            nh = {P: 4, 2 * P: 2}.get(w, 1)
            for h0 in range(0, GH, nh):
                yield j, part, h0, nh, w


MAX_UNITS = list(max_units())
MAX_END = 6


def max_chunk(late, kt):
    first = 2 if late else 0
    n = MAX_END - first
    if not first <= kt < MAX_END:
        return []
    a, b = (kt - first) * len(MAX_UNITS) // n, (kt - first + 1) * len(MAX_UNITS) // n
    return MAX_UNITS[a:b]


def build(nc, ins, out):
    with ExitStack() as ctx:
        def sb(name, shape, dt=F32):
            return ctx.enter_context(nc.sbuf_tensor(name, shape, dt))

        def sem(name):
            return ctx.enter_context(nc.semaphore(name))

        def dram(name, shape, dt):
            return nc.dram_tensor(name, shape, dt, kind="Internal").ap()

        x = sb("x", [P, NT, D])
        xn = sb("xn", [P, NT, D])
        xnT = sb("xnT", [P, DC, T])
        fT = sb("fT", [P, DC, T])
        Qs = sb("Qs", [P, 8 * T])
        Ks = sb("Ks", [P, 8 * T])
        Kg = sb("Kg", [P, T], BF16)
        Vh = sb("Vh", [P, NT, H * HV + VW - HV])
        Vg = sb("Vg", [P, NT, VW])
        Pr = sb("Pr", [P, 8 * T])
        OT = sb("OT", [P, T])
        gate = sb("gate", [P, 2, T])
        WA = sb("WA", [P, 7186])
        WB = sb("WB", [P, 4352])
        identf = sb("identf", [P, P])
        had = sb("had", [P, P])
        onesf = sb("onesf", [P, P])
        identb = sb("identb", [P, P], BF16)
        maskq = sb("maskq", [P, P], BF16)
        maskk = sb("maskk", [P, P], BF16)
        tie = sb("tie", [P, H])
        stat = sb("stat", [P, NT, 6])
        mv = sb("mv", [P, NT, 2])
        ln = sb("ln", [P, 5, NT])
        mx = sb("mx", [P, NT, 2, GH])
        mneg = sb("mneg", [P, GH, NT])
        mrow = sb("mrow", [GH * NT, P])
        mrowb = sb("mrowb", [GH * NT, P], BF16)
        rec = sb("rec", [P, 4, GH])
        otmp = sb("otmp", [P, 4, GH, HD])
        rt = sb("rt", [P, 6, NT * H])
        sel = sb("sel", [P, NT, 2, H])
        kvs = sb("kvs", [P, NT, 2, HD])
        su = sb("su", [P, DC + 3 * FC])
        sig3 = sb("sig3", [P, NT, 3])
        gam = sb("gam", [P, 12])

        psA = ctx.enter_context(nc.psum_tensor("psA", [P, 2, 2 * HALF], F32))
        psD = ctx.enter_context(nc.psum_tensor("psD", [P, 2, HALF], F32))
        psO = ctx.enter_context(nc.psum_tensor("psO", [P, 2 * HALF], F32))

        lr = rt[:].rearrange("p k n -> p (k n)")[:, 0:10 * NT * (E + 1)].rearrange("p (k n) -> p k n", k=10)
        seT = OT[0:E, :]

        def carve(t):
            at = [0]

            def part(*dims):
                n = int(np.prod(dims))
                v = t[:, at[0]:at[0] + n]
                at[0] += n
                return v.rearrange("p (a b) -> p a b", a=dims[0]) if len(dims) == 2 else v
            return part

        part = carve(WA)
        w_lat, w_kr = part(DC, P), part(DC, 2 * RD)
        w_qr, w_qrot = part(H * RD), part(H * RD)
        w_u, w_vu = part(D), part(D)
        w_o0, w_g0, w_qkv0 = part(DC, D), part(DC, H), part(DC, 3 * D)
        part = carve(WA)
        w_qkv2, w_o2, w_rt2 = part(DC, 3 * D), part(DC, D), part(DC, E + 1)
        w_eg, w_eu, w_sg, w_sd = part(DC, E * P), part(DC, E * P), part(DC, D), part(DC, D)
        w_ed = Ks[:, 5 * T:7 * T].rearrange("p (e d) -> p e d", e=E)
        w_su = OT[:, 0:DC * D].rearrange("p (c d) -> p c d", c=DC)
        part = carve(WB)
        w_up, w_dn, ws_dp = part(DC, INTER), part(FC, D), part(D)
        part = carve(Ks[:, 4 * T:])
        w_gt, h256, w_o1, w_sa = part(DC, INTER), part(DC, D), part(DC, D), part(DC, 2 * RANK)
        bor = part(D)[0:1, :]
        part = carve(WB)
        w31, w32, w33 = part(DC, F3), part(DC, F3), part(F3C, D)
        w3m = Vh[:].rearrange("p j v -> p (j v)")[:, 0:4 * DC * D].rearrange("p (c d) -> p c d", d=D)
        q_tmp = Kg
        cos, sin = gate[:, 0, :], gate[:, 1, :]
        lat = OT
        kr, kr_t = (xn[:].rearrange("p j d -> p (j d)")[0:RD, n * T:(n + 1) * T] for n in range(2))
        kv_tmp = Pr[:, 7680:8192]
        Q1 = OT
        K1 = Ks[:, 0:T]
        V1 = Ks[:, T:T + NT * (D + 1)].rearrange("p (j d) -> p j d", j=NT)
        fT8 = fT[:].rearrange("p c (e d) -> p (c e) d", d=D)

        def Vh_heads(j):
            return Vh[:, j, 0:H * HV].rearrange("p (h v) -> p h v", v=HV)

        def slot(t, n, rows=P, base=0):
            return t[base:base + rows, n * T:(n + 1) * T]

        def split_place(u):
            b = 2560 * (u % 3)
            return (Pr[:, b:b + T],
                    Pr[:, b + T:b + 2560].bitcast(BF16).rearrange("p (s t) -> p s t", s=3))

        def tile_cols(j):
            return slice(j * P, (j + 1) * P)

        d_qr = dram("d_qr", (H * RD, T), F32)
        d_qn = dram("d_qn", (D, T), F32)
        d_kn = dram("d_kn", (D, T), F32)
        d_gq = dram("d_gq", (3, D, T), BF16)
        d_gk = dram("d_gk", (3, HD, T), BF16)
        d_q2 = dram("d_q2", (3, D, T), BF16)
        d_k2 = dram("d_k2", (3, D, T), BF16)
        d_cb = dram("d_cb", (E, T), F32)

        GROUPS = {0: list(range(0, 2 * NG)), 2: list(range(2 * NG, 3 * NG))}
        LAST = 3 * NG - 1

        def is_mla(i):
            return i < NG

        def head_rows(t, i, h, rows, a, b):
            if is_mla(i):
                o = ((i % 2) * GH + h) * T
                return t[0:rows, o + a:o + b]
            o = ((i % 4) * GH + h) * T
            return t[:].bitcast(BF16)[0:rows, o + a:o + b]

        def key_rows(i, h, rows, a, b):
            return Kg[0:rows, a:b] if NG <= i < 2 * NG else head_rows(Ks, i, h, rows, a, b)

        def high(ap):
            return ap.bitcast(BF16).rearrange("p (t w) -> p t w", w=2)[:, :, 1]

        def values(i, kt, h):
            return Vg[:, kt, :] if NG <= i < 2 * NG else Vh[:, kt, (h + GH * (i % NG)) * HV:(h + GH * (i % NG)) * HV + VW]

        def score_scale(i):
            return float(1.0 / np.sqrt(np.float32(HD + RD))) if is_mla(i) else HD ** -0.5

        def maxima(i):
            return i + 1 if i < 2 * NG else (2 * NG + 1 if i == "L1" else i + 2)

        def maxima_of(i):
            return 2 * NG + 1 if i == "L1" else maxima(i)

        def numbered(names):
            through, n = {}, 0
            for name, count in names:
                n += count
                through[name] = n
            return through

        A_GROUP = 4 * GH + 4 * GH // 2
        A = numbered(
            [("xnT0", DC), ("lat", 1), ("qn", 2), ("kn", 2), ("v0", 2), ("gq", 2), ("gk", 1)]
            + [(f"att{i}", A_GROUP) for i in GROUPS[0]] + [("oT0", DC)]
            + [("xnT1", DC), ("qk1", 1), ("v1", 2), ("xh", DC), ("s1", NT), ("gate1", FC)]
            + [("xnT2", DC), ("cT", 1), ("q2", 2), ("k2", 2), ("v2", 2)]
            + [(f"att{i}", A_GROUP) for i in GROUPS[2]] + [("oT2", DC), ("gate2", E + DC)]
            + [("xnT3", DC), ("k3", DC), ("g3", DC), ("sig3", F3C)])
        NMAX = len(MAX_UNITS)

        def d_groups(groups):
            return [x for i in groups for x in ((f"max{i}", NMAX), (f"mrow{i}", 1), (f"o{i}", 2))]

        def d_attention(groups):
            names = [(f"max{groups[0]}", NMAX), (f"mrow{groups[0]}", 1)]
            for i in groups:
                nxt = i + 1 if i + 1 in groups else None
                for kt in range(NT):
                    if nxt is not None:
                        names.append((f"max{nxt}.{kt}", len(max_chunk(is_mla(nxt), kt))))
                    if kt == 1 and i - 1 in groups:
                        names.append((f"o{i - 1}", 2))
                    if nxt is not None and kt == MAX_END:
                        names.append((f"mrow{nxt}", 1))
            return names + [(f"o{groups[-1]}", 2)]

        MAX1 = [(j, part, min(HALF, (j + 1) * P) if part == 0 else (j + 1) * P - HALF)
                for j in range(NT) for part in range(1 + (j >= NT // 2))]
        DU = numbered(
            [("kr", 2), ("rope", 2 * H), ("rt0", 1), ("kv0", NT)]
            + d_attention(GROUPS[0]) + [("wdn", FC // 2), ("down0", NT // 2)]
            + [("maxL1", len(MAX1)), ("mrowL1", 1), ("up1", 2 * FC), ("pv1", NT), ("down1", NT // 2)]
            + [("rt2", 1)] + d_attention(GROUPS[2]) + [("gsum", 1), ("up2", 2 * (E + DC))]
            + [(f"down2.{u}", 2) for u in range(NT // 2)]
            + [("v3", 2 * DC), ("q3", 2 * DC), ("up3", 2 * F3C), ("down3", NT // 2)])

        x_in, consts_in, w0_in, w1_in, w2_in, w3_in, moe_in, w1b_in, w3m_in = (
            sem(n) for n in ("x_in", "consts_in", "w0_in", "w1_in", "w2_in", "w3_in", "moe_in", "w1b_in", "w3m_in"))
        a_filled, a_drained, d_filled, d_drained = (
            sem(n) for n in ("a_filled", "a_drained", "d_filled", "d_drained"))
        o_drained = sem("o_drained")
        dve_step, pool_step = sem("dve_step"), sem("pool_step")
        v_cleared, rotated = sem("v_cleared"), sem("rotated")
        ln_var, ln_std, xn_ready = sem("ln_var"), sem("ln_std"), sem("xn_ready")
        kr_ready, rope_sum, mla_stored, kr_in = sem("kr_ready"), sem("rope_sum"), sem("mla_stored"), sem("kr_in")
        rt_shift, rt_exp, ksel_ready = sem("rt_shift"), sem("rt_exp"), sem("ksel_ready")
        split_done = sem("split_done")
        split_stored = [sem(f"split_stored{n}") for n in range(3)]
        kg_in = sem("kg_in")
        stack_in = [sem(f"stack_in{n}") for n in range(4)]
        max_ready, mrow_in = sem("max_ready"), sem("mrow_in")
        pv_done = sem("pv_done")
        butterflies, had_ready, ones1_ready = sem("butterflies"), sem("had_ready"), sem("ones1_ready")
        se_args, se_ready, comb_ready, comb_out, comb_in = (
            sem(n) for n in ("se_args", "se_ready", "comb_ready", "comb_out", "comb_in"))
        gsum_ready, quantised = sem("gsum_ready"), sem("quantised")
        gated, cum_ready, y3_ready, stored = sem("gated"), sem("cum_ready"), sem("y3_ready"), sem("stored")
        STACK_DMAS = {0: 3, 1: len(Q_PARTS), 2: len(Q_PARTS) + len(K_PARTS) + 1}
        N_KR, N_KG, N_MLA = 16, len(K_PARTS) + 1, 4 + H // 2
        N_CONSTS, N_W0, N_W1, N_W1B, N_W2, N_W3, N_W3M, N_MOE = 8, 9, 4, 5, 7, 5, 4, 2

        def stacks(i):
            return 16 * sum(STACK_DMAS[k // NG] for k in range(i % 4, i + 1, 4))

        block = ctx.enter_context(nc.Block())

        @block.sync
        def _(sp):
            def load(dst, src, s):
                sp.dma_start(dst, src).then_inc(s, 16)

            def tiles(name):
                return ins[name].rearrange("(c p) n -> p c n", p=P)

            for j in range(0, NT, 2):
                load(x[:, j:j + 2, :], ins["x"].rearrange("(j p) d -> p j d", p=P)[:, j:j + 2, :], x_in)
            for dst, name in ((identf, "c_ident"), (had, "c_had"), (identb, "c_identb"), (maskq, "c_maskq"),
                              (maskk, "c_maskk"), (tie, "c_tie")):
                src = ins[name]
                load(dst[:], src if dst.dtype == src.dtype else src.bitcast(BF16), consts_in)
            load(w_lat, tiles("w_lat"), w0_in)
            load(w_kr[:, :, 0:RD], tiles("Wkr"), w0_in)
            load(w_qr[0:LAT, :], ins["Wqr"], w0_in)
            load(w_u[0:LAT, :], ins["Wqu"], w0_in)
            load(w_u[LAT:P, :], ins["Wku"], w0_in)
            load(w_vu[LAT:P, :], ins["Wvu"], w0_in)
            load(cos, ins["c_cos"], consts_in)
            load(sin, ins["c_sin"], consts_in)
            load(w_o0, tiles("Wo0"), w0_in)
            load(w_g0, tiles("Wg0T"), w0_in)
            load(w_qkv0, tiles("Wqkv0T"), w0_in)
            load(w_up, tiles("W_upT"), w1_in)
            load(w_dn, tiles("W_downT"), w1_in)
            load(ws_dp, ins["ws_dp"].broadcast_to([P, D]), w1_in)
            load(su[:], ins["su"], w1_in)

            for u in range(4):
                sp.wait_ge(a_drained, A["lat"] + u + 1)
                load((d_qn, d_kn)[u // 2][tile_cols(u % 2), :], slot(Ks, 4 + u), mla_stored)
            for p in range(H // 2):
                sp.wait_ge(rope_sum, p + 1)
                load(d_qr[tile_cols(p), :], slot(Qs, p), mla_stored)
            sp.wait_ge(mla_stored, 16 * N_MLA)
            sp.wait_ge(kr_ready, 1)
            for n in range(8):
                load(slot(Ks, n, RD), kr, kr_in)
                load(slot(Ks, n, 1, MLA), ins["c_ones"], kr_in)

            def load_group(i):
                s, g = stack_in[i % 4], i % NG
                if is_mla(i):
                    o = (i % 2) * GH * T
                    for t, a, b, d in ((Qs, 0, RD, d_qr), (Qs, RD, MLA, d_qn), (Ks, RD, MLA, d_kn)):
                        n = GH * (b - a)
                        load(t[a:b, o:o + GH * T].rearrange("p (h t) -> p h t", h=GH),
                             d[g * n:(g + 1) * n, :].rearrange("(h d) t -> d h t", d=b - a), s)
                    return
                o, rows = (i % 4) * GH * T, slice(g * GH * HD, (g + 1) * GH * HD)

                def parts(t, d, order):
                    for r, part in enumerate(order):
                        load(t[:].bitcast(BF16)[r * HD:(r + 1) * HD, o:o + GH * T].rearrange("p (h t) -> p h t", h=GH),
                             d[part, rows, :].rearrange("(h d) t -> d h t", d=HD), s)
                parts(Qs, d_gq if i < 2 * NG else d_q2, Q_PARTS)
                if i >= 2 * NG:
                    parts(Ks, d_k2, K_PARTS)
                    load(Ks[:].bitcast(BF16)[STACK:STACK + 1, o:o + GH * T], ins["c_ones4b"].bitcast(BF16), s)

            def maxima_row(i):
                sp.wait_ge(d_drained, DU[f"mrow{i}"])
                if is_mla(i):
                    o = (i % 2) * GH * T
                    load(Qs[MLA:MLA + 1, o:o + GH * T], mrow[:], mrow_in)
                else:
                    o = (i % 4) * GH * T
                    load(Qs[:].bitcast(BF16)[STACK:STACK + 1, o:o + GH * T], mrowb[:], mrow_in)

            load_group(0)
            load_group(1)
            for u in range(2):
                sp.wait_ge(split_done, u + 1)
                load(d_gq[:, tile_cols(u), :].rearrange("s d t -> d s t"), split_place(u)[1], split_stored[u])
            sp.wait_ge(split_done, 3)
            load(d_gk.rearrange("s d t -> d s t"), split_place(2)[1][0:HD], split_stored[2])
            sp.wait_ge(split_stored[2], 16)
            for r, part in enumerate(K_PARTS):
                load(Kg[r * HD:(r + 1) * HD, :], d_gk[part], kg_in)
            load(Kg[STACK:STACK + 1, :], ins["c_ones4b"][:, 0:T].bitcast(BF16), kg_in)
            sp.wait_ge(split_stored[0], 16)
            sp.wait_ge(split_stored[1], 16)
            maxima_row(0)
            for i in GROUPS[0]:
                if i + 1 in GROUPS[0]:
                    maxima_row(i + 1)
                for k in {0: (2,), 1: (3,), 2: (4, 5), 3: (6, 7)}.get(i, ()):
                    sp.wait_ge(a_filled, A[f"att{i}"])
                    load_group(k)

            sp.wait_ge(a_filled, A[f"att{2 * NG - 1}"])
            load(w_sa, tiles("Wsa"), w1b_in)
            load(w_o1, tiles("Wo1T"), w1b_in)
            load(h256, tiles("c_h256"), w1b_in)
            load(w_gt, tiles("W_gateT"), w1b_in)
            load(bor, ins["bo"], w1b_in)

            sp.wait_ge(d_drained, DU["down0"])
            load(w_qkv2, tiles("Wqkv2T"), w2_in)
            load(w_o2, tiles("Wo2T"), w2_in)
            load(w_rt2, tiles("Wrt2T"), w2_in)
            load(w_eg, tiles("WegT"), w2_in)
            load(w_eu, tiles("WeuT"), w2_in)
            load(w_sg, tiles("WsgT"), w2_in)
            load(w_sd, tiles("WsdT"), w2_in)

            sp.wait_ge(d_drained, DU["mrowL1"])
            load(Q1[RANK:RANK + 1, :], mrow[0:NT, :], mrow_in)

            sp.wait_ge(d_drained, DU["down1"])
            load(w31, tiles("w31T"), w3_in)
            load(w32, tiles("w32T"), w3_in)
            full = F3 // P
            load(w33[:, 0:full, :], ins["w33T"][0:full * P, :].rearrange("(c p) n -> p c n", p=P), w3_in)
            load(w33[0:F3 - full * P, full, :], ins["w33T"][full * P:F3, :], w3_in)
            load(su[:, 0:4 * DC], ins["b3"], w3_in)

            sp.wait_ge(a_drained, A["cT"])
            load(d_cb, seT[:], comb_out)
            for u in range(4):
                n = 3 + u
                sp.wait_ge(split_done, n + 1)
                load((d_q2, d_k2)[u // 2][:, tile_cols(u % 2), :].rearrange("s d t -> d s t"),
                     split_place(n)[1], split_stored[n % 3])
            sp.wait_ge(split_stored[0], 16 * 3)
            sp.wait_ge(split_stored[1], 16 * 2)
            sp.wait_ge(split_stored[2], 16 * 2)
            for i in GROUPS[2]:
                load_group(i)
            for i in GROUPS[2]:
                maxima_row(i)
            sp.wait_ge(a_filled, A[f"att{LAST}"])
            load(w_ed, ins["WedT"].rearrange("(e p) n -> p e n", p=P), moe_in)
            sp.wait_ge(pv_done, NT * (LAST + 1))
            for n, name in enumerate(("Wq3T", "Wk3T", "Wv3T", "Wg3T")):
                load(w3m[:, n * DC:(n + 1) * DC, :], tiles(name), w3m_in)
            sp.wait_ge(comb_out, 16)
            for e in range(E):
                load(slot(Pr, e), d_cb[e:e + 1, :].broadcast_to([P, T]), comb_in)
            sp.wait_ge(d_drained, DU[f"o{LAST}"])
            load(w_su, tiles("WsuT"), moe_in)

            for u in range(NT // 2):
                sp.wait_ge(d_drained, DU["down3"] - NT // 2 + u + 1)
                load(out.rearrange("(j p) d -> p j d", p=P)[:, 2 * u:2 * u + 2, :], x[:, 2 * u:2 * u + 2, :], stored)
            sp.wait_ge(stored, 16 * NT // 2)

        @block.gpsimd
        def _(pool):
            steps = [0]

            def link(instr):
                steps[0] += 1
                instr.then_inc(pool_step, 1)
                pool.wait_ge(pool_step, steps[0])

            link(pool.memset(Vh[:], 0.0))
            link(pool.memset(Vg[:], 0.0))
            for j in range(NT):
                op = pool.memset(Vh_heads(j)[:, :, HD:HV], 1.0)
            op.then_inc(v_cleared, 1)
            pool.memset(Vg[:, :, HD:HD + 1], 1.0).then_inc(v_cleared, 1)
            pool.memset(onesf[:], 1.0).then_inc(v_cleared, 1)

            pool.wait_ge(w0_in, 16 * N_W0)
            h2 = RD // 2
            pool.tensor_scalar(w_kr[:, :, RD:RD + h2], w_kr[:, :, h2:RD], -1.0, None, ALU.mult).then_inc(rotated, 1)
            pool.tensor_copy(w_kr[:, :, RD + h2:2 * RD], w_kr[:, :, 0:h2]).then_inc(rotated, 1)
            src = w_qr[0:LAT, :].rearrange("p (h d) -> p h d", d=RD)
            dst = w_qrot[0:LAT, :].rearrange("p (h d) -> p h d", d=RD)
            pool.tensor_scalar(dst[:, :, 0:h2], src[:, :, h2:RD], -1.0, None, ALU.mult).then_inc(rotated, 1)
            pool.tensor_copy(dst[:, :, h2:RD], src[:, :, 0:h2]).then_inc(rotated, 1)

            pool.wait_ge(d_drained, DU["kr"])
            pool.tensor_tensor(kr, kr, kr_t, ALU.add).then_inc(kr_ready, 1)
            for p in range(H // 2):
                pool.wait_ge(d_drained, DU["kr"] + 4 * (p + 1))
                pool.tensor_tensor(slot(Qs, p), slot(Qs, p), slot(Ks, p % 4), ALU.add).then_inc(rope_sum, 1)

            pool.wait_ge(w1_in, 16 * N_W1)
            a, b = w_dn, fT8
            for s in range(3):
                g = 1 << s
                for q in range(0, FC, 2 * g):
                    lo, hi = slice(q, q + g), slice(q + g, q + 2 * g)
                    link(pool.tensor_tensor(b[:, lo], a[:, lo], a[:, hi], ALU.add))
                    op = pool.tensor_tensor(b[:, hi], a[:, lo], a[:, hi], ALU.subtract)
                    if s < 2:
                        link(op)
                    else:
                        op.then_inc(butterflies, 1)
                a, b = b, a
            pool.wait_ge(w1b_in, 16 * N_W1B)
            link(pool.tensor_scalar(h256[:, 0, :], h256[:, 0, :], su[:, 0:1], None, ALU.mult))
            pool.tensor_scalar(h256[:, 1, :], h256[:, 1, :], su[:, 1:2], None, ALU.mult).then_inc(had_ready, 1)

            pool.wait_ge(comb_in, 16 * E)
            for e in range(E):
                pool.wait_ge(a_drained, A["oT2"] + e + 1)
                pool.tensor_tensor(gate[:, e % 2, :], gate[:, e % 2, :], slot(Pr, e), ALU.mult).then_inc(gated, 1)

            for c in range(DC):
                pool.wait_ge(cum_ready, c + 1)
                pool.wait_ge(d_drained, DU["v3"] + 2 * (c + 1))
                pool.tensor_tensor(slot(Qs, 4 + c), slot(Qs, c), slot(Qs, 6 + c), ALU.mult).then_inc(y3_ready, 1)

        @block.scalar
        def _(act):
            n = [0]

            def take():
                n[0] += 1
                act.wait_ge(a_filled, n[0])
                return psA[:, (n[0] - 1) % 2, :]

            def copy_units(dsts):
                for dst in dsts:
                    src = take()
                    act.activation(dst, src[0:dst.shape[0], :] if len(dst.shape) == 2 else src, ACT.Copy).then_inc(a_drained, 1)

            def std():
                std.n += 1
                act.wait_ge(ln_var, std.n)
                act.activation(ln[:, 1, :], ln[:, 0, :], ACT.Sqrt).then_inc(ln_std, 1)
            std.n = 0

            def value_units():
                for u in range(2):
                    src = take().rearrange("p (j h d) -> p j h d", j=4, h=H)
                    for j in range(4):
                        op = act.activation(Vh_heads(4 * u + j)[:, :, 0:HD], src[:, j], ACT.Copy)
                    op.then_inc(a_drained, 1)

            def attention(groups):
                for i in groups:
                    for kt in range(NT):
                        s = NT * i + kt
                        if s >= 2:
                            act.wait_ge(pv_done, s - 1)
                        place = Pr[:, (s % 2) * GH * T:(s % 2 + 1) * GH * T].rearrange("p (h t) -> p h t", h=GH)
                        q0 = kt * P
                        if kt < NT // 2:
                            for h in range(GH):
                                src = take()
                                act.activation(place[:, h, q0:T], src[:, q0:T], ACT.Exp,
                                               scale=score_scale(i)).then_inc(a_drained, 1)
                        else:
                            for h in range(0, GH, 2):
                                src = take().rearrange("p (h t) -> p h t", h=2)
                                act.activation(place[:, h:h + 2, q0:T], src[:, :, q0 - HALF:HALF], ACT.Exp,
                                               scale=score_scale(i)).then_inc(a_drained, 1)
                        if kt == 0 and i > groups[0]:
                            output(i - 1)
                output(groups[-1])

            def output(i):
                act.wait_ge(pv_done, NT * (i + 1))
                if f"o{i - 1}" in DU:
                    act.wait_ge(d_drained, DU[f"o{i - 1}"])
                if i == GROUPS[2][0]:
                    act.wait_ge(comb_out, 16)
                act.activation(OT[:], psO[:], ACT.Copy).then_inc(o_drained, 1)

            std()
            copy_units([xnT[:, c, :] for c in range(DC)])
            copy_units([lat[:]] + [slot(Ks, 4 + u) for u in range(4)])
            act.wait_ge(v_cleared, 3)
            value_units()
            act.wait_ge(rt_shift, 1)
            act.activation(rt[:, 2, :], rt[:, 1, :], ACT.Exp).then_inc(rt_exp, 1)
            copy_units([split_place(u)[0] for u in range(2)])
            copy_units([split_place(2)[0][0:HD]])
            for s in split_stored:
                act.wait_ge(s, 16)
            attention(GROUPS[0])
            copy_units([fT[:, c, :] for c in range(DC)])
            std()
            copy_units([xnT[:, c, :] for c in range(DC)])
            src = take()
            act.activation(Q1[0:RANK, :], src[0:RANK, :], ACT.Copy)
            act.activation(K1[0:RANK, :], src[RANK:2 * RANK, :], ACT.Copy).then_inc(a_drained, 1)
            for u in range(2):
                src = take().rearrange("p (j d) -> p j d", d=D)
                act.activation(V1[:, 4 * u:4 * u + 4, 0:D], src, ACT.Copy).then_inc(a_drained, 1)
            copy_units([fT[:, c, :] for c in range(DC)])
            for kt in range(NT):
                src = take()
                act.activation(slot(Pr, kt)[:, kt * P:T], src[:, kt * P:T], ACT.Exp,
                               scale=float(1.0 / np.sqrt(RANK))).then_inc(a_drained, 1)
            for m in range(FC):
                src = take()
                if m >= 2:
                    act.wait_ge(d_drained, DU["mrowL1"] + 2 * (m - 1))
                act.activation(gate[:, m % 2, :], src, ACT.Silu,
                               scale=su[:, DC + 2 * FC + m:DC + 2 * FC + m + 1]).then_inc(a_drained, 1)
            std()
            copy_units([xnT[:, c, :] for c in range(DC)])
            act.wait_ge(se_args, 1)
            act.activation(sig3[:], lr[:, 9, 0:3 * NT].rearrange("p (j s) -> p j s", s=3), ACT.Sigmoid).then_inc(se_ready, 1)
            copy_units([seT[:]])
            for u in range(4):
                if u == 3:
                    act.wait_ge(split_stored[0], 32)
                copy_units([split_place(3 + u)[0]])
            value_units()
            act.wait_ge(split_stored[0], 16 * 3)
            act.wait_ge(split_stored[1], 16 * 2)
            act.wait_ge(split_stored[2], 16 * 2)
            attention(GROUPS[2])
            copy_units([fT[:, c, :] for c in range(DC)])
            for m in range(E + DC):
                src = take()
                if m >= 2:
                    act.wait_ge(d_drained, DU["gsum"] + 2 * (m - 1))
                act.activation(gate[:, m % 2, :], src, ACT.Silu).then_inc(a_drained, 1)
            std()
            copy_units([xnT[:, c, :] for c in range(DC)])
            act.wait_ge(w3_in, 16 * N_W3)
            for c in range(DC):
                act.activation(slot(Qs, c), take(), ACT.Identity, bias=su[:, DC + c:DC + c + 1]).then_inc(a_drained, 1)
            for c in range(DC):
                act.activation(slot(Qs, 2 + c), take(), ACT.Sigmoid,
                               bias=su[:, 3 * DC + c:3 * DC + c + 1]).then_inc(a_drained, 1)
            for m in range(F3C):
                src = take()
                if m >= 2:
                    act.wait_ge(d_drained, DU["q3"] + 2 * (m - 1))
                r = f3_rows(m)
                act.activation(gate[0:r, m % 2, :], src[0:r, :], ACT.Sigmoid).then_inc(a_drained, 1)
            assert n[0] == A["sig3"]

        @block.vector
        def _(dve):
            n = [0]
            steps = [0]

            def take():
                n[0] += 1
                dve.wait_ge(d_filled, n[0])
                return psD[:, (n[0] - 1) % 2, :]

            def link(instr):
                steps[0] += 1
                instr.then_inc(dve_step, 1)
                dve.wait_ge(dve_step, steps[0])

            def at(name):
                assert n[0] == DU[name], (name, n[0], DU[name])

            def norm(layer):
                if layer == 0:
                    dve.wait_ge(x_in, 16 * NT // 2)
                else:
                    dve.wait_ge(d_drained, n[0])
                for j in range(NT):
                    op = dve.bn_stats(stat[:, j, :], x[:, j, :])
                link(op)
                for j in range(NT):
                    op = dve.bn_aggr(mv[:, j, :], stat[:, j, :])
                link(op)
                dve.tensor_scalar(ln[:, 0, :], mv[:, :, 1], EPS_LN, None, ALU.add).then_inc(ln_var, 1)
                dve.wait_ge(ln_std, layer + 1)
                link(dve.reciprocal(ln[:, 2, :], ln[:, 1, :]))
                link(dve.tensor_tensor(ln[:, 3, :], ln[:, 0, :], ln[:, 2, :], ALU.mult))
                link(dve.tensor_tensor(ln[:, 3, :], ln[:, 3, :], ln[:, 1, :], ALU.add))
                link(dve.tensor_scalar(ln[:, 3, :], ln[:, 3, :], 0.5, None, ALU.mult))
                link(dve.reciprocal(ln[:, 4, :], ln[:, 3, :]))
                for j in range(NT):
                    dve.tensor_scalar(xn[:, j, :], x[:, j, :], mv[:, j, 0:1], ln[:, 4, j:j + 1],
                                      ALU.subtract, ALU.mult).then_inc(xn_ready, 1)

            def rope(dst_cos, dst_sin, rows_cos, rows_sin):
                for dst, rows, table in ((dst_cos, rows_cos, cos), (dst_sin, rows_sin, sin)):
                    for half in range(2):
                        c = slice(half * HALF, (half + 1) * HALF)
                        src = take()
                        dve.tensor_tensor(dst[:, c], src[rows, :], table[rows, c], ALU.mult).then_inc(d_drained, 1)

            def first_of(dst, eq, best, width, rank):
                link(dve.tensor_tensor(eq, eq, rank, ALU.mult))
                link(dve.tensor_reduce(best, eq, AX, ALU.max))
                link(dve.tensor_tensor(dst, eq, best.unsqueeze(2).broadcast_to([P, NT, width]), ALU.is_equal))

            def split(u, filled, rows=P):
                dve.wait_ge(a_drained, filled)
                v, b = split_place(u)
                v, b = v[0:rows], b[0:rows]
                link(dve.tensor_copy(b[:, 0], v))
                link(dve.tensor_tensor(v, v, b[:, 0], ALU.subtract))
                link(dve.tensor_copy(b[:, 1], v))
                dve.tensor_tensor(b[:, 2], v, b[:, 1], ALU.subtract).then_inc(split_done, 1)

            def row_maxima(units):
                for j, part, h0, nh, w in units:
                    src = take()[:, 0:nh * w].rearrange("p (h k) -> p h k", h=nh)
                    dve.tensor_reduce(mx[:, j, part, h0:h0 + nh], src, AX, ALU.max).then_inc(d_drained, 1)

            def negated_maxima(heads):
                dve.wait_ge(d_drained, n[0])
                dve.tensor_reduce(mneg[:, 0:heads, :], mx[:, :, :, 0:heads].rearrange("p j s h -> p h j s"),
                                  AX, ALU.max, negate=True).then_inc(max_ready, 1)
                max_n[0] += 1
                dve.wait_ge(max_ready, max_n[0])

            max_n = [0]

            def maxima_rows(dst, rows):
                if max_n[0] > 1:
                    dve.wait_ge(mrow_in, 16 * (max_n[0] - 1))
                src = take()
                dve.tensor_copy(dst[0:rows, :], src[0:rows, 0:P]).then_inc(d_drained, 1)

            def outputs(i):
                for b in range(2):
                    src = take().rearrange("p (j h v) -> p j h v", j=4, h=GH)
                    link(dve.reciprocal(rec[:], src[:, :, :, HD]))
                    g = i % NG
                    cols = slice(g * GH * HD, (g + 1) * GH * HD)
                    shared = NG <= i < 2 * NG
                    dst = otmp[:] if shared else xn[:, 4 * b:4 * b + 4, cols].rearrange("p j (h d) -> p j h d", h=GH)
                    dve.tensor_tensor(dst, src[:, :, :, 0:HD], rec[:].unsqueeze(3).broadcast_to([P, 4, GH, HD]),
                                      ALU.mult).then_inc(d_drained, 1)
                    dve.wait_ge(d_drained, n[0])
                    if shared:
                        xs = x[:, 4 * b:4 * b + 4, cols].rearrange("p j (h d) -> p j h d", h=GH)
                        link(dve.tensor_tensor(xs, xs, otmp[:], ALU.add))

            def attention(groups):
                def maxima_row(i):
                    negated_maxima(GH)
                    maxima_rows(mrow if is_mla(i) else mrowb, GH * NT)
                row_maxima(MAX_UNITS)
                maxima_row(groups[0])
                for i in groups:
                    nxt = i + 1 if i + 1 in groups else None
                    for kt in range(NT):
                        if nxt is not None:
                            row_maxima(max_chunk(is_mla(nxt), kt))
                        if kt == 1 and i - 1 in groups:
                            outputs(i - 1)
                        if nxt is not None and kt == MAX_END:
                            maxima_row(nxt)
                outputs(groups[-1])

            def add_down(u, width=2):
                src = take().rearrange("p (j d) -> p j d", j=2)
                xs = x[:, 2 * u:2 * u + 2, :]
                dve.tensor_tensor(xs, xs, src, ALU.add).then_inc(d_drained, 1)

            def gated_up(dst, gate_rows, half, scale=None):
                src = take()
                c = slice(half * HALF, (half + 1) * HALF)
                r = gate_rows.shape[0]
                if scale is None:
                    dve.tensor_tensor(dst[:, c], src[0:r, :], gate_rows[:, c], ALU.mult).then_inc(d_drained, 1)
                else:
                    dve.scalar_tensor_tensor(dst[:, c], src[0:r, :], scale, gate_rows[:, c],
                                             ALU.mult, ALU.mult).then_inc(d_drained, 1)

            def biased_times(dst, other, half, bias):
                src = take()
                c = slice(half * HALF, (half + 1) * HALF)
                dve.scalar_tensor_tensor(dst[:, c], src, bias, other[:, c], ALU.add, ALU.mult).then_inc(d_drained, 1)

            link(dve.memset(mx[:], LOWEST))
            norm(0)
            dve.wait_ge(consts_in, 16 * N_CONSTS)
            for half in range(2):
                c = slice(half * HALF, (half + 1) * HALF)
                src = take()
                link(dve.tensor_tensor(kr[:, c], src[0:RD, :], cos[0:RD, c], ALU.mult))
                dve.tensor_tensor(kr_t[:, c], src[RD:P, :], sin[RD:P, c], ALU.mult).then_inc(d_drained, 1)
            at("kr")
            for p in range(H // 2):
                if p >= 4:
                    dve.wait_ge(rope_sum, p - 3)
                rope(slot(Qs, p), slot(Ks, p % 4), slice(0, P), slice(0, P))
            at("rope")
            logits, shifted, e_x = (rt[:, k, :].rearrange("p (j h) -> p j h", h=H) for k in range(3))
            small = rt[:, 3, :].rearrange("p (k j) -> p k j", j=NT)
            dve.tensor_copy(rt[:, 0, :], take()[:, 0:NT * H]).then_inc(d_drained, 1)
            dve.wait_ge(d_drained, n[0])
            link(dve.tensor_reduce(small[:, 0], logits, AX, ALU.max))
            top = small[:, 0].unsqueeze(2).broadcast_to([P, NT, H])
            dve.tensor_tensor(shifted, logits, top, ALU.subtract).then_inc(rt_shift, 1)
            eq = rt[:, 4, :].rearrange("p (j h) -> p j h", h=H)
            link(dve.tensor_tensor(eq, logits, top, ALU.is_equal))
            ind = rt[:, 5, :].rearrange("p (j h) -> p j h", h=H)
            first_of(ind, eq, small[:, 1], H, tie[:].unsqueeze(1).broadcast_to([P, NT, H]))
            dve.wait_ge(rt_exp, 1)
            link(dve.tensor_reduce(small[:, 2], e_x, AX, ALU.add))
            link(dve.reciprocal(small[:, 3], small[:, 2]))
            link(dve.tensor_copy(sel[:, :, 0, :], ind))
            link(dve.tensor_tensor(sel[:, :, 1, :], ind, small[:, 3].unsqueeze(2).broadcast_to([P, NT, H]), ALU.mult))
            at("rt0")
            for j in range(NT):
                src = take().rearrange("p (s d) -> p s d", d=HD)
                w = sel[:, j].rearrange("p s h -> p (s h)").unsqueeze(2).broadcast_to([P, 2 * H, HD])
                dve.tensor_tensor(kv_tmp.rearrange("p (s d) -> p s d", d=HD), src, w, ALU.mult).then_inc(d_drained, 1)
                dve.wait_ge(d_drained, n[0])
                link(dve.tensor_reduce(kvs[:, j], kv_tmp.rearrange("p (s h d) -> p s d h", s=2, h=H), AX, ALU.add))
            dve.wait_ge(v_cleared, 3)
            dve.tensor_copy(Vg[:, :, 0:HD], kvs[:, :, 1, :]).then_inc(ksel_ready, 1)
            at("kv0")
            split(0, A["v0"] + 1)
            split(1, A["v0"] + 2)
            split(2, A["gk"], HD)
            attention(GROUPS[0])
            dve.wait_ge(w1_in, 16 * N_W1)
            for u in range(FC // 2):
                src = take().rearrange("p (j d) -> p j d", j=2)
                for k in range(2):
                    m = 2 * u + k
                    op = dve.scalar_tensor_tensor(w_dn[:, m, :], src[:, k, :], su[:, DC + m:DC + m + 1], ws_dp,
                                                  ALU.mult, ALU.mult)
                op.then_inc(d_drained, 1)
            at("wdn")
            for u in range(NT // 2):
                add_down(u)
            at("down0")

            norm(1)
            link(dve.memset(K1[RANK:RANK + 1, :], 1.0))
            dve.memset(V1[:, :, D:D + 1], 1.0).then_inc(ones1_ready, 1)
            for j, part, w in MAX1:
                dve.tensor_reduce(mx[:, j, part, 0:1], take()[:, 0:w], AX, ALU.max).then_inc(d_drained, 1)
            negated_maxima(1)
            maxima_rows(mrow, NT)
            at("mrowL1")
            for m in range(FC):
                dve.wait_ge(a_drained, A["s1"] + m + 1)
                for half in range(2):
                    gated_up(slot(Qs, m), gate[:, m % 2, :], half, su[:, DC + FC + m:DC + FC + m + 1])
            at("up1")
            for j in range(NT):
                src = take()
                link(dve.reciprocal(rec[:, 0, 0:1], src[:, D:D + 1]))
                dve.scalar_tensor_tensor(x[:, j, :], src[:, 0:D], rec[:, 0, 0:1], x[:, j, :],
                                         ALU.mult, ALU.add).then_inc(d_drained, 1)
                dve.wait_ge(d_drained, n[0])
            at("pv1")
            for u in range(NT // 2):
                add_down(u)
            at("down1")

            norm(2)
            NR = E + 1
            r9 = [lr[:, k, :].rearrange("p (j e) -> p j e", e=NR) for k in range(9)]
            sc, eq, ind1, ind2, rest, t1, comb = (r9[k][:, :, 0:E] for k in (0, 1, 2, 3, 4, 5, 6))
            m1, m2, best = (lr[:, 7, k * NT:(k + 1) * NT] for k in range(3))
            rank = tie[:, H - E:H].unsqueeze(1).broadcast_to([P, NT, E])
            args = lr[:, 9, 0:3 * NT].rearrange("p (j s) -> p j s", s=3)

            def over(v):
                return v.unsqueeze(2).broadcast_to([P, NT, E])

            dve.tensor_copy(lr[:, 0, :], take()[:, 0:NT * NR]).then_inc(d_drained, 1)
            at("rt2")
            dve.wait_ge(d_drained, n[0])
            link(dve.tensor_reduce(m1, sc, AX, ALU.max))
            link(dve.tensor_tensor(eq, sc, over(m1), ALU.is_equal))
            first_of(ind1, eq, best, E, rank)
            link(dve.tensor_scalar(t1, ind1, -1.0, 1.0, ALU.mult, ALU.add))
            link(dve.tensor_tensor(rest, sc, t1, ALU.mult))
            link(dve.tensor_scalar(t1, ind1, LOWEST, None, ALU.mult))
            link(dve.tensor_tensor(rest, rest, t1, ALU.add))
            link(dve.tensor_reduce(m2, rest, AX, ALU.max))
            link(dve.tensor_tensor(eq, rest, over(m2), ALU.is_equal))
            first_of(ind2, eq, best, E, rank)
            link(dve.tensor_tensor(args[:, :, 0], m1, m2, ALU.subtract))
            link(dve.tensor_tensor(args[:, :, 1], m2, m1, ALU.subtract))
            dve.tensor_copy(args[:, :, 2], r9[0][:, :, E]).then_inc(se_args, 1)
            dve.wait_ge(se_ready, 1)
            link(dve.tensor_tensor(ind1, ind1, over(sig3[:, :, 0]), ALU.mult))
            link(dve.tensor_tensor(ind2, ind2, over(sig3[:, :, 1]), ALU.mult))
            dve.tensor_tensor(comb, ind1, ind2, ALU.add).then_inc(comb_ready, 1)
            for u in range(4):
                if 3 + u >= 6:
                    dve.wait_ge(split_stored[0], 32)
                split(3 + u, A["cT"] + u + 1)
            attention(GROUPS[2])
            dve.wait_ge(w3_in, 16 * N_W3)
            link(dve.memset(gam[:], 0.0))
            full, last = F3 // P, F3 % P
            for k, w in enumerate((w31, w32, w33[:, 0:full, :])):
                link(dve.tensor_reduce(gam[:, k:k + 1], w.rearrange("p c n -> p (c n)"), AX, ALU.add,
                                       apply_absolute_value=True))
            dve.tensor_reduce(gam[0:last, 3:4], w33[0:last, full, :], AX, ALU.add,
                              apply_absolute_value=True).then_inc(gsum_ready, 1)
            src = take()
            dve.tensor_copy(gam[:, 4:8], src[:, 0:4]).then_inc(d_drained, 1)
            at("gsum")
            dve.wait_ge(d_drained, n[0])
            link(dve.tensor_tensor(gam[:, 6:7], gam[:, 6:7], gam[:, 7:8], ALU.add))
            link(dve.tensor_scalar(gam[:, 4:7], gam[:, 4:7], 1.0 / (D * F3), EPS_Q, ALU.mult, ALU.add))
            link(dve.tensor_scalar(gam[:, 8:11], gam[:, 4:7], 0.5, None, ALU.mult))
            link(dve.tensor_scalar(gam[:, 4:7], gam[:, 4:7], -0.5, None, ALU.mult))
            pieces = [(k, w[0:(f3_rows(c) if k == 2 else P), c, :]) for k, w in enumerate((w31, w32, w33))
                      for c in range(w.shape[1])]

            def quantise(k, v):
                r = v.shape[0]
                tmp = q_tmp[0:r, 0:v.shape[1]]
                link(dve.tensor_scalar(tmp, v, gam[0:r, 4 + k:5 + k], None, ALU.is_lt))
                link(dve.scalar_tensor_tensor(v, v, gam[0:r, 8 + k:9 + k], tmp, ALU.is_gt, ALU.subtract))

            for m in range(E + DC):
                if m < E:
                    dve.wait_ge(gated, m + 1)
                else:
                    dve.wait_ge(a_drained, A["oT2"] + m + 1)
                for half in range(2):
                    gated_up(slot(Qs, m) if m < E else slot(Ks, m - E), gate[:, m % 2, :], half)
                if m < len(pieces):
                    quantise(*pieces[m])
            assert len(pieces) <= E + DC
            dve.tensor_copy(gam[:, 11:12], gam[:, 10:11]).then_inc(quantised, 1)
            at("up2")
            for u in range(NT // 2):
                add_down(u)
                dve.wait_ge(d_drained, n[0])
                src = take().rearrange("p (j d) -> p j d", j=2)
                for k in range(2):
                    j = 2 * u + k
                    op = dve.scalar_tensor_tensor(x[:, j, :], src[:, k, :], sig3[:, j, 2:3], x[:, j, :],
                                                  ALU.mult, ALU.add)
                op.then_inc(d_drained, 1)

            norm(3)
            for c in range(DC):
                dve.wait_ge(a_drained, A["xnT3"] + c + 1)
                for half in range(2):
                    biased_times(slot(Qs, 4 + c), slot(Qs, c), half, su[:, 2 * DC + c:2 * DC + c + 1])
                dve.wait_ge(d_drained, n[0])
                dve.tensor_tensor_scan(slot(Qs, 6 + c), onesf[:, 0:1].broadcast_to([P, T]), slot(Qs, 4 + c), 0.0,
                                       ALU.mult, ALU.add).then_inc(cum_ready, 1)
            at("v3")
            for c in range(DC):
                dve.wait_ge(a_drained, A["k3"] + c + 1)
                for half in range(2):
                    biased_times(slot(Qs, c), slot(Qs, 2 + c), half, su[:, c:c + 1])
            at("q3")
            for m in range(F3C):
                dve.wait_ge(a_drained, A["g3"] + m + 1)
                r = f3_rows(m)
                for half in range(2):
                    gated_up(slot(Ks, m, r), gate[0:r, m % 2, :], half)
            at("up3")
            for u in range(NT // 2):
                add_down(u)
            at("down3")

        @block.tensor
        def _(pe):
            na, nd = [0], [0]

            def a_unit():
                na[0] += 1
                if na[0] > 2:
                    pe.wait_ge(a_drained, na[0] - 2)
                return psA[:, (na[0] - 1) % 2, :]

            def d_unit():
                nd[0] += 1
                if nd[0] > 2:
                    pe.wait_ge(d_drained, nd[0] - 2)
                return psD[:, (nd[0] - 1) % 2, :]

            def at(name_a, name_d):
                assert name_a is None or na[0] == A[name_a], (name_a, na[0])
                assert name_d is None or nd[0] == DU[name_d], (name_d, nd[0])

            def product(dst, terms, start=True, stop=True):
                for k, (lhsT, rhs) in enumerate(terms):
                    op = pe.matmul(dst, lhsT, rhs, start=start and k == 0, stop=stop and k == len(terms) - 1)
                return op

            def features(weights, rhs, chunks=None):
                dst = a_unit()
                for half in range(2):
                    c = slice(half * HALF, (half + 1) * HALF)
                    terms = [(weights(k), rhs(k, c)) for k in (chunks or range(DC))]
                    op = product(dst[0:terms[0][0].shape[1], c], terms)
                op.then_inc(a_filled, 1)

            def features_half(weights, rhs, half):
                dst = d_unit()
                c = slice(half * HALF, (half + 1) * HALF)
                terms = [(weights(k), rhs(k, c)) for k in range(DC)]
                product(dst[0:terms[0][0].shape[1], :], terms).then_inc(d_filled, 1)

            def normed(k, c):
                return xnT[:, k, c]

            def cols(w, a, b):
                return lambda k: w[:, k, a:b]

            def transposed(src, ready=None):
                for c in range(DC):
                    dst = a_unit()
                    for j in range(NT):
                        if ready is not None and c == 0:
                            pe.wait_ge(xn_ready, ready + j + 1)
                        op = pe.transpose(dst[:, tile_cols(j)], src[:, j, c * P:(c + 1) * P], identf[:])
                    op.then_inc(a_filled, 1)

            def value_units(lhsT, rhs, chunks):
                for u in range(2):
                    dst = a_unit()
                    for j in range(4):
                        op = product(dst[:, j * D:(j + 1) * D],
                                     [(lhsT(k, tile_cols(4 * u + j)), rhs(k)) for k in chunks])
                    op.then_inc(a_filled, 1)

            def maxima_unit(i, j, h0, nh, w, part):
                dst = d_unit()
                rows = MLA if is_mla(i) else STACK
                for k in range(nh):
                    h = h0 + k
                    q = head_rows(Qs, i, h, rows, j * P, (j + 1) * P)
                    kk = key_rows(i, h, rows, part * HALF, part * HALF + w)
                    if is_mla(i):
                        q, kk = high(q), high(kk)
                    diagonal = part == (j >= NT // 2)
                    op = pe.matmul(dst[:, k * w:(k + 1) * w], q, kk, start=True, stop=not diagonal)
                    if diagonal:
                        op = pe.matmul(dst[:, (k + 1) * w - P:(k + 1) * w], identb[:], maskq[:], start=False, stop=True)
                op.then_inc(d_filled, 1)

            def maxima_transpose(i, heads):
                pe.wait_ge(max_ready, maxima_of(i))
                dst = d_unit()
                pe.transpose(dst[0:heads * NT, 0:P], mneg[:, 0:heads, :].rearrange("p h j -> p (h j)"),
                             identf[:]).then_inc(d_filled, 1)

            def scores_T(dst, base, k, q, kt, half):
                lo = max(kt * P, half * HALF)
                diagonal = kt * P >= half * HALF
                out_ = dst[:, base + lo - half * HALF:base + HALF]
                op = pe.matmul(out_, k, q(lo, (half + 1) * HALF), start=True, stop=not diagonal)
                if diagonal:
                    op = pe.matmul(out_[:, 0:P], identb[:], maskk[:], start=False, stop=True)
                return op

            def score_units(i, kt):
                rows = MLA + 1 if is_mla(i) else STACK + 1

                def one(heads):
                    dst = a_unit()
                    for b, h in enumerate(heads):
                        k = key_rows(i, h, rows, kt * P, (kt + 1) * P)
                        q = lambda lo, hi: head_rows(Qs, i, h, rows, lo, hi)
                        if len(heads) == 1:
                            for half in range(2):
                                op = scores_T(dst, half * HALF, k, q, kt, half)
                        else:
                            op = scores_T(dst, b * HALF, k, q, kt, 1)
                    op.then_inc(a_filled, 1)
                step = 1 if kt < NT // 2 else 2
                return [list(range(h, h + step)) for h in range(0, GH, step)], one

            def values_product(i, kt, scored):
                s = NT * i + kt
                pe.wait_ge(a_drained, scored)
                if kt == 0 and i > 0:
                    pe.wait_ge(o_drained, i)
                for half in range(2):
                    if kt * P >= (half + 1) * HALF:
                        continue
                    lo, hi = max(kt * P, half * HALF), (half + 1) * HALF
                    last_kt = hi // P - 1
                    for h in range(GH):
                        e = Pr[:, ((s % 2) * GH + h) * T + lo:((s % 2) * GH + h) * T + hi]
                        op = pe.matmul(psO[h * VW:(h + 1) * VW, lo:hi], values(i, kt, h), e,
                                       start=kt == 0, stop=kt == last_kt, tile_position=(0, h * VW),
                                       skip_group_check=True)
                op.then_inc(pv_done, 1)

            def output_transposes(i):
                pe.wait_ge(o_drained, i + 1)
                for b in range(2):
                    dst = d_unit()
                    for j in range(4):
                        op = pe.transpose(dst[:, tile_cols(j)], OT[:, tile_cols(4 * b + j)], identf[:])
                    op.then_inc(d_filled, 1)

            def attention(groups):
                def arrived(i):
                    pe.wait_ge(stack_in[i % 4], stacks(i))
                    if is_mla(i):
                        pe.wait_ge(kr_in, 16 * N_KR)
                    elif i < 2 * NG:
                        pe.wait_ge(kg_in, 16 * N_KG)
                arrived(groups[0])
                for j, part, h0, nh, w in MAX_UNITS:
                    maxima_unit(groups[0], j, h0, nh, w, part)
                maxima_transpose(groups[0], GH)
                behind = None
                for i in groups:
                    nxt = i + 1 if i + 1 in groups else None
                    pe.wait_ge(mrow_in, 16 * maxima_of(i))
                    for kt in range(NT):
                        heads, one = score_units(i, kt)
                        ahead = []
                        if nxt is not None:
                            ahead = max_chunk(is_mla(nxt), kt)
                            if ahead and kt == (2 if is_mla(nxt) else 0):
                                arrived(nxt)
                        for k, hs in enumerate(heads):
                            one(hs)
                            for j, part, h0, nh, w in ahead[k * len(ahead) // len(heads):(k + 1) * len(ahead) // len(heads)]:
                                maxima_unit(nxt, j, h0, nh, w, part)
                        scored = na[0]
                        if behind is not None:
                            values_product(*behind)
                        behind = (i, kt, scored)
                        if kt == 1 and i - 1 in groups:
                            output_transposes(i - 1)
                        if nxt is not None and kt == MAX_END:
                            maxima_transpose(nxt, GH)
                values_product(*behind)
                output_transposes(groups[-1])

            pe.wait_ge(consts_in, 16 * N_CONSTS)
            pe.wait_ge(w0_in, 16 * N_W0)
            transposed(xn, ready=0)
            at("xnT0", None)
            pe.wait_ge(a_drained, A["xnT0"])
            features(cols(w_lat, 0, P), normed)
            pe.wait_ge(rotated, 4)
            features_half(cols(w_kr, 0, P), normed, 0)
            features_half(cols(w_kr, 0, P), normed, 1)
            pe.wait_ge(a_drained, A["lat"])
            ql = lambda k, c: lat[0:LAT, c]
            kvl = lambda k, c: lat[LAT:P, c]
            for m in range(2):
                features(lambda k: w_u[0:LAT, tile_cols(m)], ql, [0])
            for m in range(2):
                features(lambda k: w_u[LAT:P, tile_cols(m)], kvl, [0])
            value_units(kvl, lambda k: w_vu[LAT:P, :], [0])
            at("v0", "kr")
            for p in range(H // 2):
                for w in (w_qr, w_qrot):
                    for half in range(2):
                        pe.matmul(d_unit(), w[0:LAT, tile_cols(p)], lat[0:LAT, half * HALF:(half + 1) * HALF],
                                  start=True, stop=True).then_inc(d_filled, 1)
            dst = d_unit()
            for j in range(NT):
                op = product(dst[:, j * H:(j + 1) * H], [(xnT[:, k, tile_cols(j)], w_g0[:, k, :]) for k in range(DC)])
            op.then_inc(d_filled, 1)
            for j in range(NT):
                product(d_unit(), [(xnT[:, k, tile_cols(j)], w_qkv0[:, k, D:3 * D]) for k in range(DC)]).then_inc(d_filled, 1)
            for m in range(2):
                features(cols(w_qkv0, m * P, (m + 1) * P), normed)
            pe.wait_ge(ksel_ready, 1)
            dst = a_unit()
            for j in range(NT):
                op = pe.transpose(dst[0:HD, tile_cols(j)], kvs[:, j, 0, :], identf[:])
            op.then_inc(a_filled, 1)
            at("gk", "kv0")
            attention(GROUPS[0])
            pe.wait_ge(butterflies, 1)
            for u in range(FC // 2):
                pe.matmul(d_unit(), had[:], fT8[:, 2 * u:2 * u + 2, :].rearrange("p c d -> p (c d)"), start=True, stop=True).then_inc(d_filled, 1)
            transposed(xn)
            pe.wait_ge(a_drained, A["oT0"])

            def down(groups_of_terms, head=None):
                for u in range(NT // 2):
                    dst = d_unit()
                    for k in range(2):
                        j = 2 * u + k
                        op = product(dst[:, k * D:(k + 1) * D], groups_of_terms(tile_cols(j)))
                    op.then_inc(d_filled, 1)

            down(lambda t: [(fT[:, k, t], w_o0[:, k, :]) for k in range(DC)])
            at("oT0", "down0")

            transposed(xn, ready=NT)
            pe.wait_ge(a_drained, A["xnT1"])
            pe.wait_ge(w1b_in, 16 * N_W1B)
            features(cols(w_sa, 0, 2 * RANK), normed)
            value_units(normed, lambda k: w_o1[:, k, :], range(DC))
            pe.wait_ge(a_drained, A["qk1"])
            for j, part, w in MAX1:
                dst = d_unit()
                diagonal = part == (j >= NT // 2)
                op = pe.matmul(dst[:, 0:w], Q1[0:RANK, tile_cols(j)], K1[0:RANK, part * HALF:part * HALF + w],
                               start=True, stop=not diagonal)
                if diagonal:
                    op = pe.matmul(dst[:, w - P:w], identb[:], maskq[:], start=False, stop=True)
                op.then_inc(d_filled, 1)
            pe.wait_ge(had_ready, 1)
            for c in range(DC):
                features(cols(h256, c * P, (c + 1) * P), normed)
            maxima_transpose("L1", 1)
            pe.wait_ge(mrow_in, 16 * maxima_of("L1"))
            pe.wait_ge(ones1_ready, 1)
            for kt in range(NT):
                dst = a_unit()
                for half in range(2):
                    if kt * P < (half + 1) * HALF:
                        op = scores_T(dst, half * HALF, K1[0:RANK + 1, tile_cols(kt)],
                                      lambda lo, hi: Q1[0:RANK + 1, lo:hi], kt, half)
                op.then_inc(a_filled, 1)
            at("s1", "mrowL1")
            hadamard = lambda k, c: fT[:, k, c]
            for m in range(FC):
                features(cols(w_gt, m * P, (m + 1) * P), hadamard)
                for half in range(2):
                    features_half(cols(w_up, m * P, (m + 1) * P), hadamard, half)
            for j in range(NT):
                dst = d_unit()
                product(dst[:, 0:D + 1], [(slot(Pr, kt)[:, tile_cols(j)], V1[:, kt, :]) for kt in range(j + 1)]).then_inc(d_filled, 1)
            pe.wait_ge(d_drained, DU["up1"])
            down(lambda t: [(onesf[0:1, :], bor[0:1, :])] + [(slot(Qs, m)[:, t], w_dn[:, m, :]) for m in range(FC)])
            at("gate1", "down1")

            transposed(xn, ready=2 * NT)
            pe.wait_ge(a_drained, A["xnT2"])
            pe.wait_ge(w2_in, 16 * N_W2)
            dst = d_unit()
            for j in range(NT):
                op = product(dst[:, j * (E + 1):(j + 1) * (E + 1)],
                             [(xnT[:, k, tile_cols(j)], w_rt2[:, k, :]) for k in range(DC)])
            op.then_inc(d_filled, 1)
            pe.wait_ge(comb_ready, 1)
            dst = a_unit()
            comb = lr[:, 6, :].rearrange("p (j e) -> p j e", e=E + 1)
            for j in range(NT):
                op = pe.transpose(dst[0:E, tile_cols(j)], comb[:, j, 0:E], identf[:])
            op.then_inc(a_filled, 1)
            for m in range(4):
                features(cols(w_qkv2, m * P, (m + 1) * P), normed)
            value_units(normed, lambda k: w_qkv2[:, k, 2 * D:3 * D], range(DC))
            at("v2", "rt2")
            attention(GROUPS[2])
            pe.wait_ge(gsum_ready, 1)
            pe.matmul(d_unit()[:, 0:4], onesf[:], gam[:, 0:4], start=True, stop=True).then_inc(d_filled, 1)
            transposed(xn)
            for m in range(E + DC):
                if m == E:
                    pe.wait_ge(moe_in, 16 * N_MOE)
                a, b = tile_cols(m % E).start, tile_cols(m % E).stop
                features(cols(w_eg if m < E else w_sg, a, b), normed)
                for half in range(2):
                    features_half(cols(w_eu if m < E else w_su, a, b), normed, half)
            pe.wait_ge(moe_in, 16 * N_MOE)
            pe.wait_ge(a_drained, A["oT2"])
            pe.wait_ge(d_drained, DU["up2"])
            for u in range(NT // 2):
                for terms in (
                        lambda t: [(fT[:, k, t], w_o2[:, k, :]) for k in range(DC)]
                        + [(slot(Qs, e)[:, t], w_ed[:, e, :]) for e in range(E)],
                        lambda t: [(slot(Ks, m)[:, t], w_sd[:, m, :]) for m in range(DC)]):
                    dst = d_unit()
                    for k in range(2):
                        op = product(dst[:, k * D:(k + 1) * D], terms(tile_cols(2 * u + k)))
                    op.then_inc(d_filled, 1)

            transposed(xn, ready=3 * NT)
            pe.wait_ge(a_drained, A["xnT3"])
            pe.wait_ge(w3_in, 16 * N_W3)
            pe.wait_ge(w3m_in, 16 * N_W3M)
            w3 = lambda n, c: (lambda k: w3m[:, n * DC + k, c * P:(c + 1) * P])
            for c in range(DC):
                features(w3(1, c), normed)
                for half in range(2):
                    features_half(w3(2, c), normed, half)
            for c in range(DC):
                features(w3(3, c), normed)
                for half in range(2):
                    features_half(w3(0, c), normed, half)
            pe.wait_ge(quantised, 1)
            for m in range(F3C):
                a, b = m * P, m * P + f3_rows(m)
                features(cols(w31, a, b), normed)
                for half in range(2):
                    features_half(cols(w32, a, b), normed, half)
            pe.wait_ge(d_drained, DU["up3"])
            pe.wait_ge(y3_ready, DC)
            for u in range(NT // 2):
                dst = d_unit()
                for k in range(2):
                    t = tile_cols(2 * u + k)
                    product(dst[:, k * D:(k + 1) * D],
                            [(slot(Ks, m, f3_rows(m))[:, t], w33[0:f3_rows(m), m, :]) for m in range(F3C)], stop=False)
                    for c in range(DC):
                        op = pe.matmul(dst[:, k * D + c * P:k * D + (c + 1) * P], slot(Qs, 4 + c)[:, t], identf[:],
                                       start=False, stop=c == DC - 1)
                op.then_inc(d_filled, 1)
            at("sig3", "down3")


def constants():
    def bf16(v):
        return (np.ascontiguousarray(v, np.float32).view(np.uint32) >> 16).astype(np.uint16)

    freqs = 1.0 / 10000.0 ** (np.arange(0, RD, 2, dtype=np.float32) / RD)
    ang = np.outer(np.arange(T, dtype=np.float32), freqs)
    table = lambda f: np.ascontiguousarray(np.tile(f(ang), (1, 4)).T.astype(np.float32))
    k = np.arange(D)
    parity = np.array([bin(v).count("1") & 1 for v in range(D)])
    hadamard = (1.0 - 2.0 * parity[k[:, None] & k[None, :]]).astype(np.float32)
    later = np.triu(np.ones((P, P), np.float32), 1) * np.float32(-1e30)
    return {
        "c_ident": np.eye(P, dtype=np.float32), "c_identb": bf16(np.eye(P)),
        "c_had": hadamard[:P, :P] / np.float32(np.sqrt(INTER)),
        "c_h256": hadamard / np.float32(np.sqrt(D)),
        "c_maskq": bf16(later), "c_maskk": bf16(later.T),
        "c_tie": np.tile(np.arange(H, 0, -1, dtype=np.float32), (P, 1)),
        "c_cos": table(np.cos), "c_sin": table(np.sin),
        "c_ones": np.ones((1, T), np.float32), "c_ones4b": bf16(np.ones((1, GH * T))),
    }


def kernel(**inputs):
    import concourse.bacc as bacc
    from concourse.bass_utils import run_bass_kernel_spmd

    a = {k: np.asarray(v) for k, v in inputs.items()}
    col = lambda v: v.reshape(-1, P).T
    flat = lambda v: v.reshape(-1, v.shape[-1])
    arrays = {
        "x": a["L0_attn_x"].reshape(T, D),
        "w_lat": np.concatenate([a["L0_attn_Wqd"], a["L0_attn_Wkvd"]], 1),
        "Wkr": a["L0_attn_Wkr"], "Wqr": a["L0_attn_Wqr"], "Wqu": a["L0_attn_Wqu"], "Wku": a["L0_attn_Wku"],
        "Wvu": a["L0_attn_Wvu"], "Wo0": a["L0_attn_Wo"], "Wg0T": a["L0_ffn_W_gate"].T,
        "Wqkv0T": a["L0_ffn_W_qkv"].T,
        "W_upT": a["L1_ffn_W_up"].T, "W_gateT": a["L1_ffn_W_gate"].T, "W_downT": a["L1_ffn_W_down"].T,
        "Wo1T": a["L1_attn_Wo"].T, "Wsa": np.concatenate([a["L1_attn_Ws"], a["L1_attn_Wa"]], 1),
        "ws_dp": a["L1_ffn_Wscale_dp"].reshape(1, D), "bo": a["L1_attn_bo"].reshape(1, D),
        "su": np.concatenate([col(a["L1_ffn_SU_ug"]), col(a["L1_ffn_SU_dp"]), col(a["L1_ffn_Wscale_ug"])], 1),
        "Wqkv2T": a["L2_attn_w_qkv"].T, "Wo2T": a["L2_attn_w_out"].T,
        "Wrt2T": np.concatenate([a["L2_ffn_gate_w"], a["L2_ffn_se_gate_w"]], 0).T,
        "WegT": flat(a["L2_ffn_w_gate"]).T, "WeuT": flat(a["L2_ffn_w_up"]).T,
        "WsgT": a["L2_ffn_sh_gate"].T, "WsuT": a["L2_ffn_sh_up"].T, "WsdT": a["L2_ffn_sh_down"].T,
        "WedT": flat(a["L2_ffn_w_down"].transpose(0, 2, 1)),
        "Wq3T": a["L3_attn_Wq"].T, "Wk3T": a["L3_attn_Wk"].T, "Wv3T": a["L3_attn_Wv"].T, "Wg3T": a["L3_attn_Wg"].T,
        "b3": np.concatenate([col(a[f"L3_attn_b{n}"]) for n in "qkvg"], 1),
        "w31T": a["L3_ffn_w1"].T, "w32T": a["L3_ffn_w2"].T, "w33T": a["L3_ffn_w3"].T,
        **constants(),
    }
    arrays = {k: np.ascontiguousarray(v) for k, v in arrays.items()}
    nc = bacc.Bacc("TRN2", target_bir_lowering=False, num_devices=1)
    ins = {k: nc.dram_tensor(f"in_{k}", v.shape, mybir.dt.from_np(v.dtype), kind="ExternalInput").ap() for k, v in arrays.items()}
    out = nc.dram_tensor("out", (T, D), F32, kind="ExternalOutput").ap()
    build(nc, ins, out)
    r = run_bass_kernel_spmd(nc, [{f"in_{k}": v for k, v in arrays.items()}], core_ids=[0])
    return np.asarray(r.results[0]["out"]).reshape(1, T, D)
```

```python
from contextlib import ExitStack

import numpy as np
import concourse.bass as bass
from concourse import mybir

F32, F32R, BF16 = mybir.dt.float32, mybir.dt.float32r, mybir.dt.bfloat16
ALU = mybir.AluOpType
ACT = mybir.ActivationFunctionType
AX = mybir.AxisListType.X

P = 128
T, D = 1024, 256
NT, DC = T // P, D // P
HALF = 512
H, HD, RD, LAT = 16, 16, 64, 64
GH = 4
NG = H // GH
HV, VW = HD + 1, 32
RANK = 32
INTER, E, TOP, F3 = 1024, 8, 2, 704
FC = INTER // P
F3C = (F3 + P - 1) // P
EPS_LN, EPS_Q = 1e-5, 1e-8
LOWEST = -3.0e38
Q_PARTS = (0, 0, 0, 1, 1, 2)
K_PARTS = (0, 1, 2, 0, 1, 0)
STACK = len(Q_PARTS) * HD
MLA = RD + HD
MLA_ONE = RD + 3 * HD


def f3_rows(m):
    return min(P, F3 - m * P)


def max_units():
    for j in range(NT):
        for part in range(1 + (j >= NT // 2)):
            w = min(HALF, (j + 1) * P) if part == 0 else (j + 1) * P - HALF
            nh = {P: 4, 2 * P: 2}.get(w, 1)
            for h0 in range(0, GH, nh):
                yield j, part, h0, nh, w


MAX_UNITS = list(max_units())
MAX_END = 5


def max_chunk(late, kt):
    first = 1 if late else 0
    if not first <= kt < MAX_END:
        return []
    before = lambda k: sum(NT - n for n in range(first, k)) * len(MAX_UNITS)
    return MAX_UNITS[before(kt) // sum(NT - n for n in range(first, MAX_END)):
                     before(kt + 1) // sum(NT - n for n in range(first, MAX_END))]


def numbered(names):
    through, n = {}, 0
    for name, count in names:
        n += count
        through[name] = n
    return through


def build(nc, ins, out):
    with ExitStack() as ctx:
        offset = {}

        def sb(name, shape, dt=F32):
            t = ctx.enter_context(nc.sbuf_tensor(name, shape, dt))
            offset[name] = nc.sbuf_base - int(np.prod(shape[1:])) * (2 if dt == BF16 else 4)
            return t

        def over(base, name, shape, at=0):
            return nc.alloc_sbuf_tensor_at(name, shape, F32R, offset=offset[base] + 4 * at)

        def sem(name):
            return ctx.enter_context(nc.semaphore(name))

        def dram(name, shape, dt):
            return nc.dram_tensor(name, shape, dt, kind="Internal").ap()

        x = sb("x", [P, NT, D])
        xn = sb("xn", [P, NT, D])
        xnT = sb("xnT", [P, DC, T])
        fT = sb("fT", [P, DC, T])
        gate = sb("gate", [P, 2, T])
        Qs = sb("Qs", [P, 8 * T])
        Ks = sb("Ks", [P, 8 * T])
        Kg = sb("Kg", [P, T], BF16)
        Vh = sb("Vh", [P, NT, H * HV + VW - HV])
        Vg = sb("Vg", [P, NT, VW])
        Pr = sb("Pr", [P, 8 * T])
        OT = sb("OT", [P, T])
        WA = sb("WA", [P, 7186])
        WB = sb("WB", [P, 4352])
        identf = sb("identf", [P, P])
        had = sb("had", [P, P])
        onesf = sb("onesf", [P, P])
        identb = sb("identb", [P, P], BF16)
        maskq = sb("maskq", [P, P], BF16)
        maskk = sb("maskk", [P, P], BF16)
        tie = sb("tie", [P, H])
        stat = sb("stat", [P, NT, 6])
        mv = sb("mv", [P, NT, 2])
        ln = sb("ln", [P, 5, NT])
        mx = sb("mx", [P, NT, 2, GH])
        mneg = sb("mneg", [P, GH, NT])
        mrow = sb("mrow", [GH * NT, P])
        mrowb = sb("mrowb", [GH * NT, P], BF16)
        rec = sb("rec", [P, 4, GH])
        otmp = sb("otmp", [P, 4, GH, HD])
        rt = sb("rt", [P, 6, NT * H])
        sel = sb("sel", [P, NT, 2, H])
        kvs = sb("kvs", [P, NT, 2, HD])
        su = sb("su", [P, DC + 3 * FC])
        sig3 = sb("sig3", [P, NT, 3])
        gam = sb("gam", [P, 12])

        Qr, Kr = over("Qs", "Qr", [P, 8 * T]), over("Ks", "Kr", [P, 8 * T])
        Qr2 = [over("WB", "Qr2a", [P, GH * T]), over("fT", "Qr2b", [P, GH * T])]
        Kr2 = over("WA", "Kr2", [P, T], 5152)

        W3q = over("WB", "W3q", [P, WB.shape[1]])
        xn_high, xn_low = over("Pr", "xn_high", [P, DC, T]), over("Pr", "xn_low", [P, DC, T], 2 * T)
        hid_high, hid_low = over("Qs", "hid_high", [P, 8 * T]), over("Ks", "hid_low", [P, 8 * T])
        HIGH_PLACES = (0, 1, 2, 3, 6, 7)

        psA = ctx.enter_context(nc.psum_tensor("psA", [P, 2, 2 * HALF], F32))
        psD = ctx.enter_context(nc.psum_tensor("psD", [P, 2, HALF], F32))
        psO = ctx.enter_context(nc.psum_tensor("psO", [P, 2 * HALF], F32))

        lr = rt[:].rearrange("p k n -> p (k n)")[:, 0:10 * NT * (E + 1)].rearrange("p (k n) -> p k n", k=10)
        seT = OT[0:E, :]

        def carve(t):
            at = [0]

            def part(*dims):
                n = int(np.prod(dims))
                v = t[:, at[0]:at[0] + n]
                at[0] += n
                return v.rearrange("p (a b) -> p a b", a=dims[0]) if len(dims) == 2 else v
            return part

        part = carve(WA)
        w_lat, w_kr = part(DC, P), part(DC, 2 * RD)
        w_qr, w_qrot = part(H * RD), part(H * RD)
        w_u, w_vu = part(D), part(D)
        w_o0, w_g0, w_qkv0 = part(DC, D), part(DC, H), part(DC, 3 * D)
        w_qkv0_at = 3616
        part = carve(WA)
        w_qkv2, w_o2, w_rt2 = part(DC, 3 * D), part(DC, D), part(DC, E + 1)
        w_eg, w_eu, w_sg, w_sd = part(DC, E * P), part(DC, E * P), part(DC, D), part(DC, D)
        w_ed = Ks[:, 5 * T:7 * T].rearrange("p (e d) -> p e d", e=E)
        w_su = OT[:, 0:DC * D].rearrange("p (c d) -> p c d", c=DC)
        part = carve(WB)
        w_up, w_dn, ws_dp = part(DC, INTER), part(FC, D), part(D)
        part = carve(Ks[:, 4 * T:])
        w_gt, h256, w_o1, w_sa = part(DC, INTER), part(DC, D), part(DC, D), part(DC, 2 * RANK)
        bor = part(D)[0:1, :]
        part = carve(WB)
        w31, w32, w33 = part(DC, F3), part(DC, F3), part(F3C, D)
        part = carve(W3q)
        q31, q32, q33 = part(DC, F3), part(DC, F3), part(F3C, D)
        w3m = Vh[:].rearrange("p j v -> p (j v)")[:, 0:4 * DC * D].rearrange("p (c d) -> p c d", d=D)
        q_tmp = Kg
        cos, sin = gate[:, 0, :], gate[:, 1, :]
        lat = OT
        kr, kr_t = (xn[:].rearrange("p j d -> p (j d)")[0:RD, n * T:(n + 1) * T] for n in range(2))
        kv_tmp = WA[:, 6400:6400 + 2 * D]
        Q1 = OT
        K1 = Ks[:, 0:T]
        V1 = Ks[:, T:T + NT * (D + 1)].rearrange("p (j d) -> p j d", j=NT)
        fT8 = fT[:].rearrange("p c (e d) -> p (c e) d", d=D)

        def Vh_heads(j):
            return Vh[:, j, 0:H * HV].rearrange("p (h v) -> p h v", v=HV)

        def slot(t, n, rows=P, base=0):
            return t[base:base + rows, n * T:(n + 1) * T]

        def split_place(u):
            if u < 3:
                b = (0, w_qkv0_at, 3 * HALF)[u]
                return ((xnT[:, 0, :], xnT[:, 1, :], OT[:])[u],
                        WA[:, b:b + 3 * HALF].bitcast(BF16).rearrange("p (s t) -> p s t", s=3))
            b = 2560 * (u % 3)
            return (Pr[:, b:b + T],
                    Pr[:, b + T:b + 2560].bitcast(BF16).rearrange("p (s t) -> p s t", s=3))

        def tile_cols(j):
            return slice(j * P, (j + 1) * P)

        d_qr = dram("d_qr", (2, H * RD, T), F32)
        d_qn = dram("d_qn", (2, D, T), F32)
        d_kn = dram("d_kn", (2, D, T), F32)
        d_gq = dram("d_gq", (3, D, T), BF16)
        d_gk = dram("d_gk", (3, HD, T), BF16)
        d_q2 = dram("d_q2", (3, D, T), BF16)
        d_k2 = dram("d_k2", (3, D, T), BF16)
        d_cb = dram("d_cb", (E, T), F32)

        GROUPS = {0: list(range(0, 2 * NG)), 2: list(range(2 * NG, 3 * NG))}
        LAST = 3 * NG - 1

        def is_mla(i):
            return i < NG

        def late(i):
            return i <= NG

        def head_rows(t, i, h, rows, a, b):
            if is_mla(i):
                o = ((i % 2) * GH + h) * T
                return (Qr if t is Qs else Kr)[0:rows, o + a:o + b]
            o = ((i % 4) * GH + h) * T
            return t[:].bitcast(BF16)[0:rows, o + a:o + b]

        def key_rows(i, h, rows, a, b):
            return Kg[0:rows, a:b] if NG <= i < 2 * NG else head_rows(Ks, i, h, rows, a, b)

        def high(ap):
            return ap.bitcast(BF16).rearrange("p (t w) -> p t w", w=2)[:, :, 1]

        def values(i, kt, h):
            return Vg[:, kt, :] if NG <= i < 2 * NG else Vh[:, kt, (h + GH * (i % NG)) * HV:(h + GH * (i % NG)) * HV + VW]

        def score_scale(i):
            return float(1.0 / np.sqrt(np.float32(HD + RD))) if is_mla(i) else HD ** -0.5

        def maxima(i):
            return i + 1 if i < 2 * NG else (2 * NG + 1 if i == "L1" else i + 2)

        def maxima_of(i):
            return 2 * NG + 1 if i == "L1" else maxima(i)

        A_GROUP = 4 * GH + 4 * GH // 2
        A = numbered(
            [("xnT0", DC), ("lat", 1), ("qn", 2), ("kn", 2), ("v0", 2), ("gq", 2), ("gk", 1)]
            + [(f"att{i}", A_GROUP) for i in GROUPS[0]] + [("oT0", DC)]
            + [("xnT1", DC), ("qk1", 1), ("v1", 2), ("xh", DC), ("s1", NT), ("gate1", FC)]
            + [("xnT2", DC), ("cT", 1), ("qk2", 4), ("v2", 2)]
            + [(f"att{i}", A_GROUP) for i in GROUPS[2]] + [("oT2", DC), ("gate2", E + DC)]
            + [("xnT3", DC), ("k3", DC), ("g3", DC), ("sig3", F3C)])
        NMAX = len(MAX_UNITS)

        def d_groups(groups):
            return [x for i in groups for x in ((f"max{i}", NMAX), (f"mrow{i}", 1), (f"o{i}", 2))]

        def d_attention(groups):
            names = [(f"max{groups[0]}", NMAX), (f"mrow{groups[0]}", 1)]
            for i in groups:
                nxt = i + 1 if i + 1 in groups else None
                for kt in range(NT):
                    if nxt is not None:
                        names.append((f"max{nxt}.{kt}", len(max_chunk(late(nxt), kt))))
                    if kt == 1 and i - 1 in groups:
                        names.append((f"o{i - 1}", 2))
                    if nxt is not None and kt == MAX_END:
                        names.append((f"mrow{nxt}", 1))
            return names + [(f"o{groups[-1]}", 2)]

        MAX1 = [(j, part, min(HALF, (j + 1) * P) if part == 0 else (j + 1) * P - HALF)
                for j in range(NT) for part in range(1 + (j >= NT // 2))]
        first_max = [("max", 0, u) for u in MAX_UNITS]
        PRE0 = [("rope", 0), ("rope", 1), ("router",), ("low", 0), ("rope", 2), ("low", 1), ("rope", 3), ("kv", 0), ("kv", 1),
                ("low", 2), ("rope", 4), ("kv", 2), ("low", 3), ("rope", 5), ("kv", 3), ("kv", 4), ("low", 4), ("rope", 6), ("kv", 5),
                ("low", 5), ("rope", 7), ("kv", 6), ("low", 6)]
        beside = {4: ("low", 7), 7: ("kv", 7), 10: ("ksel",), 12: ("gq", 0), 18: ("gq", 1), 24: ("gk",)}
        for k in range(NMAX):
            PRE0 += first_max[k:k + 1] + ([beside[k]] if k in beside else [])

        DU = numbered(
            [("kr", 2)] + [("".join(map(str, item[:2])), {"rope": 4, "low": 0, "ksel": 0, "gq": 0, "gk": 0}.get(item[0], 1)) for item in PRE0]
            + d_attention(GROUPS[0])[1:] + [("wdn", FC // 2), ("down0", NT // 2)]
            + [("maxL1", len(MAX1)), ("mrowL1", 1), ("up1", 2 * FC), ("pv1", NT), ("down1", NT // 2)]
            + [("rt2", 1)] + d_attention(GROUPS[2]) + [("gsum", 1), ("up2", 2 * (E + DC))]
            + [(f"down2.{u}", 2) for u in range(NT // 2)]
            + [("v3", 2 * DC), ("q3", 2 * DC), ("up3", 2 * F3C), ("down3", NT // 2)])

        x_in, consts_in, w0_in, w1_in, w2_in, w3_in, moe_in, w1b_in, w3m_in = (
            sem(n) for n in ("x_in", "consts_in", "w0_in", "w1_in", "w2_in", "w3_in", "moe_in", "w1b_in", "w3m_in"))
        a_filled, a_drained, d_filled, d_drained = (
            sem(n) for n in ("a_filled", "a_drained", "d_filled", "d_drained"))
        o_drained = sem("o_drained")
        ident_in, w0b_in = sem("ident_in"), sem("w0b_in")
        dve_step, pool_step = sem("dve_step"), sem("pool_step")
        v_cleared, rotated = sem("v_cleared"), sem("rotated")
        ln_var, ln_std, xn_ready = sem("ln_var"), sem("ln_std"), sem("xn_ready")
        kr_ready, rope_sum, rope_high, low_ready = sem("kr_ready"), sem("rope_sum"), sem("rope_high"), sem("low_ready")
        mla_stored, kr_in = sem("mla_stored"), sem("kr_in")
        rt_shift, rt_exp, ksel_ready = sem("rt_shift"), sem("rt_exp"), sem("ksel_ready")
        split_done = sem("split_done")
        split_stored = [sem(f"split_stored{n}") for n in range(3)]
        kg_in = sem("kg_in")
        rest_in = [sem(f"rest_in{n}") for n in range(2)]
        stack_in = [sem(f"stack_in{n}") for n in range(4)]
        max_ready, mrow_in = sem("max_ready"), sem("mrow_in")
        pv_done = sem("pv_done")
        butterflies, had_ready, ones1_ready = sem("butterflies"), sem("had_ready"), sem("ones1_ready")
        se_args, se_ready, comb_ready, comb_out, comb_in = (
            sem(n) for n in ("se_args", "se_ready", "comb_ready", "comb_out", "comb_in"))
        high3_ready, low3_ready, hid_split = sem("high3_ready"), sem("low3_ready"), sem("hid_split")
        hid_cut = sem("hid_cut")
        gsum_ready, quantised = sem("gsum_ready"), sem("quantised")
        gated, cum_ready, y3_ready, stored = sem("gated"), sem("cum_ready"), sem("y3_ready"), sem("stored")
        STACK_DMAS = {0: 3, 1: len(Q_PARTS), 2: len(Q_PARTS) + len(K_PARTS) + 1}
        REST_DMAS = 6
        N_KR, N_KG, N_MLA = 5, len(K_PARTS) + 1, 8 + H
        N_CONSTS, N_W0, N_W0B, N_W1, N_W1B, N_W2, N_W3, N_W3M, N_MOE = 7, 6, 3, 4, 5, 7, 5, 4, 2

        def stacks(i):
            return 16 * sum(STACK_DMAS[k // NG] for k in range(i % 4, i + 1, 4))

        block = ctx.enter_context(nc.Block())

        @block.sync
        def _(sp):
            def load(dst, src, s):
                sp.dma_start(dst, src).then_inc(s, 16)

            def tiles(name):
                return ins[name].rearrange("(c p) n -> p c n", p=P)

            for j in range(0, NT, 2):
                load(x[:, j:j + 2, :], ins["x"].rearrange("(j p) d -> p j d", p=P)[:, j:j + 2, :], x_in)
            load(identf[:], ins["c_ident"], ident_in)
            load(w_lat, tiles("w_lat"), w0_in)
            load(w_kr[:, :, 0:RD], tiles("Wkr"), w0_in)
            load(w_qr[0:LAT, :], ins["Wqr"], w0_in)
            load(w_u[0:LAT, :], ins["Wqu"], w0_in)
            load(w_u[LAT:P, :], ins["Wku"], w0_in)
            load(w_vu[LAT:P, :], ins["Wvu"], w0_in)
            load(cos, ins["c_cos"], consts_in)
            load(sin, ins["c_sin"], consts_in)
            for dst, name in ((tie, "c_tie"), (identb, "c_identb"), (maskq, "c_maskq"), (maskk, "c_maskk"), (had, "c_had")):
                src = ins[name]
                load(dst[:], src if dst.dtype == src.dtype else src.bitcast(BF16), consts_in)
            load(w_g0, tiles("Wg0T"), w0b_in)
            load(w_qkv0, tiles("Wqkv0T"), w0b_in)
            load(w_o0, tiles("Wo0"), w0b_in)

            for u in range(4):
                sp.wait_ge(low_ready, u + 1)
                for part in range(2):
                    load((d_qn, d_kn)[u // 2][part, tile_cols(u % 2), :], slot(Ks, 4 * part + u), mla_stored)
            sp.wait_ge(mla_stored, 16 * 8)
            sp.wait_ge(v_cleared, 3)
            sp.wait_ge(kr_ready, 1)
            def shared_key(first):
                places = Kr[0:RD, first * T:(first + GH) * T].bitcast(F32).rearrange("p (h t) -> p h t", h=GH)
                load(places, kr_t.unsqueeze(1).broadcast_to([RD, GH, T]), kr_in)
            shared_key(0)
            load(Kr[MLA_ONE:MLA_ONE + 1, :].bitcast(F32), onesf[0:8 * T // P, :], kr_in)
            load(Kr2[0:RD, :].bitcast(F32), kr, kr_in)
            load(Kr2[RD:2 * RD, :].bitcast(F32), kr_t, kr_in)

            def load_group(i):
                s, g = stack_in[i % 4], i % NG
                if is_mla(i):
                    o = (i % 2) * GH * T
                    for k, (t, a, n, d) in enumerate((
                            (Qr, 0, RD, d_qr[0]), (Qr, RD, HD, d_qn[0]), (Kr, RD, HD, d_kn[0]),
                            (Qr, RD + HD, HD, d_qn[0]), (Qr, RD + 2 * HD, HD, d_qn[1]),
                            (Kr, RD + HD, HD, d_kn[1]), (Kr, RD + 2 * HD, HD, d_kn[0]),
                            (Qr2[i % 2], 0, RD, d_qr[0]), (Qr2[i % 2], RD, RD, d_qr[1]))):
                        at = 0 if t is Qr2[i % 2] else o
                        load(t[a:a + n, at:at + GH * T].bitcast(F32).rearrange("p (h t) -> p h t", h=GH),
                             d[g * GH * n:(g + 1) * GH * n, :].rearrange("(h d) t -> d h t", d=n),
                             s if k < STACK_DMAS[0] else rest_in[i % 2])
                    return
                o, rows = (i % 4) * GH * T, slice(g * GH * HD, (g + 1) * GH * HD)

                def parts(t, d, order):
                    for r, part in enumerate(order):
                        load(t[:].bitcast(BF16)[r * HD:(r + 1) * HD, o:o + GH * T].rearrange("p (h t) -> p h t", h=GH),
                             d[part, rows, :].rearrange("(h d) t -> d h t", d=HD), s)
                parts(Qs, d_gq if i < 2 * NG else d_q2, Q_PARTS)
                if i >= 2 * NG:
                    parts(Ks, d_k2, K_PARTS)
                    load(Ks[:].bitcast(BF16)[STACK:STACK + 1, o:o + GH * T], ins["c_ones4b"].bitcast(BF16), s)

            def maxima_row(i):
                sp.wait_ge(d_drained, DU[f"mrow{i}"])
                if is_mla(i):
                    o = (i % 2) * GH * T
                    load(Qr[MLA_ONE:MLA_ONE + 1, o:o + GH * T].bitcast(F32), mrow[:], mrow_in)
                else:
                    o = (i % 4) * GH * T
                    load(Qs[:].bitcast(BF16)[STACK:STACK + 1, o:o + GH * T], mrowb[:], mrow_in)

            for p in range(H // 2):
                sp.wait_ge(low_ready, 4 + p + 1)
                for part in range(2):
                    load(d_qr[part, tile_cols(p), :], slot(Pr, 4 * (1 - part) + p % 4), mla_stored)
                sp.wait_ge(mla_stored, 16 * (8 + 2 * (p + 1)))
                if p in (1, H // 2 - 1):
                    load_group(min(p // 2, 1))
                    if p == 1:
                        shared_key(GH)
            maxima_row(0)
            for u in range(2):
                sp.wait_ge(split_done, u + 1)
                load(d_gq[:, tile_cols(u), :].rearrange("s d t -> d s t"), split_place(u)[1], split_stored[u])
            sp.wait_ge(split_done, 3)
            load(d_gk.rearrange("s d t -> d s t"), split_place(2)[1][0:HD], split_stored[2])
            sp.wait_ge(split_stored[2], 16)
            for r, part in enumerate(K_PARTS):
                load(Kg[r * HD:(r + 1) * HD, :], d_gk[part], kg_in)
            load(Kg[STACK:STACK + 1, :], ins["c_ones4b"][:, 0:T].bitcast(BF16), kg_in)
            sp.wait_ge(split_stored[0], 16)
            sp.wait_ge(split_stored[1], 16)
            for i in GROUPS[0]:
                if i + 1 in GROUPS[0]:
                    maxima_row(i + 1)
                for k in {0: (2,), 1: (3,), 2: (4, 5), 3: (6, 7)}.get(i, ()):
                    sp.wait_ge(a_filled, A[f"att{i}"])
                    load_group(k)
                if i == NG - 2:
                    load(w_up, tiles("W_upT"), w1_in)
                    load(w_dn, tiles("W_downT"), w1_in)
                    load(ws_dp, ins["ws_dp"].broadcast_to([P, D]), w1_in)
                    load(su[:], ins["su"], w1_in)

            sp.wait_ge(a_filled, A[f"att{2 * NG - 1}"])
            load(w_sa, tiles("Wsa"), w1b_in)
            load(w_o1, tiles("Wo1T"), w1b_in)
            load(h256, tiles("c_h256"), w1b_in)
            load(w_gt, tiles("W_gateT"), w1b_in)
            load(bor, ins["bo"], w1b_in)

            sp.wait_ge(d_drained, DU["down0"])
            load(w_qkv2, tiles("Wqkv2T"), w2_in)
            load(w_o2, tiles("Wo2T"), w2_in)
            load(w_rt2, tiles("Wrt2T"), w2_in)
            load(w_eg, tiles("WegT"), w2_in)
            load(w_eu, tiles("WeuT"), w2_in)
            load(w_sg, tiles("WsgT"), w2_in)
            load(w_sd, tiles("WsdT"), w2_in)

            sp.wait_ge(d_drained, DU["mrowL1"])
            load(Q1[RANK:RANK + 1, :], mrow[0:NT, :], mrow_in)

            sp.wait_ge(d_drained, DU["down1"])
            load(w31, tiles("w31T"), w3_in)
            load(w32, tiles("w32T"), w3_in)
            full = F3 // P
            load(w33[:, 0:full, :], ins["w33T"][0:full * P, :].rearrange("(c p) n -> p c n", p=P), w3_in)
            load(w33[0:F3 - full * P, full, :], ins["w33T"][full * P:F3, :], w3_in)
            load(su[:, 0:4 * DC], ins["b3"], w3_in)

            sp.wait_ge(a_drained, A["cT"])
            load(d_cb, seT[:], comb_out)
            for u in range(4):
                n = 3 + u
                sp.wait_ge(split_done, n + 1)
                load((d_q2, d_k2)[u % 2][:, tile_cols(u // 2), :].rearrange("s d t -> d s t"),
                     split_place(n)[1], split_stored[n % 3])
                if u == 1:
                    sp.wait_ge(split_stored[0], 16 * 2)
                    sp.wait_ge(split_stored[1], 16 * 2)
                    load_group(GROUPS[2][0])
                    load_group(GROUPS[2][1])
            sp.wait_ge(split_stored[0], 16 * 3)
            sp.wait_ge(split_stored[2], 16 * 2)
            load_group(GROUPS[2][2])
            load_group(GROUPS[2][3])
            for i in GROUPS[2]:
                maxima_row(i)
            sp.wait_ge(a_filled, A[f"att{LAST}"])
            load(w_ed, ins["WedT"].rearrange("(e p) n -> p e n", p=P), moe_in)
            sp.wait_ge(pv_done, NT * (LAST + 1))
            for n, name in enumerate(("Wq3T", "Wk3T", "Wv3T", "Wg3T")):
                load(w3m[:, n * DC:(n + 1) * DC, :], tiles(name), w3m_in)
            sp.wait_ge(comb_out, 16)
            for e in range(E):
                load(slot(Pr, e), d_cb[e:e + 1, :].broadcast_to([P, T]), comb_in)
            sp.wait_ge(d_drained, DU[f"o{LAST}"])
            load(w_su, tiles("WsuT"), moe_in)

            for u in range(NT // 2):
                sp.wait_ge(d_drained, DU["down3"] - NT // 2 + u + 1)
                load(out.rearrange("(j p) d -> p j d", p=P)[:, 2 * u:2 * u + 2, :], x[:, 2 * u:2 * u + 2, :], stored)
            sp.wait_ge(stored, 16 * NT // 2)

        @block.gpsimd
        def _(pool):
            steps = [0]

            def link(instr):
                steps[0] += 1
                instr.then_inc(pool_step, 1)
                pool.wait_ge(pool_step, steps[0])

            link(pool.memset(Vh[:], 0.0))
            link(pool.memset(Vg[:], 0.0))
            for j in range(NT):
                op = pool.memset(Vh_heads(j)[:, :, HD:HV], 1.0)
            op.then_inc(v_cleared, 1)
            pool.memset(Vg[:, :, HD:HD + 1], 1.0).then_inc(v_cleared, 1)
            pool.memset(onesf[:], 1.0).then_inc(v_cleared, 1)

            pool.wait_ge(w0_in, 16 * N_W0)
            h2 = RD // 2
            pool.tensor_scalar(w_kr[:, :, RD:RD + h2], w_kr[:, :, h2:RD], -1.0, None, ALU.mult).then_inc(rotated, 1)
            pool.tensor_copy(w_kr[:, :, RD + h2:2 * RD], w_kr[:, :, 0:h2]).then_inc(rotated, 1)
            src = w_qr[0:LAT, :].rearrange("p (h d) -> p h d", d=RD)
            dst = w_qrot[0:LAT, :].rearrange("p (h d) -> p h d", d=RD)
            pool.tensor_scalar(dst[:, :, 0:h2], src[:, :, h2:RD], -1.0, None, ALU.mult).then_inc(rotated, 1)
            pool.tensor_copy(dst[:, :, h2:RD], src[:, :, 0:h2]).then_inc(rotated, 1)

            pool.wait_ge(d_drained, DU["kr"])
            link(pool.tensor_tensor(kr, kr, kr_t, ALU.add))
            link(pool.tensor_copy(kr_t.bitcast(F32R), kr))
            pool.tensor_tensor(kr.bitcast(F32R), kr, kr_t, ALU.subtract).then_inc(kr_ready, 1)

            for p in range(H // 2):
                pool.wait_ge(d_drained, DU[f"rope{p}"])
                pool.tensor_tensor(slot(Pr, p % 4), slot(Pr, p % 4), slot(Pr, 4 + p % 4), ALU.add).then_inc(rope_sum, 1)

            def split(u, filled, rows=P):
                pool.wait_ge(a_drained, filled)
                v, b = split_place(u)
                v, b = v[0:rows], b[0:rows]
                link(pool.tensor_copy(b[:, 0], v))
                link(pool.tensor_tensor(v, v, b[:, 0], ALU.subtract))
                link(pool.tensor_copy(b[:, 1], v))
                pool.tensor_tensor(b[:, 2], v, b[:, 1], ALU.subtract).then_inc(split_done, 1)

            split(0, A["v0"] + 1)
            split(1, A["v0"] + 2)
            split(2, A["gk"], HD)

            pool.wait_ge(w1_in, 16 * N_W1)
            pool.wait_ge(a_filled, A[f"att{NG - 1}"])
            a, b = w_dn, fT8
            for s in range(3):
                g = 1 << s
                for q in range(0, FC, 2 * g):
                    lo, hi = slice(q, q + g), slice(q + g, q + 2 * g)
                    link(pool.tensor_tensor(b[:, lo], a[:, lo], a[:, hi], ALU.add))
                    op = pool.tensor_tensor(b[:, hi], a[:, lo], a[:, hi], ALU.subtract)
                    if s < 2:
                        link(op)
                    else:
                        op.then_inc(butterflies, 1)
                a, b = b, a
            pool.wait_ge(w1b_in, 16 * N_W1B)
            link(pool.tensor_scalar(h256[:, 0, :], h256[:, 0, :], su[:, 0:1], None, ALU.mult))
            pool.tensor_scalar(h256[:, 1, :], h256[:, 1, :], su[:, 1:2], None, ALU.mult).then_inc(had_ready, 1)

            pool.wait_ge(comb_in, 16 * E)
            for e in range(E):
                pool.wait_ge(a_drained, A["oT2"] + e + 1)
                pool.tensor_tensor(gate[:, e % 2, :], gate[:, e % 2, :], slot(Pr, e), ALU.mult).then_inc(gated, 1)

            for c in range(DC):
                pool.wait_ge(high3_ready, c + 1)
                pool.tensor_tensor(xn_low[:, c, :], xnT[:, c, :], xn_high[:, c, :], ALU.subtract).then_inc(low3_ready, 1)
            for c in range(DC):
                pool.wait_ge(cum_ready, c + 1)
                pool.wait_ge(d_drained, DU["v3"] + 2 * (c + 1))
                pool.tensor_tensor(slot(Qs, 4 + c), slot(Qs, c), slot(Qs, 6 + c), ALU.mult).then_inc(y3_ready, 1)
            for m in range(F3C):
                r = f3_rows(m)
                pool.wait_ge(hid_cut, m + 1)
                pool.tensor_tensor(slot(hid_low, m, r), slot(Ks, m, r), slot(hid_high, HIGH_PLACES[m], r),
                                   ALU.subtract).then_inc(hid_split, 1)

        @block.scalar
        def _(act):
            n = [0]

            def take():
                n[0] += 1
                act.wait_ge(a_filled, n[0])
                return psA[:, (n[0] - 1) % 2, :]

            def copy_units(dsts):
                for dst in dsts:
                    src = take()
                    act.activation(dst, src[0:dst.shape[0], :] if len(dst.shape) == 2 else src, ACT.Copy).then_inc(a_drained, 1)

            def std():
                std.n += 1
                act.wait_ge(ln_var, std.n)
                act.activation(ln[:, 1, :], ln[:, 0, :], ACT.Sqrt).then_inc(ln_std, 1)
            std.n = 0

            def value_units():
                for u in range(2):
                    src = take().rearrange("p (j h d) -> p j h d", j=4, h=H)
                    for j in range(4):
                        op = act.activation(Vh_heads(4 * u + j)[:, :, 0:HD], src[:, j], ACT.Copy)
                    op.then_inc(a_drained, 1)

            def attention(groups):
                for i in groups:
                    for kt in range(NT):
                        s = NT * i + kt
                        if s >= 2:
                            act.wait_ge(pv_done, s - 1)
                        place = Pr[:, (s % 2) * GH * T:(s % 2 + 1) * GH * T].rearrange("p (h t) -> p h t", h=GH)
                        q0 = kt * P
                        if kt < NT // 2:
                            for h in range(GH):
                                src = take()
                                act.activation(place[:, h, q0:T], src[:, q0:T], ACT.Exp,
                                               scale=score_scale(i)).then_inc(a_drained, 1)
                        else:
                            for h in range(0, GH, 2):
                                src = take().rearrange("p (h t) -> p h t", h=2)
                                act.activation(place[:, h:h + 2, q0:T], src[:, :, q0 - HALF:HALF], ACT.Exp,
                                               scale=score_scale(i)).then_inc(a_drained, 1)
                        if kt == 0 and i > groups[0]:
                            output(i - 1)
                output(groups[-1])

            def output(i):
                act.wait_ge(pv_done, NT * (i + 1))
                if i == 0:
                    act.wait_ge(split_done, 3)
                if f"o{i - 1}" in DU:
                    act.wait_ge(d_drained, DU[f"o{i - 1}"])
                if i == GROUPS[2][0]:
                    act.wait_ge(comb_out, 16)
                act.activation(OT[:], psO[:], ACT.Copy).then_inc(o_drained, 1)

            std()
            copy_units([xnT[:, c, :] for c in range(DC)])
            copy_units([lat[:]])
            for u in range(4):
                src = take()
                act.activation(slot(Ks, 4 + u), src, ACT.Copy)
                act.activation(slot(Ks, u).bitcast(F32R), src, ACT.Copy).then_inc(a_drained, 1)
            act.wait_ge(v_cleared, 3)
            value_units()
            for item in PRE0:
                if item[0] == "rope":
                    p = item[1]
                    act.wait_ge(rope_sum, p + 1)
                    act.activation(slot(Pr, 4 + p % 4).bitcast(F32R), slot(Pr, p % 4), ACT.Copy).then_inc(rope_high, 1)
                elif item[0] == "router":
                    act.wait_ge(rt_shift, 1)
                    act.activation(rt[:, 2, :], rt[:, 1, :], ACT.Exp).then_inc(rt_exp, 1)
            act.wait_ge(a_filled, n[0] + 2)
            copy_units([split_place(u)[0] for u in range(2)])
            copy_units([split_place(2)[0][0:HD]])
            act.wait_ge(mla_stored, 16 * N_MLA)
            attention(GROUPS[0])
            copy_units([fT[:, c, :] for c in range(DC)])
            std()
            copy_units([xnT[:, c, :] for c in range(DC)])
            src = take()
            act.activation(Q1[0:RANK, :], src[0:RANK, :], ACT.Copy)
            act.activation(K1[0:RANK, :], src[RANK:2 * RANK, :], ACT.Copy).then_inc(a_drained, 1)
            for u in range(2):
                src = take().rearrange("p (j d) -> p j d", d=D)
                act.activation(V1[:, 4 * u:4 * u + 4, 0:D], src, ACT.Copy).then_inc(a_drained, 1)
            copy_units([fT[:, c, :] for c in range(DC)])
            for kt in range(NT):
                src = take()
                act.activation(slot(Pr, kt)[:, kt * P:T], src[:, kt * P:T], ACT.Exp,
                               scale=float(1.0 / np.sqrt(RANK))).then_inc(a_drained, 1)
            for m in range(FC):
                src = take()
                if m >= 2:
                    act.wait_ge(d_drained, DU["mrowL1"] + 2 * (m - 1))
                act.activation(gate[:, m % 2, :], src, ACT.Silu,
                               scale=su[:, DC + 2 * FC + m:DC + 2 * FC + m + 1]).then_inc(a_drained, 1)
            std()
            copy_units([xnT[:, c, :] for c in range(DC)])
            act.wait_ge(se_args, 1)
            act.activation(sig3[:], lr[:, 9, 0:3 * NT].rearrange("p (j s) -> p j s", s=3), ACT.Sigmoid).then_inc(se_ready, 1)
            copy_units([seT[:]])
            for u in range(4):
                if u == 3:
                    act.wait_ge(split_stored[0], 32)
                copy_units([split_place(3 + u)[0]])
            value_units()
            act.wait_ge(split_stored[0], 16 * 3)
            act.wait_ge(split_stored[1], 16 * 2)
            act.wait_ge(split_stored[2], 16 * 2)
            attention(GROUPS[2])
            copy_units([fT[:, c, :] for c in range(DC)])
            for m in range(E + DC):
                src = take()
                if m >= 2:
                    act.wait_ge(d_drained, DU["gsum"] + 2 * (m - 1))
                act.activation(gate[:, m % 2, :], src, ACT.Silu).then_inc(a_drained, 1)
            std()
            copy_units([xnT[:, c, :] for c in range(DC)])
            act.wait_ge(a_drained, A["xnT3"])
            for c in range(DC):
                act.activation(xn_high[:, c, :], xnT[:, c, :], ACT.Copy).then_inc(high3_ready, 1)
            act.wait_ge(w3_in, 16 * N_W3)
            for c in range(DC):
                act.activation(slot(Qs, c), take(), ACT.Identity, bias=su[:, DC + c:DC + c + 1]).then_inc(a_drained, 1)
            for c in range(DC):
                act.activation(slot(Qs, 2 + c), take(), ACT.Sigmoid,
                               bias=su[:, 3 * DC + c:3 * DC + c + 1]).then_inc(a_drained, 1)
            act.wait_ge(y3_ready, DC)

            def cut(m):
                act.wait_ge(d_drained, DU["q3"] + 2 * (m + 1))
                r = f3_rows(m)
                act.activation(slot(hid_high, HIGH_PLACES[m], r), slot(Ks, m, r), ACT.Copy).then_inc(hid_cut, 1)

            for m in range(F3C):
                src = take()
                if m >= 2:
                    act.wait_ge(d_drained, DU["q3"] + 2 * (m - 1))
                r = f3_rows(m)
                act.activation(gate[0:r, m % 2, :], src[0:r, :], ACT.Sigmoid).then_inc(a_drained, 1)
                if m >= 1:
                    cut(m - 1)
            cut(F3C - 1)
            assert n[0] == A["sig3"]

        @block.vector
        def _(dve):
            n = [0]
            steps = [0]

            def take():
                n[0] += 1
                dve.wait_ge(d_filled, n[0])
                return psD[:, (n[0] - 1) % 2, :]

            def link(instr):
                steps[0] += 1
                instr.then_inc(dve_step, 1)
                dve.wait_ge(dve_step, steps[0])

            def at(name):
                assert n[0] == DU[name], (name, n[0], DU[name])

            def norm(layer):
                if layer == 0:
                    dve.wait_ge(x_in, 16 * NT // 2)
                else:
                    dve.wait_ge(d_drained, n[0])
                for j in range(NT):
                    op = dve.bn_stats(stat[:, j, :], x[:, j, :])
                link(op)
                for j in range(NT):
                    op = dve.bn_aggr(mv[:, j, :], stat[:, j, :])
                link(op)
                dve.tensor_scalar(ln[:, 0, :], mv[:, :, 1], EPS_LN, None, ALU.add).then_inc(ln_var, 1)
                dve.wait_ge(ln_std, layer + 1)
                link(dve.reciprocal(ln[:, 2, :], ln[:, 1, :]))
                link(dve.tensor_tensor(ln[:, 3, :], ln[:, 0, :], ln[:, 2, :], ALU.mult))
                link(dve.tensor_tensor(ln[:, 3, :], ln[:, 3, :], ln[:, 1, :], ALU.add))
                link(dve.tensor_scalar(ln[:, 3, :], ln[:, 3, :], 0.5, None, ALU.mult))
                link(dve.reciprocal(ln[:, 4, :], ln[:, 3, :]))
                for j in range(NT):
                    dve.tensor_scalar(xn[:, j, :], x[:, j, :], mv[:, j, 0:1], ln[:, 4, j:j + 1],
                                      ALU.subtract, ALU.mult).then_inc(xn_ready, 1)

            def rope(dst_cos, dst_sin, rows_cos, rows_sin):
                for dst, rows, table in ((dst_cos, rows_cos, cos), (dst_sin, rows_sin, sin)):
                    for half in range(2):
                        c = slice(half * HALF, (half + 1) * HALF)
                        src = take()
                        dve.tensor_tensor(dst[:, c], src[rows, :], table[rows, c], ALU.mult).then_inc(d_drained, 1)

            def first_of(dst, eq, best, width, rank):
                link(dve.tensor_tensor(eq, eq, rank, ALU.mult))
                link(dve.tensor_reduce(best, eq, AX, ALU.max))
                link(dve.tensor_tensor(dst, eq, best.unsqueeze(2).broadcast_to([P, NT, width]), ALU.is_equal))

            def split(u, filled, rows=P):
                dve.wait_ge(a_drained, filled)
                v, b = split_place(u)
                v, b = v[0:rows], b[0:rows]
                link(dve.tensor_copy(b[:, 0], v))
                link(dve.tensor_tensor(v, v, b[:, 0], ALU.subtract))
                link(dve.tensor_copy(b[:, 1], v))
                dve.tensor_tensor(b[:, 2], v, b[:, 1], ALU.subtract).then_inc(split_done, 1)

            def row_maxima(units):
                for j, part, h0, nh, w in units:
                    src = take()[:, 0:nh * w].rearrange("p (h k) -> p h k", h=nh)
                    dve.tensor_reduce(mx[:, j, part, h0:h0 + nh], src, AX, ALU.max).then_inc(d_drained, 1)

            def negated_maxima(heads):
                dve.wait_ge(d_drained, n[0])
                dve.tensor_reduce(mneg[:, 0:heads, :], mx[:, :, :, 0:heads].rearrange("p j s h -> p h j s"),
                                  AX, ALU.max, negate=True).then_inc(max_ready, 1)
                max_n[0] += 1
                dve.wait_ge(max_ready, max_n[0])

            max_n = [0]

            def maxima_rows(dst, rows):
                if max_n[0] > 1:
                    dve.wait_ge(mrow_in, 16 * (max_n[0] - 1))
                src = take()
                dst = dst[0:rows, :]
                dve.tensor_copy(dst.bitcast(F32R) if dst.dtype == F32 and rows > NT else dst,
                                src[0:rows, 0:P]).then_inc(d_drained, 1)

            def outputs(i):
                for b in range(2):
                    src = take().rearrange("p (j h v) -> p j h v", j=4, h=GH)
                    link(dve.reciprocal(rec[:], src[:, :, :, HD]))
                    g = i % NG
                    cols = slice(g * GH * HD, (g + 1) * GH * HD)
                    shared = NG <= i < 2 * NG
                    dst = otmp[:] if shared else xn[:, 4 * b:4 * b + 4, cols].rearrange("p j (h d) -> p j h d", h=GH)
                    dve.tensor_tensor(dst, src[:, :, :, 0:HD], rec[:].unsqueeze(3).broadcast_to([P, 4, GH, HD]),
                                      ALU.mult).then_inc(d_drained, 1)
                    dve.wait_ge(d_drained, n[0])
                    if shared:
                        xs = x[:, 4 * b:4 * b + 4, cols].rearrange("p j (h d) -> p j h d", h=GH)
                        link(dve.tensor_tensor(xs, xs, otmp[:], ALU.add))

            def magnitudes():
                dve.wait_ge(w3_in, 16 * N_W3)
                link(dve.memset(gam[:], 0.0))
                full, last = F3 // P, F3 % P
                for k, w in enumerate((w31, w32, w33[:, 0:full, :])):
                    link(dve.tensor_reduce(gam[:, k:k + 1], w.rearrange("p c n -> p (c n)"), AX, ALU.add,
                                           apply_absolute_value=True))
                dve.tensor_reduce(gam[0:last, 3:4], w33[0:last, full, :], AX, ALU.add,
                                  apply_absolute_value=True).then_inc(gsum_ready, 1)

            def attention(groups):
                def maxima_row(i):
                    negated_maxima(GH)
                    maxima_rows(mrow if is_mla(i) else mrowb, GH * NT)
                if groups[0] > 0:
                    row_maxima(MAX_UNITS)
                maxima_row(groups[0])
                for i in groups:
                    nxt = i + 1 if i + 1 in groups else None
                    for kt in range(NT):
                        if nxt is not None:
                            row_maxima(max_chunk(late(nxt), kt))
                        if kt == 1 and i - 1 in groups:
                            outputs(i - 1)
                        if nxt is not None and kt == MAX_END:
                            maxima_row(nxt)
                if groups[0] > 0:
                    magnitudes()
                outputs(groups[-1])

            def add_down(u, width=2):
                src = take().rearrange("p (j d) -> p j d", j=2)
                xs = x[:, 2 * u:2 * u + 2, :]
                dve.tensor_tensor(xs, xs, src, ALU.add).then_inc(d_drained, 1)

            def gated_up(dst, gate_rows, half, scale=None):
                src = take()
                c = slice(half * HALF, (half + 1) * HALF)
                r = gate_rows.shape[0]
                if scale is None:
                    dve.tensor_tensor(dst[:, c], src[0:r, :], gate_rows[:, c], ALU.mult).then_inc(d_drained, 1)
                else:
                    dve.scalar_tensor_tensor(dst[:, c], src[0:r, :], scale, gate_rows[:, c],
                                             ALU.mult, ALU.mult).then_inc(d_drained, 1)

            def biased_times(dst, other, half, bias):
                src = take()
                c = slice(half * HALF, (half + 1) * HALF)
                dve.scalar_tensor_tensor(dst[:, c], src, bias, other[:, c], ALU.add, ALU.mult).then_inc(d_drained, 1)

            link(dve.memset(mx[:], LOWEST))
            norm(0)
            dve.wait_ge(consts_in, 16 * N_CONSTS)
            for half in range(2):
                c = slice(half * HALF, (half + 1) * HALF)
                src = take()
                link(dve.tensor_tensor(kr[:, c], src[0:RD, :], cos[0:RD, c], ALU.mult))
                dve.tensor_tensor(kr_t[:, c], src[RD:P, :], sin[RD:P, c], ALU.mult).then_inc(d_drained, 1)
            at("kr")

            def low(v, high):
                dve.tensor_tensor(v.bitcast(F32R), v, high, ALU.subtract).then_inc(low_ready, 1)

            for u in range(4):
                dve.wait_ge(a_drained, A["lat"] + u + 1)
                low(slot(Ks, 4 + u), slot(Ks, u))

            def rope_low(p):
                dve.wait_ge(rope_high, p + 1)
                low(slot(Pr, p % 4), slot(Pr, 4 + p % 4))

            def router():
                logits, shifted, e_x = (rt[:, k, :].rearrange("p (j h) -> p j h", h=H) for k in range(3))
                small = rt[:, 3, :].rearrange("p (k j) -> p k j", j=NT)
                dve.tensor_copy(rt[:, 0, :], take()[:, 0:NT * H]).then_inc(d_drained, 1)
                dve.wait_ge(d_drained, n[0])
                link(dve.tensor_reduce(small[:, 0], logits, AX, ALU.max))
                top = small[:, 0].unsqueeze(2).broadcast_to([P, NT, H])
                dve.tensor_tensor(shifted, logits, top, ALU.subtract).then_inc(rt_shift, 1)
                eq = rt[:, 4, :].rearrange("p (j h) -> p j h", h=H)
                link(dve.tensor_tensor(eq, logits, top, ALU.is_equal))
                ind = rt[:, 5, :].rearrange("p (j h) -> p j h", h=H)
                first_of(ind, eq, small[:, 1], H, tie[:].unsqueeze(1).broadcast_to([P, NT, H]))
                dve.wait_ge(rt_exp, 1)
                link(dve.tensor_reduce(small[:, 2], e_x, AX, ALU.add))
                link(dve.reciprocal(small[:, 3], small[:, 2]))
                link(dve.tensor_copy(sel[:, :, 0, :], ind))
                link(dve.tensor_tensor(sel[:, :, 1, :], ind, small[:, 3].unsqueeze(2).broadcast_to([P, NT, H]), ALU.mult))

            def selected(j):
                src = take().rearrange("p (s d) -> p s d", d=HD)
                w = sel[:, j].rearrange("p s h -> p (s h)").unsqueeze(2).broadcast_to([P, 2 * H, HD])
                dve.tensor_tensor(kv_tmp.rearrange("p (s d) -> p s d", d=HD), src, w, ALU.mult).then_inc(d_drained, 1)
                dve.wait_ge(d_drained, n[0])
                link(dve.tensor_reduce(kvs[:, j], kv_tmp.rearrange("p (s h d) -> p s d h", s=2, h=H), AX, ALU.add))

            for item in PRE0:
                if item[0] == "rope":
                    p = item[1]
                    if p >= 4:
                        dve.wait_ge(mla_stored, 16 * (8 + 2 * (p - 3)))
                    rope(slot(Pr, p % 4), slot(Pr, 4 + p % 4), slice(0, P), slice(0, P))
                elif item[0] == "low":
                    rope_low(item[1])
                elif item[0] == "ksel":
                    dve.wait_ge(v_cleared, 3)
                    dve.tensor_copy(Vg[:, :, 0:HD], kvs[:, :, 1, :]).then_inc(ksel_ready, 1)
                elif item[0] == "router":
                    router()
                elif item[0] == "kv":
                    selected(item[1])
                elif item[0] == "max":
                    row_maxima([item[2]])
            attention(GROUPS[0])
            dve.wait_ge(w1_in, 16 * N_W1)
            for u in range(FC // 2):
                src = take().rearrange("p (j d) -> p j d", j=2)
                for k in range(2):
                    m = 2 * u + k
                    op = dve.scalar_tensor_tensor(w_dn[:, m, :], src[:, k, :], su[:, DC + m:DC + m + 1], ws_dp,
                                                  ALU.mult, ALU.mult)
                op.then_inc(d_drained, 1)
            at("wdn")
            for u in range(NT // 2):
                add_down(u)
            at("down0")

            norm(1)
            link(dve.memset(K1[RANK:RANK + 1, :], 1.0))
            dve.memset(V1[:, :, D:D + 1], 1.0).then_inc(ones1_ready, 1)
            for j, part, w in MAX1:
                dve.tensor_reduce(mx[:, j, part, 0:1], take()[:, 0:w], AX, ALU.max).then_inc(d_drained, 1)
            negated_maxima(1)
            maxima_rows(mrow, NT)
            at("mrowL1")
            for m in range(FC):
                dve.wait_ge(a_drained, A["s1"] + m + 1)
                for half in range(2):
                    gated_up(slot(Qs, m), gate[:, m % 2, :], half, su[:, DC + FC + m:DC + FC + m + 1])
            at("up1")
            for j in range(NT):
                src = take()
                link(dve.reciprocal(rec[:, 0, 0:1], src[:, D:D + 1]))
                dve.scalar_tensor_tensor(x[:, j, :], src[:, 0:D], rec[:, 0, 0:1], x[:, j, :],
                                         ALU.mult, ALU.add).then_inc(d_drained, 1)
                dve.wait_ge(d_drained, n[0])
            at("pv1")
            for u in range(NT // 2):
                add_down(u)
            at("down1")

            norm(2)
            NR = E + 1
            r9 = [lr[:, k, :].rearrange("p (j e) -> p j e", e=NR) for k in range(9)]
            sc, eq, ind1, ind2, rest, t1, comb = (r9[k][:, :, 0:E] for k in (0, 1, 2, 3, 4, 5, 6))
            m1, m2, best = (lr[:, 7, k * NT:(k + 1) * NT] for k in range(3))
            rank = tie[:, H - E:H].unsqueeze(1).broadcast_to([P, NT, E])
            args = lr[:, 9, 0:3 * NT].rearrange("p (j s) -> p j s", s=3)

            def spread(v):
                return v.unsqueeze(2).broadcast_to([P, NT, E])

            dve.tensor_copy(lr[:, 0, :], take()[:, 0:NT * NR]).then_inc(d_drained, 1)
            at("rt2")
            dve.wait_ge(d_drained, n[0])
            link(dve.tensor_reduce(m1, sc, AX, ALU.max))
            link(dve.tensor_tensor(eq, sc, spread(m1), ALU.is_equal))
            first_of(ind1, eq, best, E, rank)
            link(dve.tensor_scalar(t1, ind1, -1.0, 1.0, ALU.mult, ALU.add))
            link(dve.tensor_tensor(rest, sc, t1, ALU.mult))
            link(dve.tensor_scalar(t1, ind1, LOWEST, None, ALU.mult))
            link(dve.tensor_tensor(rest, rest, t1, ALU.add))
            link(dve.tensor_reduce(m2, rest, AX, ALU.max))
            link(dve.tensor_tensor(eq, rest, spread(m2), ALU.is_equal))
            first_of(ind2, eq, best, E, rank)
            link(dve.tensor_tensor(args[:, :, 0], m1, m2, ALU.subtract))
            link(dve.tensor_tensor(args[:, :, 1], m2, m1, ALU.subtract))
            dve.tensor_copy(args[:, :, 2], r9[0][:, :, E]).then_inc(se_args, 1)
            dve.wait_ge(se_ready, 1)
            link(dve.tensor_tensor(ind1, ind1, spread(sig3[:, :, 0]), ALU.mult))
            link(dve.tensor_tensor(ind2, ind2, spread(sig3[:, :, 1]), ALU.mult))
            dve.tensor_tensor(comb, ind1, ind2, ALU.add).then_inc(comb_ready, 1)
            for u in range(4):
                if 3 + u >= 6:
                    dve.wait_ge(split_stored[0], 32)
                split(3 + u, A["cT"] + u + 1)
            attention(GROUPS[2])
            src = take()
            dve.tensor_copy(gam[:, 4:8], src[:, 0:4]).then_inc(d_drained, 1)
            at("gsum")
            dve.wait_ge(d_drained, n[0])
            link(dve.tensor_tensor(gam[:, 6:7], gam[:, 6:7], gam[:, 7:8], ALU.add))
            link(dve.tensor_scalar(gam[:, 4:7], gam[:, 4:7], 1.0 / (D * F3), EPS_Q, ALU.mult, ALU.add))
            link(dve.tensor_scalar(gam[:, 8:11], gam[:, 4:7], 0.5, None, ALU.mult))
            link(dve.tensor_scalar(gam[:, 4:7], gam[:, 4:7], -0.5, None, ALU.mult))
            pieces = [(k, *(t[0:(f3_rows(c) if k == 2 else P), c, :] for t in (w, q)))
                      for k, (w, q) in enumerate(((w31, q31), (w32, q32), (w33, q33))) for c in range(w.shape[1])]

            def quantise(k, v, dst):
                r = v.shape[0]
                tmp = q_tmp[0:r, 0:v.shape[1]]
                link(dve.tensor_scalar(tmp, v, gam[0:r, 4 + k:5 + k], None, ALU.is_lt))
                link(dve.scalar_tensor_tensor(dst, v, gam[0:r, 8 + k:9 + k], tmp, ALU.is_gt, ALU.subtract))

            for m in range(E + DC):
                if m < E:
                    dve.wait_ge(gated, m + 1)
                else:
                    dve.wait_ge(a_drained, A["oT2"] + m + 1)
                for half in range(2):
                    gated_up(slot(Qs, m) if m < E else slot(Ks, m - E), gate[:, m % 2, :], half)
                if m < len(pieces):
                    quantise(*pieces[m])
            assert len(pieces) <= E + DC
            dve.tensor_copy(gam[:, 11:12], gam[:, 10:11]).then_inc(quantised, 1)
            at("up2")
            for u in range(NT // 2):
                add_down(u)
                dve.wait_ge(d_drained, n[0])
                src = take().rearrange("p (j d) -> p j d", j=2)
                for k in range(2):
                    j = 2 * u + k
                    op = dve.scalar_tensor_tensor(x[:, j, :], src[:, k, :], sig3[:, j, 2:3], x[:, j, :],
                                                  ALU.mult, ALU.add)
                op.then_inc(d_drained, 1)

            norm(3)
            for c in range(DC):
                dve.wait_ge(a_drained, A["xnT3"] + c + 1)
                for half in range(2):
                    biased_times(slot(Qs, 4 + c), slot(Qs, c), half, su[:, 2 * DC + c:2 * DC + c + 1])
                dve.wait_ge(d_drained, n[0])
                dve.tensor_tensor_scan(slot(Qs, 6 + c), onesf[:, 0:1].broadcast_to([P, T]), slot(Qs, 4 + c), 0.0,
                                       ALU.mult, ALU.add).then_inc(cum_ready, 1)
            at("v3")
            for c in range(DC):
                dve.wait_ge(a_drained, A["k3"] + c + 1)
                for half in range(2):
                    biased_times(slot(Qs, c), slot(Qs, 2 + c), half, su[:, c:c + 1])
            at("q3")
            for m in range(F3C):
                dve.wait_ge(a_drained, A["g3"] + m + 1)
                r = f3_rows(m)
                for half in range(2):
                    gated_up(slot(Ks, m, r), gate[0:r, m % 2, :], half)
            at("up3")
            for u in range(NT // 2):
                add_down(u)
            at("down3")

        @block.tensor
        def _(pe):
            na, nd = [0], [0]

            def a_unit():
                na[0] += 1
                if na[0] > 2:
                    pe.wait_ge(a_drained, na[0] - 2)
                return psA[:, (na[0] - 1) % 2, :]

            def d_unit():
                nd[0] += 1
                if nd[0] > 2:
                    pe.wait_ge(d_drained, nd[0] - 2)
                return psD[:, (nd[0] - 1) % 2, :]

            def at(name_a, name_d):
                assert name_a is None or na[0] == A[name_a], (name_a, na[0])
                assert name_d is None or nd[0] == DU[name_d], (name_d, nd[0])

            def product(dst, terms, start=True, stop=True):
                for k, (lhsT, rhs) in enumerate(terms):
                    op = pe.matmul(dst, lhsT, rhs, start=start and k == 0, stop=stop and k == len(terms) - 1)
                return op

            def features(weights, rhs, chunks=None):
                dst = a_unit()
                for half in range(2):
                    c = slice(half * HALF, (half + 1) * HALF)
                    terms = [(weights(k), rhs(k, c)) for k in (chunks or range(DC))]
                    op = product(dst[0:terms[0][0].shape[1], c], terms)
                op.then_inc(a_filled, 1)

            def features_half(weights, rhs, half, chunks=None):
                dst = d_unit()
                c = slice(half * HALF, (half + 1) * HALF)
                terms = [(weights(k), rhs(k, c)) for k in (chunks or range(DC))]
                product(dst[0:terms[0][0].shape[1], :], terms).then_inc(d_filled, 1)

            def normed(k, c):
                return xnT[:, k, c]

            def cols(w, a, b):
                return lambda k: w[:, k, a:b]

            def transposed(src, ready=None):
                for c in range(DC):
                    dst = a_unit()
                    for j in range(NT):
                        if ready is not None and c == 0:
                            pe.wait_ge(xn_ready, ready + j + 1)
                        op = pe.transpose(dst[:, tile_cols(j)], src[:, j, c * P:(c + 1) * P], identf[:])
                    op.then_inc(a_filled, 1)

            def value_units(lhsT, rhs, chunks):
                for u in range(2):
                    dst = a_unit()
                    for j in range(4):
                        op = product(dst[:, j * D:(j + 1) * D],
                                     [(lhsT(k, tile_cols(4 * u + j)), rhs(k)) for k in chunks])
                    op.then_inc(a_filled, 1)

            def maxima_unit(i, j, h0, nh, w, part):
                dst = d_unit()
                rows = MLA if is_mla(i) else STACK
                for k in range(nh):
                    h = h0 + k
                    q = head_rows(Qs, i, h, rows, j * P, (j + 1) * P)
                    kk = key_rows(i, h, rows, part * HALF, part * HALF + w)
                    if is_mla(i):
                        q, kk = high(q), high(kk)
                    diagonal = part == (j >= NT // 2)
                    op = pe.matmul(dst[:, k * w:(k + 1) * w], q, kk, start=True, stop=not diagonal)
                    if diagonal:
                        op = pe.matmul(dst[:, (k + 1) * w - P:(k + 1) * w], identb[:], maskq[:], start=False, stop=True)
                op.then_inc(d_filled, 1)

            def maxima_transpose(i, heads):
                pe.wait_ge(max_ready, maxima_of(i))
                dst = d_unit()
                pe.transpose(dst[0:heads * NT, 0:P], mneg[:, 0:heads, :].rearrange("p h j -> p (h j)"),
                             identf[:]).then_inc(d_filled, 1)

            def scores_T(dst, base, k, q, kt, half, second=None):
                lo = max(kt * P, half * HALF)
                diagonal = kt * P >= half * HALF
                out_ = dst[:, base + lo - half * HALF:base + HALF]
                if second is not None:
                    pe.matmul(out_, second[0], second[1](lo, (half + 1) * HALF), start=True, stop=False)
                op = pe.matmul(out_, k, q(lo, (half + 1) * HALF), start=second is None, stop=not diagonal)
                if diagonal:
                    op = pe.matmul(out_[:, 0:P], identb[:], maskk[:], start=False, stop=True)
                return op

            def score_units(i, kt):
                rows = MLA_ONE + 1 if is_mla(i) else STACK + 1

                def one(heads):
                    dst = a_unit()
                    for b, h in enumerate(heads):
                        second = (Kr2[:, tile_cols(kt)], lambda lo, hi: Qr2[i % 2][:, h * T + lo:h * T + hi]) if is_mla(i) else None
                        k = key_rows(i, h, rows, kt * P, (kt + 1) * P)
                        q = lambda lo, hi: head_rows(Qs, i, h, rows, lo, hi)
                        if len(heads) == 1:
                            for half in range(2):
                                op = scores_T(dst, half * HALF, k, q, kt, half, second)
                        else:
                            op = scores_T(dst, b * HALF, k, q, kt, 1, second)
                    op.then_inc(a_filled, 1)
                step = 1 if kt < NT // 2 else 2
                return [list(range(h, h + step)) for h in range(0, GH, step)], one

            def values_product(i, kt, scored, halves):
                s = NT * i + kt
                pe.wait_ge(a_drained, scored)
                if kt == 0 and i > 0:
                    pe.wait_ge(o_drained, i)
                for half in halves:
                    if kt * P >= (half + 1) * HALF:
                        continue
                    lo, hi = max(kt * P, half * HALF), (half + 1) * HALF
                    last_kt = hi // P - 1
                    for h in range(GH):
                        e = Pr[:, ((s % 2) * GH + h) * T + lo:((s % 2) * GH + h) * T + hi]
                        op = pe.matmul(psO[h * VW:(h + 1) * VW, lo:hi], values(i, kt, h), e,
                                       start=kt == 0, stop=kt == last_kt, tile_position=(0, h * VW),
                                       skip_group_check=True)
                if 1 in halves:
                    op.then_inc(pv_done, 1)

            def output_transposes(i):
                pe.wait_ge(o_drained, i + 1)
                for b in range(2):
                    dst = d_unit()
                    for j in range(4):
                        op = pe.transpose(dst[:, tile_cols(j)], OT[:, tile_cols(4 * b + j)], identf[:])
                    op.then_inc(d_filled, 1)

            def arrived(i):
                pe.wait_ge(stack_in[i % 4], stacks(i))
                if is_mla(i):
                    pe.wait_ge(kr_in, 16 * N_KR)
                elif i < 2 * NG:
                    pe.wait_ge(kg_in, 16 * N_KG)

            def attention(groups):
                if groups[0] > 0:
                    arrived(groups[0])
                    for j, part, h0, nh, w in MAX_UNITS:
                        maxima_unit(groups[0], j, h0, nh, w, part)
                    maxima_transpose(groups[0], GH)
                behind = None
                for i in groups:
                    nxt = i + 1 if i + 1 in groups else None
                    if is_mla(i):
                        pe.wait_ge(rest_in[i % 2], 16 * REST_DMAS * (i // 2 + 1))
                    pe.wait_ge(mrow_in, 16 * maxima_of(i))
                    for kt in range(NT):
                        heads, one = score_units(i, kt)
                        ahead = []
                        if nxt is not None:
                            ahead = max_chunk(late(nxt), kt)
                        for k, hs in enumerate(heads):
                            one(hs)
                            if behind is not None and k == 1:
                                values_product(*behind, (0,) if len(heads) > 2 else (0, 1))
                            if behind is not None and k == 2:
                                values_product(*behind, (1,))
                            if ahead and k == 0 and kt == (1 if late(nxt) else 0):
                                arrived(nxt)
                            for j, part, h0, nh, w in ahead[k * len(ahead) // len(heads):(k + 1) * len(ahead) // len(heads)]:
                                maxima_unit(nxt, j, h0, nh, w, part)
                        scored = na[0]
                        behind = (i, kt, scored)
                        if kt == 1 and i - 1 in groups:
                            output_transposes(i - 1)
                        if nxt is not None and kt == MAX_END:
                            maxima_transpose(nxt, GH)
                values_product(*behind, (0, 1))
                output_transposes(groups[-1])

            pe.wait_ge(ident_in, 16)
            transposed(xn, ready=0)
            at("xnT0", None)
            pe.wait_ge(a_drained, A["xnT0"])
            pe.wait_ge(w0_in, 16 * N_W0)
            features(cols(w_lat, 0, P), normed)
            pe.wait_ge(rotated, 2)
            features_half(cols(w_kr, 0, P), normed, 0)
            features_half(cols(w_kr, 0, P), normed, 1)
            pe.wait_ge(a_drained, A["lat"])
            ql = lambda k, c: lat[0:LAT, c]
            kvl = lambda k, c: lat[LAT:P, c]
            for m in range(2):
                features(lambda k: w_u[0:LAT, tile_cols(m)], ql, [0])
            for m in range(2):
                features(lambda k: w_u[LAT:P, tile_cols(m)], kvl, [0])
            value_units(kvl, lambda k: w_vu[LAT:P, :], [0])
            at("v0", "kr")
            pe.wait_ge(rotated, 4)
            pe.wait_ge(w0b_in, 16 * N_W0B)
            pe.wait_ge(consts_in, 16 * N_CONSTS)
            for item in PRE0:
                if item[0] == "rope":
                    for w in (w_qr, w_qrot):
                        for half in range(2):
                            pe.matmul(d_unit(), w[0:LAT, tile_cols(item[1])], lat[0:LAT, half * HALF:(half + 1) * HALF],
                                      start=True, stop=True).then_inc(d_filled, 1)
                elif item[0] == "router":
                    dst = d_unit()
                    for j in range(NT):
                        op = product(dst[:, j * H:(j + 1) * H],
                                     [(xnT[:, k, tile_cols(j)], w_g0[:, k, :]) for k in range(DC)])
                    op.then_inc(d_filled, 1)
                elif item[0] == "kv":
                    j = item[1]
                    product(d_unit(), [(xnT[:, k, tile_cols(j)], w_qkv0[:, k, D:3 * D]) for k in range(DC)]).then_inc(d_filled, 1)
                elif item[0] == "gq":
                    features(cols(w_qkv0, item[1] * P, (item[1] + 1) * P), normed)
                elif item[0] == "gk":
                    pe.wait_ge(ksel_ready, 1)
                    dst = a_unit()
                    for j in range(NT):
                        op = pe.transpose(dst[0:HD, tile_cols(j)], kvs[:, j, 0, :], identf[:])
                    op.then_inc(a_filled, 1)
                elif item[0] == "max":
                    if item[2] == MAX_UNITS[0]:
                        arrived(0)
                    j, part, h0, nh, w = item[2]
                    maxima_unit(0, j, h0, nh, w, part)
            maxima_transpose(0, GH)
            at("gk", "mrow0")
            attention(GROUPS[0])
            pe.wait_ge(butterflies, 1)
            for u in range(FC // 2):
                pe.matmul(d_unit(), had[:], fT8[:, 2 * u:2 * u + 2, :].rearrange("p c d -> p (c d)"), start=True, stop=True).then_inc(d_filled, 1)
            transposed(xn)
            pe.wait_ge(a_drained, A["oT0"])

            def down(groups_of_terms, head=None):
                for u in range(NT // 2):
                    dst = d_unit()
                    for k in range(2):
                        j = 2 * u + k
                        op = product(dst[:, k * D:(k + 1) * D], groups_of_terms(tile_cols(j)))
                    op.then_inc(d_filled, 1)

            down(lambda t: [(fT[:, k, t], w_o0[:, k, :]) for k in range(DC)])
            at("oT0", "down0")

            transposed(xn, ready=NT)
            pe.wait_ge(a_drained, A["xnT1"])
            pe.wait_ge(w1b_in, 16 * N_W1B)
            features(cols(w_sa, 0, 2 * RANK), normed)
            value_units(normed, lambda k: w_o1[:, k, :], range(DC))
            pe.wait_ge(a_drained, A["qk1"])
            for j, part, w in MAX1:
                dst = d_unit()
                diagonal = part == (j >= NT // 2)
                op = pe.matmul(dst[:, 0:w], high(Q1[0:RANK, tile_cols(j)]), high(K1[0:RANK, part * HALF:part * HALF + w]),
                               start=True, stop=not diagonal)
                if diagonal:
                    op = pe.matmul(dst[:, w - P:w], identb[:], maskq[:], start=False, stop=True)
                op.then_inc(d_filled, 1)
            pe.wait_ge(had_ready, 1)
            for c in range(DC):
                features(cols(h256, c * P, (c + 1) * P), normed)
            maxima_transpose("L1", 1)
            pe.wait_ge(mrow_in, 16 * maxima_of("L1"))
            pe.wait_ge(ones1_ready, 1)
            for kt in range(NT):
                dst = a_unit()
                for half in range(2):
                    if kt * P < (half + 1) * HALF:
                        op = scores_T(dst, half * HALF, K1[0:RANK + 1, tile_cols(kt)],
                                      lambda lo, hi: Q1[0:RANK + 1, lo:hi], kt, half)
                op.then_inc(a_filled, 1)
            at("s1", "mrowL1")
            hadamard = lambda k, c: fT[:, k, c]
            for m in range(FC):
                features(cols(w_gt, m * P, (m + 1) * P), hadamard)
                for half in range(2):
                    features_half(cols(w_up, m * P, (m + 1) * P), hadamard, half)
            for j in range(NT):
                dst = d_unit()
                product(dst[:, 0:D + 1], [(slot(Pr, kt)[:, tile_cols(j)], V1[:, kt, :]) for kt in range(j + 1)]).then_inc(d_filled, 1)
            pe.wait_ge(d_drained, DU["up1"])
            down(lambda t: [(onesf[0:1, :], bor[0:1, :])] + [(slot(Qs, m)[:, t], w_dn[:, m, :]) for m in range(FC)])
            at("gate1", "down1")

            transposed(xn, ready=2 * NT)
            pe.wait_ge(a_drained, A["xnT2"])
            pe.wait_ge(w2_in, 16 * N_W2)
            dst = d_unit()
            for j in range(NT):
                op = product(dst[:, j * (E + 1):(j + 1) * (E + 1)],
                             [(xnT[:, k, tile_cols(j)], w_rt2[:, k, :]) for k in range(DC)])
            op.then_inc(d_filled, 1)
            pe.wait_ge(comb_ready, 1)
            dst = a_unit()
            comb = lr[:, 6, :].rearrange("p (j e) -> p j e", e=E + 1)
            for j in range(NT):
                op = pe.transpose(dst[0:E, tile_cols(j)], comb[:, j, 0:E], identf[:])
            op.then_inc(a_filled, 1)
            for m in (0, 2, 1, 3):
                features(cols(w_qkv2, m * P, (m + 1) * P), normed)
            value_units(normed, lambda k: w_qkv2[:, k, 2 * D:3 * D], range(DC))
            at("v2", "rt2")
            attention(GROUPS[2])
            pe.wait_ge(gsum_ready, 1)
            pe.matmul(d_unit()[:, 0:4], onesf[:], gam[:, 0:4], start=True, stop=True).then_inc(d_filled, 1)
            pe.wait_ge(d_drained, DU[f"o{LAST}"])
            transposed(xn)
            for m in range(E + DC):
                if m == E:
                    pe.wait_ge(moe_in, 16 * N_MOE)
                a, b = tile_cols(m % E).start, tile_cols(m % E).stop
                features(cols(w_eg if m < E else w_sg, a, b), normed)
                for half in range(2):
                    features_half(cols(w_eu if m < E else w_su, a, b), normed, half)
            pe.wait_ge(moe_in, 16 * N_MOE)
            pe.wait_ge(a_drained, A["oT2"])
            pe.wait_ge(d_drained, DU["up2"])
            for u in range(NT // 2):
                for terms in (
                        lambda t: [(fT[:, k, t], w_o2[:, k, :]) for k in range(DC)]
                        + [(slot(Qs, e)[:, t], w_ed[:, e, :]) for e in range(E)],
                        lambda t: [(slot(Ks, m)[:, t], w_sd[:, m, :]) for m in range(DC)]):
                    dst = d_unit()
                    for k in range(2):
                        op = product(dst[:, k * D:(k + 1) * D], terms(tile_cols(2 * u + k)))
                    op.then_inc(d_filled, 1)

            transposed(xn, ready=3 * NT)
            pe.wait_ge(a_drained, A["xnT3"])
            pe.wait_ge(w3_in, 16 * N_W3)
            pe.wait_ge(w3m_in, 16 * N_W3M)
            w3 = lambda n, c: (lambda k: w3m[:, n * DC + k, c * P:(c + 1) * P])
            for c in range(DC):
                features(w3(1, c), normed)
                for half in range(2):
                    features_half(w3(2, c), normed, half)
            for c in range(DC):
                features(w3(3, c), normed)
                for half in range(2):
                    features_half(w3(0, c), normed, half)
            pe.wait_ge(quantised, 1)
            pe.wait_ge(low3_ready, DC)
            cut = lambda k, c: (xn_high, xn_low)[k // DC][:, k % DC, c]
            twice = lambda w, a, b: (lambda k: w[:, k % DC, a:b])
            for m in range(F3C):
                a, b = m * P, m * P + f3_rows(m)
                features(twice(q31, a, b), cut, range(2 * DC))
                for half in range(2):
                    features_half(twice(q32, a, b), cut, half, range(2 * DC))
            pe.wait_ge(hid_split, F3C)
            pe.wait_ge(y3_ready, DC)
            for u in range(NT // 2):
                dst = d_unit()
                for k in range(2):
                    t = tile_cols(2 * u + k)
                    product(dst[:, k * D:(k + 1) * D],
                            [(slot(*h, f3_rows(m))[:, t], q33[0:f3_rows(m), m, :]) for m in range(F3C)
                             for h in ((hid_high, HIGH_PLACES[m]), (hid_low, m))], stop=False)
                    for c in range(DC):
                        op = pe.matmul(dst[:, k * D + c * P:k * D + (c + 1) * P], slot(Qs, 4 + c)[:, t], identf[:],
                                       start=False, stop=c == DC - 1)
                op.then_inc(d_filled, 1)
            at("sig3", "down3")


def constants():
    def bf16(v):
        return (np.ascontiguousarray(v, np.float32).view(np.uint32) >> 16).astype(np.uint16)

    freqs = 1.0 / 10000.0 ** (np.arange(0, RD, 2, dtype=np.float32) / RD)
    ang = np.outer(np.arange(T, dtype=np.float32), freqs)
    table = lambda f: np.ascontiguousarray(np.tile(f(ang), (1, 4)).T.astype(np.float32))
    k = np.arange(D)
    parity = np.array([bin(v).count("1") & 1 for v in range(D)])
    hadamard = (1.0 - 2.0 * parity[k[:, None] & k[None, :]]).astype(np.float32)
    later = np.triu(np.ones((P, P), np.float32), 1) * np.float32(-1e30)
    return {
        "c_ident": np.eye(P, dtype=np.float32), "c_identb": bf16(np.eye(P)),
        "c_had": hadamard[:P, :P] / np.float32(np.sqrt(INTER)),
        "c_h256": hadamard / np.float32(np.sqrt(D)),
        "c_maskq": bf16(later), "c_maskk": bf16(later.T),
        "c_tie": np.tile(np.arange(H, 0, -1, dtype=np.float32), (P, 1)),
        "c_cos": table(np.cos), "c_sin": table(np.sin),
        "c_ones": np.ones((1, T), np.float32), "c_ones4b": bf16(np.ones((1, GH * T))),
    }


def kernel(**inputs):
    import concourse.bacc as bacc
    from concourse.bass_utils import run_bass_kernel_spmd

    a = {k: np.asarray(v) for k, v in inputs.items()}
    col = lambda v: v.reshape(-1, P).T
    flat = lambda v: v.reshape(-1, v.shape[-1])
    arrays = {
        "x": a["L0_attn_x"].reshape(T, D),
        "w_lat": np.concatenate([a["L0_attn_Wqd"], a["L0_attn_Wkvd"]], 1),
        "Wkr": a["L0_attn_Wkr"], "Wqr": a["L0_attn_Wqr"], "Wqu": a["L0_attn_Wqu"], "Wku": a["L0_attn_Wku"],
        "Wvu": a["L0_attn_Wvu"], "Wo0": a["L0_attn_Wo"], "Wg0T": a["L0_ffn_W_gate"].T,
        "Wqkv0T": a["L0_ffn_W_qkv"].T,
        "W_upT": a["L1_ffn_W_up"].T, "W_gateT": a["L1_ffn_W_gate"].T, "W_downT": a["L1_ffn_W_down"].T,
        "Wo1T": a["L1_attn_Wo"].T, "Wsa": np.concatenate([a["L1_attn_Ws"], a["L1_attn_Wa"]], 1),
        "ws_dp": a["L1_ffn_Wscale_dp"].reshape(1, D), "bo": a["L1_attn_bo"].reshape(1, D),
        "su": np.concatenate([col(a["L1_ffn_SU_ug"]), col(a["L1_ffn_SU_dp"]), col(a["L1_ffn_Wscale_ug"])], 1),
        "Wqkv2T": a["L2_attn_w_qkv"].T, "Wo2T": a["L2_attn_w_out"].T,
        "Wrt2T": np.concatenate([a["L2_ffn_gate_w"], a["L2_ffn_se_gate_w"]], 0).T,
        "WegT": flat(a["L2_ffn_w_gate"]).T, "WeuT": flat(a["L2_ffn_w_up"]).T,
        "WsgT": a["L2_ffn_sh_gate"].T, "WsuT": a["L2_ffn_sh_up"].T, "WsdT": a["L2_ffn_sh_down"].T,
        "WedT": flat(a["L2_ffn_w_down"].transpose(0, 2, 1)),
        "Wq3T": a["L3_attn_Wq"].T, "Wk3T": a["L3_attn_Wk"].T, "Wv3T": a["L3_attn_Wv"].T, "Wg3T": a["L3_attn_Wg"].T,
        "b3": np.concatenate([col(a[f"L3_attn_b{n}"]) for n in "qkvg"], 1),
        "w31T": a["L3_ffn_w1"].T, "w32T": a["L3_ffn_w2"].T, "w33T": a["L3_ffn_w3"].T,
        **constants(),
    }
    arrays = {k: np.ascontiguousarray(v) for k, v in arrays.items()}
    nc = bacc.Bacc("TRN2", target_bir_lowering=False, num_devices=1)
    ins = {k: nc.dram_tensor(f"in_{k}", v.shape, mybir.dt.from_np(v.dtype), kind="ExternalInput").ap() for k, v in arrays.items()}
    out = nc.dram_tensor("out", (T, D), F32, kind="ExternalOutput").ap()
    build(nc, ins, out)
    r = run_bass_kernel_spmd(nc, [{f"in_{k}": v for k, v in arrays.items()}], core_ids=[0])
    return np.asarray(r.results[0]["out"]).reshape(1, T, D)
```

```python
from contextlib import ExitStack

import numpy as np
import concourse.bass as bass
from concourse import mybir

F32, F32R, BF16 = mybir.dt.float32, mybir.dt.float32r, mybir.dt.bfloat16
ALU = mybir.AluOpType
ACT = mybir.ActivationFunctionType
AX = mybir.AxisListType.X

P = 128
T, D = 1024, 256
NT, DC = T // P, D // P
HALF = 512
H, HD, RD, LAT = 16, 16, 64, 64
GH = 4
NG = H // GH
HV, VW = HD + 1, 32
RANK = 32
INTER, E, F3 = 1024, 8, 704
FC = INTER // P
F3C = (F3 + P - 1) // P
EPS_LN, EPS_Q = 1e-5, 1e-8
LOWEST = -3.0e38
Q_PARTS = (0, 0, 0, 1, 1, 2)
K_PARTS = (0, 1, 2, 0, 1, 0)
STACK = len(Q_PARTS) * HD
MLA = RD + HD
MLA_ONE = RD + 3 * HD


def f3_rows(m):
    return min(P, F3 - m * P)


def max_units():
    for j in range(NT):
        for part in range(1 + (j >= NT // 2)):
            w = min(HALF, (j + 1) * P) if part == 0 else (j + 1) * P - HALF
            nh = {P: 4, 2 * P: 2}.get(w, 1)
            for h0 in range(0, GH, nh):
                yield j, part, h0, nh, w


MAX_UNITS = list(max_units())
MAX_END = 5


def max_window(i, first, early):
    if early:
        return [(i - 1, kt) for kt in range(1, MAX_END)]
    return [(i - 2, kt) for kt in range(MAX_END, NT) if i - 2 >= first] + [(i - 1, kt) for kt in range(MAX_END)]


def beside(groups, i, kt):
    for g in (i + 1, i + 2):
        if g not in groups:
            continue
        window = max_window(g, groups[0], g <= NG)
        if (i, kt) in window:
            total = sum(NT - n for _, n in window)
            at = sum(NT - n for _, n in window[:window.index((i, kt))])
            return g, MAX_UNITS[at * len(MAX_UNITS) // total:(at + NT - kt) * len(MAX_UNITS) // total]
    return None, []


def numbered(names):
    through, n = {}, 0
    for name, count in names:
        n += count
        through[name] = n
    return through


def build(nc, ins, out):
    with ExitStack() as ctx:
        offset = {}

        def sb(name, shape, dt=F32):
            t = ctx.enter_context(nc.sbuf_tensor(name, shape, dt))
            offset[name] = nc.sbuf_base - int(np.prod(shape[1:])) * (2 if dt == BF16 else 4)
            return t

        def over(base, name, shape, at=0):
            return nc.alloc_sbuf_tensor_at(name, shape, F32R, offset=offset[base] + 4 * at)

        def sem(name):
            return ctx.enter_context(nc.semaphore(name))

        def dram(name, shape, dt):
            return nc.dram_tensor(name, shape, dt, kind="Internal").ap()

        x = sb("x", [P, NT, D])
        xn = sb("xn", [P, NT, D])
        xnT = sb("xnT", [P, DC, T])
        fT = sb("fT", [P, DC, T])
        gate = sb("gate", [P, 2, T])
        Qs = sb("Qs", [P, 8 * T])
        Ks = sb("Ks", [P, 8 * T])
        Kg = sb("Kg", [P, T], BF16)
        Vh = sb("Vh", [P, NT, H * HV + VW - HV])
        Vg = sb("Vg", [P, NT, VW])
        Pr = sb("Pr", [P, 8 * T])
        OT = sb("OT", [P, T])
        WA = sb("WA", [P, 7186])
        WB = sb("WB", [P, 4352])
        identf = sb("identf", [P, P])
        had = sb("had", [P, P])
        onesf = sb("onesf", [P, P])
        identb = sb("identb", [P, P], BF16)
        maskq = sb("maskq", [P, P], BF16)
        maskk = sb("maskk", [P, P], BF16)
        tie = sb("tie", [P, H])
        stat = sb("stat", [P, NT, 6])
        mv = sb("mv", [P, NT, 2])
        ln = sb("ln", [P, 5, NT])
        mx = sb("mx", [P, NT, 2, GH])
        mneg = sb("mneg", [P, GH, NT])
        mrow = sb("mrow", [GH * NT, P])
        mrowb = sb("mrowb", [GH * NT, P], BF16)
        rec = sb("rec", [P, 4, GH])
        otmp = sb("otmp", [P, 4, GH, HD])
        rt = sb("rt", [P, 6, NT * H])
        sel = sb("sel", [P, NT, 2, H])
        kvs = sb("kvs", [P, NT, 2, HD])
        su = sb("su", [P, DC + 3 * FC])
        sig3 = sb("sig3", [P, NT, 3])
        gam = sb("gam", [P, 12])

        Qr, Kr = over("Qs", "Qr", [P, 8 * T]), over("Ks", "Kr", [P, 8 * T])
        Qr2 = [over("WB", "Qr2a", [P, GH * T]), over("fT", "Qr2b", [P, GH * T])]
        Kr2 = over("WA", "Kr2", [P, T], 2 * DC * P + 2 * H * RD + 2 * D + DC * D + DC * H + DC * 3 * D)

        lat_parts = over("Qs", "lat_parts", [P, T], 7 * T)
        wq_high, wq_low = over("fT", "wq_high", [P, 2 * T]), over("WA", "wq_low", [P, 2 * T], 2 * DC * P)

        Q1, K1 = over("OT", "Q1", [P, T]), over("Ks", "K1", [P, T])

        up_high, up_low = over("Vh", "up_high", [P, DC, INTER]), over("WB", "up_low", [P, DC, INTER])
        gt_high, gt_low = over("xn", "gt_high", [P, DC, INTER]), over("Ks", "gt_low", [P, DC, INTER], 4 * T)
        xh_high, xh_low = over("xnT", "xh_high", [P, DC, T]), over("fT", "xh_low", [P, DC, T])

        hid1_high, hid1_low = over("Pr", "hid1_high", [P, FC, T]), over("Qs", "hid1_low", [P, FC, T])
        dn_high, dn_low = over("Ks", "dn_high", [P, FC, D], T), over("WB", "dn_low", [P, FC, D], DC * INTER)

        x2_high, x2_low = over("Ks", "x2_high", [P, DC, T], 5 * T), over("xnT", "x2_low", [P, DC, T])
        pieces_k, pieces_x = over("Ks", "pieces_k", [P, 6, 2, DC, P], 2 * T), over("xn", "pieces_x", [P, 4, 2, DC, P])
        hid2_high, hid2_low = over("Pr", "hid2_high", [P, E, T]), over("Qs", "hid2_low", [P, E, T])
        ed_high = [over("Ks", f"ed_high{n}", [P, E // 2, D], (4, 7)[n] * T) for n in range(2)]
        ed_low = over("Ks", "ed_low", [P, E, D], 2 * T)
        egu_low = over("WA", "egu_low", [P, 2, DC, E * P], 2 * T)
        sg_low, su_low = over("WA", "sg_low", [P, DC, D], 6 * T), over("OT", "su_low", [P, DC, D])

        w3m_high, w3m_low = over("Ks", "w3m_high", [P, 4 * DC, D], 5 * T), over("Vh", "w3m_low", [P, 4 * DC, D])
        W3q = over("WB", "W3q", [P, WB.shape[1]])
        xn_high, xn_low = over("Pr", "xn_high", [P, DC, T]), over("Pr", "xn_low", [P, DC, T], 2 * T)
        hid_high, hid_low = over("Qs", "hid_high", [P, 8 * T]), over("Ks", "hid_low", [P, 8 * T])
        HIGH_PLACES = (0, 1, 2, 3, 6, 7)

        psA = ctx.enter_context(nc.psum_tensor("psA", [P, 2, 2 * HALF], F32))
        psD = ctx.enter_context(nc.psum_tensor("psD", [P, 2, HALF], F32))
        psO = ctx.enter_context(nc.psum_tensor("psO", [P, 2 * HALF], F32))

        lr = rt[:].rearrange("p k n -> p (k n)")[:, 0:10 * NT * (E + 1)].rearrange("p (k n) -> p k n", k=10)
        seT = OT[0:E, :]

        def carve(t):
            at = [0]

            def part(*dims):
                n = int(np.prod(dims))
                v = t[:, at[0]:at[0] + n]
                at[0] += n
                return v.rearrange("p (a b) -> p a b", a=dims[0]) if len(dims) == 2 else v
            return part

        part = carve(WA)
        w_lat, w_kr = part(DC, P), part(DC, 2 * RD)
        w_qr, w_qrot = part(H * RD), part(H * RD)
        w_u, w_vu = part(D), part(D)
        w_o0, w_g0, w_qkv0 = part(DC, D), part(DC, H), part(DC, 3 * D)
        w_qkv0_at = 2 * DC * P + 2 * H * RD + 2 * D + DC * D + DC * H
        part = carve(WA)
        w_qkv2, w_o2 = part(DC, 3 * D), part(DC, D)
        w_eg, w_eu, w_sg, w_sd = part(DC, E * P), part(DC, E * P), part(DC, D), part(DC, D)
        w_rt2 = part(DC, E + 1)
        w_egu = WA[:, 2 * T:6 * T].rearrange("p (g c n) -> p g c n", g=2, c=DC)
        w_ed = Ks[:, 2 * T:4 * T].rearrange("p (e d) -> p e d", e=E)
        w_su = OT[:, 0:DC * D].rearrange("p (c d) -> p c d", c=DC)
        part = carve(WB)
        w_up, w_dn, ws_dp = part(DC, INTER), part(FC, D), part(D)
        part = carve(Ks[:, 4 * T:])
        w_gt, h256, w_o1, w_sa = part(DC, INTER), part(DC, D), part(DC, D), part(DC, 2 * RANK)
        bo1 = part(D)
        part = carve(WB)
        w31, w32, w33 = part(DC, F3), part(DC, F3), part(F3C, D)
        part = carve(W3q)
        q31, q32, q33 = part(DC, F3), part(DC, F3), part(F3C, D)
        w3m = Vh[:].rearrange("p j v -> p (j v)")[:, 0:4 * DC * D].rearrange("p (c d) -> p c d", d=D)
        q_tmp = Kg
        cos, sin = gate[:, 0, :], gate[:, 1, :]
        lat = OT
        kr, kr_t = (xn[:].rearrange("p j d -> p (j d)")[0:RD, n * T:(n + 1) * T] for n in range(2))
        kv_tmp = WA[:, 6400:6400 + 2 * D]
        qk1 = gate[0:2 * RANK, 0, :]
        V1 = Ks[:, T:T + NT * (D + 1)].rearrange("p (j d) -> p j d", j=NT)
        fT8 = fT[:].rearrange("p c (e d) -> p (c e) d", d=D)

        def Vh_heads(j):
            return Vh[:, j, 0:H * HV].rearrange("p (h v) -> p h v", v=HV)

        def slot(t, n, rows=P, base=0):
            return t[base:base + rows, n * T:(n + 1) * T]

        def split_place(u):
            if u < 3:
                b = (0, w_qkv0_at, 3 * HALF)[u]
                return ((xnT[:, 0, :], xnT[:, 1, :], OT[:])[u],
                        WA[:, b:b + 3 * HALF].bitcast(BF16).rearrange("p (s t) -> p s t", s=3))
            b = 2560 * (u % 3)
            return (Pr[:, b:b + T],
                    Pr[:, b + T:b + 2560].bitcast(BF16).rearrange("p (s t) -> p s t", s=3))

        def tile_cols(j):
            return slice(j * P, (j + 1) * P)

        def piece(m):
            return pieces_k[:, m] if m < 6 else pieces_x[:, m - 6]

        def piece_sources(m):
            c = tile_cols(m % E)
            if m < E:
                return [(w_egu[:, :, :, c], egu_low[:, :, :, c], piece(m))]
            return [(w_sg[:, :, c], sg_low[:, :, c], piece(m)[:, 0]), (w_su[:, :, c], su_low[:, :, c], piece(m)[:, 1])]

        d_qr = dram("d_qr", (2, H * RD, T), F32)
        d_qn = dram("d_qn", (2, D, T), F32)
        d_kn = dram("d_kn", (2, D, T), F32)
        d_gq = dram("d_gq", (3, D, T), BF16)
        d_gk = dram("d_gk", (3, HD, T), BF16)
        d_q2 = dram("d_q2", (3, D, T), BF16)
        d_k2 = dram("d_k2", (3, D, T), BF16)
        d_cb = dram("d_cb", (E, T), F32)

        GROUPS = {0: list(range(0, 2 * NG)), 2: list(range(2 * NG, 3 * NG))}
        LAST = 3 * NG - 1

        def is_mla(i):
            return i < NG

        def scored(i, kt):
            return A[f"att{i}"] - A_GROUP + GH * min(kt + 1, NT // 2) + GH // 2 * max(0, kt + 1 - NT // 2)

        def head_rows(t, i, h, rows, a, b):
            if is_mla(i):
                o = ((i % 2) * GH + h) * T
                return (Qr if t is Qs else Kr)[0:rows, o + a:o + b]
            o = ((i % 4) * GH + h) * T
            return t[:].bitcast(BF16)[0:rows, o + a:o + b]

        def key_rows(i, h, rows, a, b):
            return Kg[0:rows, a:b] if NG <= i < 2 * NG else head_rows(Ks, i, h, rows, a, b)

        def high(ap):
            return ap.bitcast(BF16).rearrange("p (t w) -> p t w", w=2)[:, :, 1]

        def values(i, kt, h):
            return Vg[:, kt, :] if NG <= i < 2 * NG else Vh[:, kt, (h + GH * (i % NG)) * HV:(h + GH * (i % NG)) * HV + VW]

        def score_scale(i):
            return float(1.0 / np.sqrt(np.float32(HD + RD))) if is_mla(i) else HD ** -0.5

        def maxima(i):
            return i + 1 if i < 2 * NG else (2 * NG + 1 if i == "L1" else i + 2)

        def maxima_of(i):
            return 2 * NG + 1 if i == "L1" else maxima(i)

        A_GROUP = 4 * GH + 4 * GH // 2
        A = numbered(
            [("xnT0", DC), ("lat", 1), ("qn", 2), ("kn", 2), ("v0", 2), ("gq", 2), ("gk", 1)]
            + [(f"att{i}", A_GROUP) for i in GROUPS[0][:-1]] + [("oT0", DC), (f"att{2 * NG - 1}", A_GROUP)]
            + [("xnT1", DC), ("qk1", 1), ("v1", 2), ("xh", DC), ("s1", NT), ("gate1", FC)]
            + [("xnT2", DC), ("qk2", 4), ("v2", 2), ("cT", 1)]
            + [(f"att{i}", A_GROUP) for i in GROUPS[2]] + [("oT2", DC), ("gate2", E + DC)]
            + [("xnT3", DC), ("k3", DC), ("g3", DC), ("sig3", F3C)])
        NMAX = len(MAX_UNITS)

        DOWN0_AT = range(NT // 2, NT)

        def d_attention(groups):
            names = [(f"max{groups[0]}", NMAX), (f"mrow{groups[0]}", 1)]
            for i in groups:
                nxt = i + 1 if i + 1 in groups else None
                if i == 2 * NG - 2:
                    names.append(("wdn", FC // 2))
                for kt in range(NT):
                    if nxt is not None and kt == MAX_END:
                        names.append((f"mrow{nxt}", 1))
                    g, units = beside(groups, i, kt)
                    names.append((f"max{g} at {i}.{kt}", len(units)))
                    if kt == 1 and i - 1 in groups:
                        names.append((f"o{i - 1}", 2))
                    if i == 2 * NG - 1 and kt in DOWN0_AT:
                        names.append((f"down0 at {kt}", 1))
            return names + [(f"o{groups[-1]}", 2)]

        MAX1 = [(j, part, min(HALF, (j + 1) * P) if part == 0 else (j + 1) * P - HALF)
                for j in range(NT) for part in range(1 + (j >= NT // 2))]
        first_max = [("max", 0, u) for u in MAX_UNITS]
        PRE0 = [("rope", 0), ("rope", 1), ("rope", 2), ("low", 0), ("low", 1), ("router",), ("rope", 3), ("kv", 0),
                ("rope", 4), ("kv", 1), ("kv", 2), ("rope", 5), ("kv", 3)]
        left = list(first_max)
        for item in (("kv", 4), ("rope", 6), ("rope", 7), ("kv", 5), ("kv", 6), ("kv", 7)):
            PRE0 += [item, left.pop(0), left.pop(0), left.pop(0)]
        among = {1: ("ksel",), 2: ("gq", 0), 6: ("gq", 1), 9: ("gk",)}
        for k in range(len(left)):
            PRE0 += [left[k]] + ([among[k]] if k in among else [])

        DU = numbered(
            [("kr", 2)] + [("".join(map(str, item[:2])), {"rope": 4, "low": 0, "ksel": 0, "gq": 0, "gk": 0}.get(item[0], 1)) for item in PRE0]
            + d_attention(GROUPS[0])[1:]
            + [("maxL1", len(MAX1)), ("mrowL1", 1), ("pv1", NT), ("up1", 2 * FC), ("down1", NT // 2)]
            + [("rt2", 1)] + d_attention(GROUPS[2]) + [("gsum", 1), ("up2", 2 * (E + DC))]
            + [(f"down2.{u}", 2) for u in range(NT // 2)]
            + [("v3", 2 * DC), ("q3", 2 * DC), ("up3", 2 * F3C), ("down3", NT // 2)])

        WIDE = [(0, DU["mrow0"] - 1), (DU[f"o{2 * NG - 1}"], DU[f"max{2 * NG}"]), (DU[f"o{LAST}"], DU["down3"])]

        def d_place(n):
            banks = [psD[:, 0, :], psD[:, 1, :], psO[:, 0:HALF], psO[:, HALF:2 * HALF]]
            for first, last in WIDE:
                if first < n <= last:
                    k = (n - first - 1) % 4
                    return banks[k], n - 4 if n - 4 > first else (first if k < 2 else 0)
                if last < n <= last + 2:
                    return banks[(n - 1) % 2], last
            return banks[(n - 1) % 2], n - 2

        x_in, consts_in, w0_in, w1_in, w2_in, w3_in, moe_in, w1b_in, w3m_in = (
            sem(n) for n in ("x_in", "consts_in", "w0_in", "w1_in", "w2_in", "w3_in", "moe_in", "w1b_in", "w3m_in"))
        a_filled, a_drained, d_filled, d_drained = (
            sem(n) for n in ("a_filled", "a_drained", "d_filled", "d_drained"))
        o_drained = sem("o_drained")
        wq_high_ready, q_parts_ready = sem("wq_high_ready"), sem("q_parts_ready")
        wsu_in = sem("wsu_in")
        ed_split2 = sem("ed_split2")
        ed_cut, ed_split, hid2_cut, hid2_split = (sem(n) for n in ("ed_cut", "ed_split", "hid2_cut", "hid2_split"))
        x2_cut, x2_split, piece_cut, piece_split = (sem(n) for n in ("x2_cut", "x2_split", "piece_cut", "piece_split"))
        dn_cut, dn_split, hid1_cut, hid1_split = (sem(n) for n in ("dn_cut", "dn_split", "hid1_cut", "hid1_split"))
        parts1_ready, xh_split = sem("parts1_ready"), sem("xh_split")
        up_cut, gt_cut, xh_cut, low1_ready = sem("up_cut"), sem("gt_cut"), sem("xh_cut"), sem("low1_ready")
        ident_in, w0b_in = sem("ident_in"), sem("w0b_in")
        dve_step, pool_step = sem("dve_step"), sem("pool_step")
        v_cleared, rotated = sem("v_cleared"), sem("rotated")
        ln_var, ln_std, xn_ready = sem("ln_var"), sem("ln_std"), sem("xn_ready")
        kr_ready, rope_sum, rope_high, low_ready = sem("kr_ready"), sem("rope_sum"), sem("rope_high"), sem("low_ready")
        late_low_ready = sem("late_low_ready")
        mla_stored, kr_in = sem("mla_stored"), sem("kr_in")
        rt_shift, rt_exp, ksel_ready = sem("rt_shift"), sem("rt_exp"), sem("ksel_ready")
        split_done, late_split_done = sem("split_done"), sem("late_split_done")
        split_stored = [sem(f"split_stored{n}") for n in range(3)]
        kg_in = sem("kg_in")
        rest_in = [sem(f"rest_in{n}") for n in range(2)]
        stack_in = [sem(f"stack_in{n}") for n in range(4)]
        max_ready, mrow_in = sem("max_ready"), sem("mrow_in")
        pv_done, masked = sem("pv_done"), sem("masked")
        butterflies, had_ready, ones1_ready = sem("butterflies"), sem("had_ready"), sem("ones1_ready")
        se_args, se_ready, comb_ready, comb_out, comb_in = (
            sem(n) for n in ("se_args", "se_ready", "comb_ready", "comb_out", "comb_in"))
        high3_ready = sem("high3_ready")
        low3_ready, hid_split = sem("low3_ready"), sem("hid_split")
        w3m_cut, w3m_split = sem("w3m_cut"), sem("w3m_split")
        hid_cut = sem("hid_cut")
        gsum_ready, quantised = sem("gsum_ready"), sem("quantised")
        gated, cum_ready, y3_ready, stored = sem("gated"), sem("cum_ready"), sem("y3_ready"), sem("stored")
        STACK_DMAS = {0: 3, 1: len(Q_PARTS), 2: len(Q_PARTS) + len(K_PARTS) + 1}
        REST_DMAS = 6
        N_KR, N_KG, N_MLA = 5, len(K_PARTS) + 1, 8 + H
        N_CONSTS, N_W0, N_W0B, N_W1, N_W1B, N_W2, N_W3, N_W3M, N_MOE = 7, 7, 3, 4, 5, 7, 5, 4, 1

        def stacks(i):
            return 16 * sum(STACK_DMAS[k // NG] for k in range(i % 4, i + 1, 4))

        block = ctx.enter_context(nc.Block())

        @block.sync
        def _(sp):
            def load(dst, src, s):
                sp.dma_start(dst, src).then_inc(s, 16)

            def tiles(name):
                return ins[name].rearrange("(c p) n -> p c n", p=P)

            for j in range(0, NT, 2):
                load(x[:, j:j + 2, :], ins["x"].rearrange("(j p) d -> p j d", p=P)[:, j:j + 2, :], x_in)
            load(identf[:], ins["c_ident"], ident_in)
            load(w_lat, tiles("w_lat"), w0_in)
            load(w_kr[:, :, 0:RD], tiles("Wkr"), w0_in)
            for half in range(2):
                load(w_qr[half * LAT:(half + 1) * LAT, :], ins["Wqr"], w0_in)
            load(w_u[0:LAT, :], ins["Wqu"], w0_in)
            load(w_u[LAT:P, :], ins["Wku"], w0_in)
            load(w_vu[LAT:P, :], ins["Wvu"], w0_in)
            load(cos, ins["c_cos"], consts_in)
            load(sin, ins["c_sin"], consts_in)
            for dst, name in ((tie, "c_tie"), (identb, "c_identb"), (maskq, "c_maskq"), (maskk, "c_maskk"), (had, "c_had")):
                src = ins[name]
                load(dst[:], src if dst.dtype == src.dtype else src.bitcast(BF16), consts_in)
            load(w_g0, tiles("Wg0T"), w0b_in)
            load(w_qkv0, tiles("Wqkv0T"), w0b_in)
            load(w_o0, tiles("Wo0"), w0b_in)

            for u in range(4):
                sp.wait_ge(low_ready, u + 1)
                for part in range(2):
                    load((d_qn, d_kn)[u // 2][part, tile_cols(u % 2), :], slot(Ks, 4 * part + u), mla_stored)
            sp.wait_ge(mla_stored, 16 * 8)
            sp.wait_ge(v_cleared, 3)
            sp.wait_ge(kr_ready, 1)
            def shared_key(first):
                places = Kr[0:RD, first * T:(first + GH) * T].bitcast(F32).rearrange("p (h t) -> p h t", h=GH)
                load(places, kr_t.unsqueeze(1).broadcast_to([RD, GH, T]), kr_in)
            shared_key(0)
            load(Kr[MLA_ONE:MLA_ONE + 1, :].bitcast(F32), onesf[0:8 * T // P, :], kr_in)
            load(Kr2[0:RD, :].bitcast(F32), kr, kr_in)
            load(Kr2[RD:2 * RD, :].bitcast(F32), kr_t, kr_in)

            def load_group(i, rest=(False, True)):
                s, g = stack_in[i % 4], i % NG
                if is_mla(i):
                    o = (i % 2) * GH * T
                    for k, (t, a, n, d) in enumerate((
                            (Qr, 0, RD, d_qr[0]), (Qr, RD, HD, d_qn[0]), (Kr, RD, HD, d_kn[0]),
                            (Qr, RD + HD, HD, d_qn[0]), (Qr, RD + 2 * HD, HD, d_qn[1]),
                            (Kr, RD + HD, HD, d_kn[1]), (Kr, RD + 2 * HD, HD, d_kn[0]),
                            (Qr2[i % 2], 0, RD, d_qr[0]), (Qr2[i % 2], RD, RD, d_qr[1]))):
                        if (k >= STACK_DMAS[0]) not in rest:
                            continue
                        at = 0 if t is Qr2[i % 2] else o
                        load(t[a:a + n, at:at + GH * T].bitcast(F32).rearrange("p (h t) -> p h t", h=GH),
                             d[g * GH * n:(g + 1) * GH * n, :].rearrange("(h d) t -> d h t", d=n),
                             s if k < STACK_DMAS[0] else rest_in[i % 2])
                    return
                o, rows = (i % 4) * GH * T, slice(g * GH * HD, (g + 1) * GH * HD)

                def parts(t, d, order):
                    for r, part in enumerate(order):
                        load(t[:].bitcast(BF16)[r * HD:(r + 1) * HD, o:o + GH * T].rearrange("p (h t) -> p h t", h=GH),
                             d[part, rows, :].rearrange("(h d) t -> d h t", d=HD), s)
                parts(Qs, d_gq if i < 2 * NG else d_q2, Q_PARTS)
                if i >= 2 * NG:
                    parts(Ks, d_k2, K_PARTS)
                    load(Ks[:].bitcast(BF16)[STACK:STACK + 1, o:o + GH * T], ins["c_ones4b"].bitcast(BF16), s)

            def maxima_row(i):
                sp.wait_ge(d_drained, DU[f"mrow{i}"])
                if is_mla(i):
                    o = (i % 2) * GH * T
                    load(Qr[MLA_ONE:MLA_ONE + 1, o:o + GH * T].bitcast(F32), mrow[:], mrow_in)
                else:
                    o = (i % 4) * GH * T
                    load(Qs[:].bitcast(BF16)[STACK:STACK + 1, o:o + GH * T], mrowb[:], mrow_in)

            for p in range(H // 2):
                sp.wait_ge(low_ready, 4 + p + 1) if p < 2 else sp.wait_ge(late_low_ready, p - 1)
                for part in range(2):
                    load(d_qr[part, tile_cols(p), :], slot(Pr, 4 * (1 - part) + p % 4), mla_stored)
                if p == 0:
                    continue
                sp.wait_ge(mla_stored, 16 * (8 + 2 * (p + 1)))
                if p == 1:
                    load_group(0)
                    shared_key(GH)
            load_group(1, rest=(False,))
            maxima_row(0)
            load_group(1, rest=(True,))
            sp.wait_ge(split_done, 1)
            load(d_gk.rearrange("s d t -> d s t"), split_place(2)[1][0:HD], split_stored[2])
            sp.wait_ge(split_stored[2], 16)
            for r, part in enumerate(K_PARTS):
                load(Kg[r * HD:(r + 1) * HD, :], d_gk[part], kg_in)
            load(Kg[STACK:STACK + 1, :], ins["c_ones4b"][:, 0:T].bitcast(BF16), kg_in)
            for i in GROUPS[0]:
                if i + 1 in GROUPS[0]:
                    maxima_row(i + 1)
                if i == 1:
                    for u in range(2):
                        sp.wait_ge(split_done, 1 + u + 1)
                        load(d_gq[:, tile_cols(u), :].rearrange("s d t -> d s t"), split_place(u)[1], split_stored[u])
                if i == 2:
                    sp.wait_ge(split_stored[0], 16)
                    sp.wait_ge(split_stored[1], 16)
                for k in {0: (2,), 1: (3,), 2: (4, 5), 3: (6, 7)}.get(i, ()):
                    sp.wait_ge(a_filled, A[f"att{i}"])
                    load_group(k)
                if i == NG - 2:
                    load(w_up, tiles("W_upT"), w1_in)
                    load(w_dn, tiles("W_downT"), w1_in)
                    load(ws_dp, ins["ws_dp"].broadcast_to([P, D]), w1_in)
                    load(su[:], ins["su"], w1_in)

            sp.wait_ge(a_filled, A[f"att{2 * NG - 1}"])
            load(w_sa, tiles("Wsa"), w1b_in)
            load(w_o1, tiles("Wo1T"), w1b_in)
            load(h256, tiles("c_h256"), w1b_in)
            load(w_gt, tiles("W_gateT"), w1b_in)
            load(bo1, ins["bo"].broadcast_to([P, D]), w1b_in)

            sp.wait_ge(d_drained, DU[f"o{2 * NG - 1}"])
            load(w_qkv2, tiles("Wqkv2T"), w2_in)
            load(w_o2, tiles("Wo2T"), w2_in)
            load(w_rt2, tiles("Wrt2T"), w2_in)
            load(w_eg, tiles("WegT"), w2_in)
            load(w_eu, tiles("WeuT"), w2_in)
            load(w_sg, tiles("WsgT"), w2_in)
            load(w_sd, tiles("WsdT"), w2_in)

            sp.wait_ge(d_drained, DU["mrowL1"])
            load(Q1[3 * RANK:3 * RANK + 1, :].bitcast(F32), mrow[0:NT, :], mrow_in)

            sp.wait_ge(d_drained, DU["down1"])
            load(w31, tiles("w31T"), w3_in)
            load(w32, tiles("w32T"), w3_in)
            full = F3 // P
            load(w33[:, 0:full, :], ins["w33T"][0:full * P, :].rearrange("(c p) n -> p c n", p=P), w3_in)
            load(w33[0:F3 - full * P, full, :], ins["w33T"][full * P:F3, :], w3_in)
            load(su[:, 0:4 * DC], ins["b3"], w3_in)

            for u in range(4):
                n = 3 + u
                if u < 2:
                    sp.wait_ge(split_done, n + 1)
                else:
                    sp.wait_ge(late_split_done, u - 1)
                load((d_q2, d_k2)[u % 2][:, tile_cols(u // 2), :].rearrange("s d t -> d s t"),
                     split_place(n)[1], split_stored[n % 3])
                if u == 1:
                    sp.wait_ge(split_stored[0], 16 * 2)
                    sp.wait_ge(split_stored[1], 16 * 2)
                    load_group(GROUPS[2][0])
                    load_group(GROUPS[2][1])
            sp.wait_ge(split_stored[0], 16 * 3)
            sp.wait_ge(split_stored[2], 16 * 2)
            maxima_row(GROUPS[2][0])
            sp.wait_ge(a_drained, A["cT"])
            load(d_cb, seT[:], comb_out)
            load_group(GROUPS[2][2])
            load_group(GROUPS[2][3])
            for i in GROUPS[2][1:]:
                maxima_row(i)
            sp.wait_ge(pv_done, NT * (LAST + 1))
            for n, name in enumerate(("Wq3T", "Wk3T", "Wv3T", "Wg3T")):
                load(w3m[:, n * DC:(n + 1) * DC, :], tiles(name), w3m_in)
            sp.wait_ge(comb_out, 16)
            for e in range(E):
                load(slot(Pr, e), d_cb[e:e + 1, :].broadcast_to([P, T]), comb_in)
            sp.wait_ge(d_drained, DU[f"o{LAST}"])
            load(w_su, tiles("WsuT"), wsu_in)
            sp.wait_ge(d_filled, DU["gsum"] + 2 * 4)
            load(w_ed, ins["WedT"].rearrange("(e p) n -> p e n", p=P), moe_in)

            for u in range(NT // 2):
                sp.wait_ge(d_drained, DU["down3"] - NT // 2 + u + 1)
                load(out.rearrange("(j p) d -> p j d", p=P)[:, 2 * u:2 * u + 2, :], x[:, 2 * u:2 * u + 2, :], stored)
            sp.wait_ge(stored, 16 * NT // 2)

        @block.gpsimd
        def _(pool):
            steps = [0]

            def link(instr):
                steps[0] += 1
                instr.then_inc(pool_step, 1)
                pool.wait_ge(pool_step, steps[0])

            def clear_values():
                link(pool.memset(Vh[:], 0.0))
                for j in range(NT):
                    op = pool.memset(Vh_heads(j)[:, :, HD:HV], 1.0)
                op.then_inc(v_cleared, 1)

            link(pool.memset(Vg[:], 0.0))
            clear_values()
            pool.memset(Vg[:, :, HD:HD + 1], 1.0).then_inc(v_cleared, 1)
            pool.memset(onesf[:], 1.0).then_inc(v_cleared, 1)

            pool.wait_ge(w0_in, 16 * N_W0)
            h2 = RD // 2
            pool.tensor_scalar(w_kr[:, :, RD:RD + h2], w_kr[:, :, h2:RD], -1.0, None, ALU.mult).then_inc(rotated, 1)
            pool.tensor_copy(w_kr[:, :, RD + h2:2 * RD], w_kr[:, :, 0:h2]).then_inc(rotated, 1)
            src = w_qr.rearrange("p (h d) -> p h d", d=RD)
            dst = w_qrot.rearrange("p (h d) -> p h d", d=RD)
            pool.tensor_scalar(dst[:, :, 0:h2], src[:, :, h2:RD], -1.0, None, ALU.mult).then_inc(rotated, 1)
            pool.tensor_copy(dst[:, :, h2:RD], src[:, :, 0:h2]).then_inc(rotated, 1)

            pool.wait_ge(d_drained, DU["kr"])
            link(pool.tensor_tensor(kr, kr, kr_t, ALU.add))
            link(pool.tensor_copy(kr_t.bitcast(F32R), kr))
            pool.tensor_tensor(kr.bitcast(F32R), kr, kr_t, ALU.subtract).then_inc(kr_ready, 1)

            def rope_low(p):
                pool.wait_ge(rope_high, p + 1)
                v = slot(Pr, p % 4)
                pool.tensor_tensor(v.bitcast(F32R), v, slot(Pr, 4 + p % 4), ALU.subtract).then_inc(late_low_ready, 1)

            for p in range(H // 2):
                pool.wait_ge(d_drained, DU[f"rope{p}"])
                pool.tensor_tensor(slot(Pr, p % 4), slot(Pr, p % 4), slot(Pr, 4 + p % 4), ALU.add).then_inc(rope_sum, 1)
                if p >= 3:
                    rope_low(p - 1)
            rope_low(H // 2 - 1)

            def split_step(u, k, rows=P, done=split_done):
                v, b = split_place(u)
                v, b = v[0:rows], b[0:rows]
                if k == 0:
                    link(pool.tensor_copy(b[:, 0], v))
                elif k == 1:
                    link(pool.tensor_tensor(v, v, b[:, 0], ALU.subtract))
                elif k == 2:
                    link(pool.tensor_copy(b[:, 1], v))
                else:
                    pool.tensor_tensor(b[:, 2], v, b[:, 1], ALU.subtract).then_inc(done, 1)

            def split(u, filled, rows=P, done=split_done):
                pool.wait_ge(a_drained, filled)
                for k in range(4):
                    split_step(u, k, rows, done)

            split(2, A["gk"], HD)

            def mask_exponentials(i, kt):
                s = NT * i + kt
                pool.wait_ge(a_drained, scored(i, kt))
                block_ = Pr[:, (s % 2) * GH * T:(s % 2 + 1) * GH * T].rearrange("p (h t) -> p h t", h=GH)[:, :, tile_cols(kt)]
                pool.affine_select(out=block_, in_=block_, pattern=[[0, GH], [1, P]], compare_op=ALU.is_ge, fill=0.0,
                                   base=0, channel_multiplier=-1).then_inc(masked, 1)

            steps_1 = [(s, q, op) for s in range(3) for q in range(0, FC, 2 << s) for op in (ALU.add, ALU.subtract)]

            def butterfly(s, q, op):
                g = 1 << s
                a, b = (w_dn, fT8) if s % 2 == 0 else (fT8, w_dn)
                lo, hi = slice(q, q + g), slice(q + g, q + 2 * g)
                done = pool.tensor_tensor(b[:, lo if op == ALU.add else hi], a[:, lo], a[:, hi], op)
                if (s, q, op) == steps_1[-1]:
                    done.then_inc(butterflies, 1)
                else:
                    link(done)

            for i in GROUPS[0]:
                for kt in range(NT):
                    mask_exponentials(i, kt)
                    if i == 0:
                        split_step(kt // 4, kt % 4)
                    n = NT * (i - NG) + kt
                    if n == 0:
                        pool.wait_ge(w1_in, 16 * N_W1)
                    if 0 <= n < len(steps_1):
                        butterfly(*steps_1[n])
            pool.wait_ge(w1b_in, 16 * N_W1B)
            link(pool.tensor_scalar(h256[:, 0, :], h256[:, 0, :], su[:, 0:1], None, ALU.mult))
            pool.tensor_scalar(h256[:, 1, :], h256[:, 1, :], su[:, 1:2], None, ALU.mult).then_inc(had_ready, 1)

            for cut, low, w, high_part in ((up_cut, up_low, w_up, up_high), (gt_cut, gt_low, w_gt, gt_high)):
                pool.wait_ge(cut, 1)
                for c in range(DC):
                    pool.tensor_tensor(low[:, c, :], w[:, c, :], high_part[:, c, :], ALU.subtract).then_inc(low1_ready, 1)

            pool.wait_ge(dn_cut, 2)
            pool.tensor_tensor(dn_low[:], w_dn, dn_high[:], ALU.subtract).then_inc(dn_split, 1)

            pool.wait_ge(d_filled, DU["up1"])
            clear_values()

            split(5, A["xnT2"] + 3, done=late_split_done)
            split(6, A["xnT2"] + 4, done=late_split_done)
            for i in GROUPS[2]:
                for kt in range(NT):
                    mask_exponentials(i, kt)
            def piece_low(m):
                pool.wait_ge(piece_cut, m + 1)
                for w, low, high_part in piece_sources(m):
                    op = pool.tensor_tensor(low, w, high_part, ALU.subtract)
                op.then_inc(piece_split, 1)

            piece_low(0)
            piece_low(1)
            pool.wait_ge(comb_in, 16 * E)
            for e in range(E):
                if e > 0:
                    piece_low(e + 1)
                pool.wait_ge(a_drained, A["oT2"] + e + 1)
                pool.tensor_tensor(gate[:, e % 2, :], gate[:, e % 2, :], slot(Pr, e), ALU.mult).then_inc(gated, 1)
            piece_low(E + 1)
            pool.wait_ge(ed_cut, 1)
            pool.tensor_tensor(ed_low[:, 0:E // 2], w_ed[:, 0:E // 2], ed_high[0][:], ALU.subtract).then_inc(ed_split, 1)
            pool.wait_ge(w3m_cut, 1)
            pool.tensor_tensor(w3m_low[:], w3m, w3m_high[:], ALU.subtract).then_inc(w3m_split, 1)

            for c in range(DC):
                pool.wait_ge(cum_ready, c + 1)
                pool.wait_ge(d_drained, DU["v3"] + 2 * (c + 1))
                pool.tensor_tensor(slot(Qs, 4 + c), slot(Qs, c), slot(Qs, 6 + c), ALU.mult).then_inc(y3_ready, 1)

        @block.scalar
        def _(act):
            n = [0]

            def take():
                n[0] += 1
                act.wait_ge(a_filled, n[0])
                return psA[:, (n[0] - 1) % 2, :]

            def copy_units(dsts):
                for dst in dsts:
                    src = take()
                    act.activation(dst, src[0:dst.shape[0], :] if len(dst.shape) == 2 else src, ACT.Copy).then_inc(a_drained, 1)

            def std(pieces=NT // 2):
                for u in range(pieces):
                    norms[0] += 1
                    act.wait_ge(ln_var, norms[0])
                    s = slice(u * NT // pieces, (u + 1) * NT // pieces)
                    act.activation(ln[:, 1, s], ln[:, 0, s], ACT.Sqrt).then_inc(ln_std, 1)

            norms = [0]

            def value_units():
                for u in range(2):
                    src = take().rearrange("p (j h d) -> p j h d", j=4, h=H)
                    for j in range(4):
                        op = act.activation(Vh_heads(4 * u + j)[:, :, 0:HD], src[:, j], ACT.Copy)
                    op.then_inc(a_drained, 1)

            def attention(groups):
                for i in groups:
                    if i == 2 * NG - 1:
                        copy_units([fT[:, c, :] for c in range(DC)])
                    for kt in range(NT):
                        s = NT * i + kt
                        if s >= 2:
                            act.wait_ge(pv_done, s - 1)
                        place = Pr[:, (s % 2) * GH * T:(s % 2 + 1) * GH * T].rearrange("p (h t) -> p h t", h=GH)
                        q0 = kt * P
                        if kt < NT // 2:
                            for h in range(GH):
                                src = take()
                                act.activation(place[:, h, q0:T], src[:, q0:T], ACT.Exp,
                                               scale=score_scale(i)).then_inc(a_drained, 1)
                        else:
                            for h in range(0, GH, 2):
                                src = take().rearrange("p (h t) -> p h t", h=2)
                                act.activation(place[:, h:h + 2, q0:T], src[:, :, q0 - HALF:HALF], ACT.Exp,
                                               scale=score_scale(i)).then_inc(a_drained, 1)
                        if kt == 0 and i > groups[0]:
                            output(i - 1)
                output(groups[-1])

            def output(i):
                act.wait_ge(pv_done, NT * (i + 1))
                if i == 0:
                    act.wait_ge(split_done, 1)
                if f"o{i - 1}" in DU:
                    act.wait_ge(d_drained, DU[f"o{i - 1}"])
                if i == GROUPS[2][0]:
                    act.wait_ge(comb_out, 16)
                act.activation(OT[:], psO[:], ACT.Copy).then_inc(o_drained, 1)

            std(1)
            copy_units([xnT[:, c, :] for c in range(DC)])
            act.wait_ge(rotated, 4)
            act.activation(wq_high[:], WA[:, 2 * DC * P:2 * DC * P + 2 * T], ACT.Copy).then_inc(wq_high_ready, 1)
            src = take()
            act.activation(lat[:], src, ACT.Copy)
            act.activation(lat_parts[0:LAT, :], src[0:LAT, :], ACT.Copy).then_inc(a_drained, 1)
            for u in range(4):
                src = take()
                act.activation(slot(Ks, 4 + u), src, ACT.Copy)
                act.activation(slot(Ks, u).bitcast(F32R), src, ACT.Copy).then_inc(a_drained, 1)
            act.wait_ge(v_cleared, 3)
            value_units()
            for item in PRE0:
                if item[0] == "rope":
                    p = item[1]
                    act.wait_ge(rope_sum, p + 1)
                    act.activation(slot(Pr, 4 + p % 4).bitcast(F32R), slot(Pr, p % 4), ACT.Copy).then_inc(rope_high, 1)
                elif item[0] == "router":
                    act.wait_ge(rt_shift, 1)
                    act.activation(rt[:, 2, :], rt[:, 1, :], ACT.Exp).then_inc(rt_exp, 1)
            act.wait_ge(a_filled, n[0] + 2)
            copy_units([split_place(u)[0] for u in range(2)])
            copy_units([split_place(2)[0][0:HD]])
            act.wait_ge(mla_stored, 16 * N_MLA)
            attention(GROUPS[0])
            act.activation(up_high[:], w_up, ACT.Copy).then_inc(up_cut, 1)
            std(1)
            copy_units([xnT[:, c, :] for c in range(DC)])
            src = take()
            q, k = src[0:RANK, :], src[RANK:2 * RANK, :]
            act.activation(qk1, src[0:2 * RANK, :], ACT.Copy)
            act.activation(Q1[0:RANK, :], q, ACT.Copy)
            act.activation(K1[RANK:2 * RANK, :], k, ACT.Copy)
            act.activation(K1[0:RANK, :], k, ACT.Copy)
            act.activation(Q1[2 * RANK:3 * RANK, :], q, ACT.Copy).then_inc(a_drained, 1)
            for u in range(2):
                src = take().rearrange("p (j d) -> p j d", d=D)
                act.activation(V1[:, 4 * u:4 * u + 4, 0:D], src, ACT.Copy).then_inc(a_drained, 1)
            act.wait_ge(w1b_in, 16 * N_W1B)
            act.activation(gt_high[:], w_gt, ACT.Copy).then_inc(gt_cut, 1)
            copy_units([fT[:, c, :] for c in range(DC)])
            act.wait_ge(a_drained, A["xh"])
            for c in range(DC):
                act.activation(xh_high[:, c, :], fT[:, c, :], ACT.Copy).then_inc(xh_cut, 1)
            for kt in range(NT):
                src = take()
                act.activation(slot(Pr, kt)[:, kt * P:T], src[:, kt * P:T], ACT.Exp,
                               scale=float(1.0 / np.sqrt(RANK))).then_inc(a_drained, 1)

            def cut_hidden(m):
                act.wait_ge(d_drained, DU["pv1"] + 2 * (m + 1))
                act.activation(hid1_high[:, m, :], slot(Qs, m), ACT.Copy).then_inc(hid1_cut, 1)

            for m in range(FC):
                src = take()
                if m >= 2:
                    act.wait_ge(d_drained, DU["pv1"] + 2 * (m - 1))
                act.activation(gate[:, m % 2, :], src, ACT.Silu,
                               scale=su[:, DC + 2 * FC + m:DC + 2 * FC + m + 1]).then_inc(a_drained, 1)
                if m >= 2:
                    cut_hidden(m - 2)
                else:
                    act.wait_ge(d_filled, DU["pv1"])
                    half = slice(m * FC // 2, (m + 1) * FC // 2)
                    act.activation(dn_high[:, half], w_dn[:, half], ACT.Copy).then_inc(dn_cut, 1)
            cut_hidden(FC - 2)
            cut_hidden(FC - 1)
            std()
            copy_units([xnT[:, c, :] for c in range(DC)])
            for u in range(4):
                if u == 3:
                    act.wait_ge(split_stored[0], 32)
                copy_units([split_place(3 + u)[0]])
            act.wait_ge(v_cleared, 4)
            value_units()
            act.wait_ge(se_args, 1)
            act.activation(sig3[:], lr[:, 9, 0:3 * NT].rearrange("p (j s) -> p j s", s=3), ACT.Sigmoid).then_inc(se_ready, 1)
            copy_units([seT[:]])
            act.wait_ge(split_stored[0], 16 * 3)
            act.wait_ge(split_stored[1], 16 * 2)
            act.wait_ge(split_stored[2], 16 * 2)
            attention(GROUPS[2])

            def cut_piece(m):
                if m == E:
                    act.wait_ge(wsu_in, 16)
                for w, _, high_part in piece_sources(m):
                    op = act.activation(high_part, w, ACT.Copy)
                op.then_inc(piece_cut, 1)

            act.wait_ge(a_filled, A[f"att{LAST}"])
            for c in range(DC):
                act.activation(x2_high[:, c, :], xnT[:, c, :], ACT.Copy).then_inc(x2_cut, 1)
            for m in range(3):
                cut_piece(m)
            copy_units([fT[:, c, :] for c in range(DC)])
            for m in range(E + DC):
                src = take()
                if m >= 2:
                    act.wait_ge(d_drained, DU["gsum"] + 2 * (m - 1))
                act.activation(gate[:, m % 2, :], src, ACT.Silu).then_inc(a_drained, 1)
                if m + 3 < E + DC:
                    cut_piece(m + 3)
                if m >= DC:
                    act.activation(hid2_high[:, m - DC, :], slot(Qs, m - DC), ACT.Copy).then_inc(hid2_cut, 1)
                if m == E - 1:
                    act.wait_ge(moe_in, 16 * N_MOE)
                    for half in range(2):
                        act.activation(ed_high[half][:], w_ed[:, half * E // 2:(half + 1) * E // 2],
                                       ACT.Copy).then_inc(ed_cut, 1)
            act.wait_ge(w3m_in, 16 * N_W3M)
            act.wait_ge(d_filled, DU["up2"])
            act.activation(w3m_high[:], w3m, ACT.Copy).then_inc(w3m_cut, 1)
            std()
            srcs = []
            for c in range(DC):
                srcs.append(take())
                act.activation(xn_high[:, c, :], srcs[c], ACT.Copy).then_inc(high3_ready, 1)
            for c in range(DC):
                act.activation(xnT[:, c, :], srcs[c], ACT.Copy).then_inc(a_drained, 1)
            act.wait_ge(w3_in, 16 * N_W3)
            for c in range(DC):
                act.activation(slot(Qs, c), take(), ACT.Identity, bias=su[:, DC + c:DC + c + 1]).then_inc(a_drained, 1)
            for c in range(DC):
                act.activation(slot(Qs, 2 + c), take(), ACT.Sigmoid,
                               bias=su[:, 3 * DC + c:3 * DC + c + 1]).then_inc(a_drained, 1)
            act.wait_ge(y3_ready, DC)

            def cut(m):
                act.wait_ge(d_drained, DU["q3"] + 2 * (m + 1))
                r = f3_rows(m)
                act.activation(slot(hid_high, HIGH_PLACES[m], r), slot(Ks, m, r), ACT.Copy).then_inc(hid_cut, 1)

            for m in range(F3C):
                src = take()
                if m >= 2:
                    act.wait_ge(d_drained, DU["q3"] + 2 * (m - 1))
                r = f3_rows(m)
                act.activation(gate[0:r, m % 2, :], src[0:r, :], ACT.Sigmoid).then_inc(a_drained, 1)
                if m >= 1:
                    cut(m - 1)
            cut(F3C - 1)
            assert n[0] == A["sig3"]

        @block.vector
        def _(dve):
            n = [0]
            steps = [0]

            def take():
                n[0] += 1
                dve.wait_ge(d_filled, n[0])
                return d_place(n[0])[0]

            def link(instr):
                steps[0] += 1
                instr.then_inc(dve_step, 1)
                dve.wait_ge(dve_step, steps[0])

            def at(name):
                assert n[0] == DU[name], (name, n[0], DU[name])

            def stats(tiles=(0, NT)):
                if n[0] == 0:
                    dve.wait_ge(x_in, 16 * NT // 2)
                else:
                    dve.wait_ge(d_drained, n[0])
                for j in range(*tiles):
                    op = dve.bn_stats(stat[:, j, :], x[:, j, :])
                link(op)

            def norm(tiles=(0, NT)):
                js, s = range(*tiles), slice(*tiles)
                for j in js:
                    op = dve.bn_aggr(mv[:, j, :], stat[:, j, :])
                link(op)
                dve.tensor_scalar(ln[:, 0, s], mv[:, s, 1], EPS_LN, None, ALU.add).then_inc(ln_var, 1)
                norms[0] += 1
                dve.wait_ge(ln_std, norms[0])
                link(dve.reciprocal(ln[:, 2, s], ln[:, 1, s]))
                link(dve.tensor_tensor(ln[:, 3, s], ln[:, 0, s], ln[:, 2, s], ALU.mult))
                link(dve.tensor_tensor(ln[:, 3, s], ln[:, 3, s], ln[:, 1, s], ALU.add))
                link(dve.tensor_scalar(ln[:, 3, s], ln[:, 3, s], 0.5, None, ALU.mult))
                link(dve.reciprocal(ln[:, 4, s], ln[:, 3, s]))
                for j in js:
                    dve.tensor_scalar(xn[:, j, :], x[:, j, :], mv[:, j, 0:1], ln[:, 4, j:j + 1],
                                      ALU.subtract, ALU.mult).then_inc(xn_ready, 1)

            norms = [0]

            def rope(dst_cos, dst_sin, rows_cos, rows_sin):
                for dst, rows, table in ((dst_cos, rows_cos, cos), (dst_sin, rows_sin, sin)):
                    for half in range(2):
                        c = slice(half * HALF, (half + 1) * HALF)
                        src = take()
                        dve.tensor_tensor(dst[:, c], src[rows, :], table[rows, c], ALU.mult).then_inc(d_drained, 1)

            def first_of(dst, eq, best, width, rank):
                link(dve.tensor_tensor(eq, eq, rank, ALU.mult))
                link(dve.tensor_reduce(best, eq, AX, ALU.max))
                link(dve.tensor_tensor(dst, eq, best.unsqueeze(2).broadcast_to([P, NT, width]), ALU.is_equal))

            def split(u, filled, rows=P):
                dve.wait_ge(a_drained, filled)
                v, b = split_place(u)
                v, b = v[0:rows], b[0:rows]
                link(dve.tensor_copy(b[:, 0], v))
                link(dve.tensor_tensor(v, v, b[:, 0], ALU.subtract))
                link(dve.tensor_copy(b[:, 1], v))
                dve.tensor_tensor(b[:, 2], v, b[:, 1], ALU.subtract).then_inc(split_done, 1)

            def row_maxima(units):
                for j, part, h0, nh, w in units:
                    src = take()[:, 0:nh * w].rearrange("p (h k) -> p h k", h=nh)
                    dve.tensor_reduce(mx[:, j, part, h0:h0 + nh], src, AX, ALU.max).then_inc(d_drained, 1)

            def negated_maxima(heads):
                dve.wait_ge(d_drained, n[0])
                dve.tensor_reduce(mneg[:, 0:heads, :], mx[:, :, :, 0:heads].rearrange("p j s h -> p h j s"),
                                  AX, ALU.max, negate=True).then_inc(max_ready, 1)
                max_n[0] += 1
                dve.wait_ge(max_ready, max_n[0])

            max_n = [0]

            def maxima_rows(dst, rows):
                if max_n[0] > 1:
                    dve.wait_ge(mrow_in, 16 * (max_n[0] - 1))
                src = take()
                dst = dst[0:rows, :]
                dve.tensor_copy(dst.bitcast(F32R) if dst.dtype == F32 else dst,
                                src[0:rows, 0:P]).then_inc(d_drained, 1)

            def outputs(i):
                for b in range(2):
                    src = take().rearrange("p (j h v) -> p j h v", j=4, h=GH)
                    link(dve.reciprocal(rec[:], src[:, :, :, HD]))
                    g = i % NG
                    cols = slice(g * GH * HD, (g + 1) * GH * HD)
                    shared = NG <= i < 2 * NG
                    dst = otmp[:] if shared else xn[:, 4 * b:4 * b + 4, cols].rearrange("p j (h d) -> p j h d", h=GH)
                    dve.tensor_tensor(dst, src[:, :, :, 0:HD], rec[:].unsqueeze(3).broadcast_to([P, 4, GH, HD]),
                                      ALU.mult).then_inc(d_drained, 1)
                    dve.wait_ge(d_drained, n[0])
                    if shared:
                        xs = x[:, 4 * b:4 * b + 4, cols].rearrange("p j (h d) -> p j h d", h=GH)
                        link(dve.tensor_tensor(xs, xs, otmp[:], ALU.add))
                    if i == 2 * NG - 1:
                        stats((4 * b, 4 * b + 4))

            def down_weights():
                dve.wait_ge(w1_in, 16 * N_W1)
                for u in range(FC // 2):
                    src = take().rearrange("p (j d) -> p j d", j=2)
                    for k in range(2):
                        m = 2 * u + k
                        op = dve.scalar_tensor_tensor(w_dn[:, m, :], src[:, k, :], su[:, DC + m:DC + m + 1], ws_dp,
                                                      ALU.mult, ALU.mult)
                    op.then_inc(d_drained, 1)

            def magnitudes():
                dve.wait_ge(w3_in, 16 * N_W3)
                link(dve.memset(gam[:], 0.0))
                full, last = F3 // P, F3 % P
                for k, w in enumerate((w31, w32, w33[:, 0:full, :])):
                    link(dve.tensor_reduce(gam[:, k:k + 1], w.rearrange("p c n -> p (c n)"), AX, ALU.add,
                                           apply_absolute_value=True))
                dve.tensor_reduce(gam[0:last, 3:4], w33[0:last, full, :], AX, ALU.add,
                                  apply_absolute_value=True).then_inc(gsum_ready, 1)

            def attention(groups):
                def maxima_row(i):
                    negated_maxima(GH)
                    maxima_rows(mrow if is_mla(i) else mrowb, GH * NT)
                if groups[0] > 0:
                    row_maxima(MAX_UNITS)
                maxima_row(groups[0])
                for i in groups:
                    nxt = i + 1 if i + 1 in groups else None
                    if i == 2 * NG - 2:
                        down_weights()
                    for kt in range(NT):
                        if nxt is not None and kt == MAX_END:
                            maxima_row(nxt)
                        row_maxima(beside(groups, i, kt)[1])
                        if kt == 1 and i - 1 in groups:
                            outputs(i - 1)
                        if i == 2 * NG - 1 and kt in DOWN0_AT:
                            add_down(kt - DOWN0_AT[0])
                if groups[0] > 0:
                    magnitudes()
                outputs(groups[-1])

            def add_down(u):
                src = take().rearrange("p (j d) -> p j d", j=2)
                xs = x[:, 2 * u:2 * u + 2, :]
                dve.tensor_tensor(xs, xs, src, ALU.add).then_inc(d_drained, 1)

            def gated_up(dst, gate_rows, half, scale=None):
                src = take()
                c = slice(half * HALF, (half + 1) * HALF)
                r = gate_rows.shape[0]
                if scale is None:
                    dve.tensor_tensor(dst[:, c], src[0:r, :], gate_rows[:, c], ALU.mult).then_inc(d_drained, 1)
                else:
                    dve.scalar_tensor_tensor(dst[:, c], src[0:r, :], scale, gate_rows[:, c],
                                             ALU.mult, ALU.mult).then_inc(d_drained, 1)

            def biased_times(dst, other, half, bias):
                src = take()
                c = slice(half * HALF, (half + 1) * HALF)
                dve.scalar_tensor_tensor(dst[:, c], src, bias, other[:, c], ALU.add, ALU.mult).then_inc(d_drained, 1)

            link(dve.memset(mx[:], LOWEST))
            stats()
            norm()
            dve.wait_ge(wq_high_ready, 1)
            dve.tensor_tensor(wq_low[0:LAT, :], WA[0:LAT, 2 * DC * P:2 * DC * P + 2 * T], wq_high[0:LAT, :],
                              ALU.subtract).then_inc(q_parts_ready, 1)
            dve.wait_ge(a_drained, A["lat"])
            dve.tensor_tensor(lat_parts[LAT:P, :], lat[0:LAT, :], lat_parts[0:LAT, :], ALU.subtract).then_inc(q_parts_ready, 1)
            dve.wait_ge(consts_in, 16 * N_CONSTS)
            for half in range(2):
                c = slice(half * HALF, (half + 1) * HALF)
                src = take()
                link(dve.tensor_tensor(kr[:, c], src[0:RD, :], cos[0:RD, c], ALU.mult))
                dve.tensor_tensor(kr_t[:, c], src[RD:P, :], sin[RD:P, c], ALU.mult).then_inc(d_drained, 1)
            at("kr")

            def low(v, high):
                dve.tensor_tensor(v.bitcast(F32R), v, high, ALU.subtract).then_inc(low_ready, 1)

            for u in range(4):
                dve.wait_ge(a_drained, A["lat"] + u + 1)
                low(slot(Ks, 4 + u), slot(Ks, u))

            def rope_low(p):
                dve.wait_ge(rope_high, p + 1)
                low(slot(Pr, p % 4), slot(Pr, 4 + p % 4))

            def router():
                logits, shifted, e_x = (rt[:, k, :].rearrange("p (j h) -> p j h", h=H) for k in range(3))
                small = rt[:, 3, :].rearrange("p (k j) -> p k j", j=NT)
                dve.tensor_copy(rt[:, 0, :], take()[:, 0:NT * H]).then_inc(d_drained, 1)
                dve.wait_ge(d_drained, n[0])
                link(dve.tensor_reduce(small[:, 0], logits, AX, ALU.max))
                top = small[:, 0].unsqueeze(2).broadcast_to([P, NT, H])
                dve.tensor_tensor(shifted, logits, top, ALU.subtract).then_inc(rt_shift, 1)
                eq = rt[:, 4, :].rearrange("p (j h) -> p j h", h=H)
                link(dve.tensor_tensor(eq, logits, top, ALU.is_equal))
                ind = rt[:, 5, :].rearrange("p (j h) -> p j h", h=H)
                first_of(ind, eq, small[:, 1], H, tie[:].unsqueeze(1).broadcast_to([P, NT, H]))
                dve.wait_ge(rt_exp, 1)
                link(dve.tensor_reduce(small[:, 2], e_x, AX, ALU.add))
                link(dve.reciprocal(small[:, 3], small[:, 2]))
                link(dve.tensor_copy(sel[:, :, 0, :], ind))
                link(dve.tensor_tensor(sel[:, :, 1, :], ind, small[:, 3].unsqueeze(2).broadcast_to([P, NT, H]), ALU.mult))

            def selected(j):
                src = take().rearrange("p (s d) -> p s d", d=HD)
                w = sel[:, j].rearrange("p s h -> p (s h)").unsqueeze(2).broadcast_to([P, 2 * H, HD])
                dve.tensor_tensor(kv_tmp.rearrange("p (s d) -> p s d", d=HD), src, w, ALU.mult).then_inc(d_drained, 1)
                dve.wait_ge(d_drained, n[0])
                link(dve.tensor_reduce(kvs[:, j], kv_tmp.rearrange("p (s h d) -> p s d h", s=2, h=H), AX, ALU.add))

            for item in PRE0:
                if item[0] == "rope":
                    p = item[1]
                    if p >= 4:
                        dve.wait_ge(mla_stored, 16 * (8 + 2 * max(p - 3, 2)))
                    rope(slot(Pr, p % 4), slot(Pr, 4 + p % 4), slice(0, P), slice(0, P))
                elif item[0] == "low" and item[1] < 2:
                    rope_low(item[1])
                elif item[0] == "ksel":
                    dve.wait_ge(v_cleared, 3)
                    dve.tensor_copy(Vg[:, :, 0:HD], kvs[:, :, 1, :]).then_inc(ksel_ready, 1)
                elif item[0] == "router":
                    router()
                elif item[0] == "kv":
                    selected(item[1])
                elif item[0] == "max":
                    row_maxima([item[2]])
            attention(GROUPS[0])
            norm()
            at(f"o{2 * NG - 1}")

            link(dve.memset(K1[3 * RANK:3 * RANK + 1, :].bitcast(F32), 1.0))
            dve.memset(V1[:, :, D:D + 1], 1.0).then_inc(ones1_ready, 1)
            dve.wait_ge(a_drained, A["qk1"])
            dve.tensor_tensor(Q1[RANK:2 * RANK, :], qk1[0:RANK, :], Q1[0:RANK, :], ALU.subtract).then_inc(parts1_ready, 1)
            dve.tensor_tensor(K1[2 * RANK:3 * RANK, :], qk1[RANK:2 * RANK, :], K1[RANK:2 * RANK, :],
                              ALU.subtract).then_inc(parts1_ready, 1)
            for j, part, w in MAX1:
                dve.tensor_reduce(mx[:, j, part, 0:1], take()[:, 0:w], AX, ALU.max).then_inc(d_drained, 1)
            negated_maxima(1)
            maxima_rows(mrow, NT)
            at("mrowL1")
            for c in range(DC):
                dve.wait_ge(xh_cut, c + 1)
                dve.tensor_tensor(xh_low[:, c, :], fT[:, c, :], xh_high[:, c, :], ALU.subtract).then_inc(xh_split, 1)
            dve.wait_ge(w1b_in, 16 * N_W1B)
            for j in range(NT):
                src = take()
                link(dve.reciprocal(rec[:, 0, 0:1], src[:, D:D + 1]))
                dve.scalar_tensor_tensor(x[:, j, :], src[:, 0:D], rec[:, 0, 0:1], x[:, j, :],
                                         ALU.mult, ALU.add).then_inc(d_drained, 1)
                dve.wait_ge(d_drained, n[0])
                link(dve.tensor_tensor(x[:, j, :], x[:, j, :], bo1, ALU.add))
            at("pv1")

            def hidden_low(m):
                dve.wait_ge(hid1_cut, m + 1)
                dve.tensor_tensor(hid1_low[:, m, :], slot(Qs, m), hid1_high[:, m, :], ALU.subtract).then_inc(hid1_split, 1)

            for m in range(FC):
                dve.wait_ge(a_drained, A["s1"] + m + 1)
                for half in range(2):
                    gated_up(slot(Qs, m), gate[:, m % 2, :], half, su[:, DC + FC + m:DC + FC + m + 1])
                if m >= 2:
                    hidden_low(m - 2)
            hidden_low(FC - 2)
            hidden_low(FC - 1)
            at("up1")
            for u in range(NT // 2):
                add_down(u)
                stats((2 * u, 2 * u + 2))
                norm((2 * u, 2 * u + 2))
            at("down1")

            NR = E + 1
            r9 = [lr[:, k, :].rearrange("p (j e) -> p j e", e=NR) for k in range(9)]
            sc, eq, ind1, ind2, rest, t1, comb = (r9[k][:, :, 0:E] for k in (0, 1, 2, 3, 4, 5, 6))
            m1, m2, best = (lr[:, 7, k * NT:(k + 1) * NT] for k in range(3))
            rank = tie[:, H - E:H].unsqueeze(1).broadcast_to([P, NT, E])
            args = lr[:, 9, 0:3 * NT].rearrange("p (j s) -> p j s", s=3)

            def spread(v):
                return v.unsqueeze(2).broadcast_to([P, NT, E])

            for u in range(2):
                split(3 + u, A["xnT2"] + u + 1)
            dve.tensor_copy(lr[:, 0, :], take()[:, 0:NT * NR]).then_inc(d_drained, 1)
            at("rt2")
            dve.wait_ge(d_drained, n[0])
            link(dve.tensor_reduce(m1, sc, AX, ALU.max))
            link(dve.tensor_tensor(eq, sc, spread(m1), ALU.is_equal))
            first_of(ind1, eq, best, E, rank)
            link(dve.tensor_scalar(t1, ind1, -1.0, 1.0, ALU.mult, ALU.add))
            link(dve.tensor_tensor(rest, sc, t1, ALU.mult))
            link(dve.tensor_scalar(t1, ind1, LOWEST, None, ALU.mult))
            link(dve.tensor_tensor(rest, rest, t1, ALU.add))
            link(dve.tensor_reduce(m2, rest, AX, ALU.max))
            link(dve.tensor_tensor(eq, rest, spread(m2), ALU.is_equal))
            first_of(ind2, eq, best, E, rank)
            link(dve.tensor_tensor(args[:, :, 0], m1, m2, ALU.subtract))
            link(dve.tensor_tensor(args[:, :, 1], m2, m1, ALU.subtract))
            dve.tensor_copy(args[:, :, 2], r9[0][:, :, E]).then_inc(se_args, 1)
            dve.wait_ge(se_ready, 1)
            link(dve.tensor_tensor(ind1, ind1, spread(sig3[:, :, 0]), ALU.mult))
            link(dve.tensor_tensor(ind2, ind2, spread(sig3[:, :, 1]), ALU.mult))
            dve.tensor_tensor(comb, ind1, ind2, ALU.add).then_inc(comb_ready, 1)
            attention(GROUPS[2])
            src = take()
            dve.tensor_copy(gam[:, 4:8], src[:, 0:4]).then_inc(d_drained, 1)
            for c in range(DC):
                dve.wait_ge(x2_cut, c + 1)
                dve.tensor_tensor(x2_low[:, c, :], xnT[:, c, :], x2_high[:, c, :], ALU.subtract).then_inc(x2_split, 1)
            at("gsum")
            dve.wait_ge(d_drained, n[0])
            link(dve.tensor_tensor(gam[:, 6:7], gam[:, 6:7], gam[:, 7:8], ALU.add))
            link(dve.tensor_scalar(gam[:, 4:7], gam[:, 4:7], 1.0 / (D * F3), EPS_Q, ALU.mult, ALU.add))
            link(dve.tensor_scalar(gam[:, 8:11], gam[:, 4:7], 0.5, None, ALU.mult))
            link(dve.tensor_scalar(gam[:, 4:7], gam[:, 4:7], -0.5, None, ALU.mult))
            pieces = [(k, *(t[0:(f3_rows(c) if k == 2 else P), c, :] for t in (w, q)))
                      for k, (w, q) in enumerate(((w31, q31), (w32, q32), (w33, q33))) for c in range(w.shape[1])]

            def quantise(k, v, dst):
                r = v.shape[0]
                tmp = q_tmp[0:r, 0:v.shape[1]]
                link(dve.tensor_scalar(tmp, v, gam[0:r, 4 + k:5 + k], None, ALU.is_lt))
                link(dve.scalar_tensor_tensor(dst, v, gam[0:r, 8 + k:9 + k], tmp, ALU.is_gt, ALU.subtract))

            for m in range(E + DC):
                if m < E:
                    dve.wait_ge(gated, m + 1)
                else:
                    dve.wait_ge(a_drained, A["oT2"] + m + 1)
                for half in range(2):
                    gated_up(slot(Qs, m) if m < E else slot(Ks, m - E), gate[:, m % 2, :], half)
                if m >= DC:
                    dve.wait_ge(hid2_cut, m - DC + 1)
                    dve.tensor_tensor(hid2_low[:, m - DC, :], slot(Qs, m - DC), hid2_high[:, m - DC, :],
                                      ALU.subtract).then_inc(hid2_split, 1)
                if m == E:
                    dve.wait_ge(ed_cut, 2)
                    dve.tensor_tensor(ed_low[:, E // 2:E], w_ed[:, E // 2:E], ed_high[1][:], ALU.subtract).then_inc(ed_split2, 1)
                if m < len(pieces):
                    quantise(*pieces[m])
            assert len(pieces) <= E + DC
            dve.tensor_copy(gam[:, 11:12], gam[:, 10:11]).then_inc(quantised, 1)
            at("up2")
            for u in range(NT // 2):
                add_down(u)
                dve.wait_ge(d_drained, n[0])
                src = take().rearrange("p (j d) -> p j d", j=2)
                for k in range(2):
                    j = 2 * u + k
                    op = dve.scalar_tensor_tensor(x[:, j, :], src[:, k, :], sig3[:, j, 2:3], x[:, j, :],
                                                  ALU.mult, ALU.add)
                op.then_inc(d_drained, 1)
                stats((2 * u, 2 * u + 2))
                norm((2 * u, 2 * u + 2))

            for c in range(DC):
                dve.wait_ge(a_drained, A["xnT3"] - DC + c + 1)
                dve.tensor_tensor(xn_low[:, c, :], xnT[:, c, :], xn_high[:, c, :], ALU.subtract).then_inc(low3_ready, 1)
            for c in range(DC):
                dve.wait_ge(a_drained, A["xnT3"] + c + 1)
                for half in range(2):
                    biased_times(slot(Qs, 4 + c), slot(Qs, c), half, su[:, 2 * DC + c:2 * DC + c + 1])
                dve.wait_ge(d_drained, n[0])
                dve.tensor_tensor_scan(slot(Qs, 6 + c), onesf[:, 0:1].broadcast_to([P, T]), slot(Qs, 4 + c), 0.0,
                                       ALU.mult, ALU.add).then_inc(cum_ready, 1)
            at("v3")
            for c in range(DC):
                dve.wait_ge(a_drained, A["k3"] + c + 1)
                for half in range(2):
                    biased_times(slot(Qs, c), slot(Qs, 2 + c), half, su[:, c:c + 1])
            at("q3")

            def hidden3_low(m):
                r = f3_rows(m)
                dve.wait_ge(hid_cut, m + 1)
                dve.tensor_tensor(slot(hid_low, m, r), slot(Ks, m, r), slot(hid_high, HIGH_PLACES[m], r),
                                  ALU.subtract).then_inc(hid_split, 1)

            for m in range(F3C):
                dve.wait_ge(a_drained, A["g3"] + m + 1)
                r = f3_rows(m)
                for half in range(2):
                    gated_up(slot(Ks, m, r), gate[0:r, m % 2, :], half)
                if m >= 1:
                    hidden3_low(m - 1)
            hidden3_low(F3C - 1)
            at("up3")
            for u in range(NT // 2):
                add_down(u)
            at("down3")

        @block.tensor
        def _(pe):
            na, nd = [0], [0]

            def a_unit():
                na[0] += 1
                if na[0] > 2:
                    pe.wait_ge(a_drained, na[0] - 2)
                return psA[:, (na[0] - 1) % 2, :]

            def d_unit():
                nd[0] += 1
                bank, drained = d_place(nd[0])
                if drained > 0:
                    pe.wait_ge(d_drained, drained)
                return bank

            def at(name_a, name_d):
                assert name_a is None or na[0] == A[name_a], (name_a, na[0])
                assert name_d is None or nd[0] == DU[name_d], (name_d, nd[0])

            def product(dst, terms, start=True, stop=True):
                for k, (lhsT, rhs) in enumerate(terms):
                    op = pe.matmul(dst, lhsT, rhs, start=start and k == 0, stop=stop and k == len(terms) - 1)
                return op

            def features(weights, rhs, chunks=None):
                dst = a_unit()
                for half in range(2):
                    c = slice(half * HALF, (half + 1) * HALF)
                    terms = [(weights(k), rhs(k, c)) for k in (chunks or range(DC))]
                    op = product(dst[0:terms[0][0].shape[1], c], terms)
                op.then_inc(a_filled, 1)

            def features_half(weights, rhs, half, chunks=None):
                dst = d_unit()
                c = slice(half * HALF, (half + 1) * HALF)
                terms = [(weights(k), rhs(k, c)) for k in (chunks or range(DC))]
                product(dst[0:terms[0][0].shape[1], :], terms).then_inc(d_filled, 1)

            def normed(k, c):
                return xnT[:, k, c]

            def cols(w, a, b):
                return lambda k: w[:, k, a:b]

            def transposed(src, ready=None):
                for c in range(DC):
                    dst = a_unit()
                    for j in range(NT):
                        if ready is not None and c == 0:
                            pe.wait_ge(xn_ready, ready + j + 1)
                        op = pe.transpose(dst[:, tile_cols(j)], src[:, j, c * P:(c + 1) * P], identf[:])
                    op.then_inc(a_filled, 1)

            def value_units(lhsT, rhs, chunks, logits=None):
                for u in range(2):
                    dst = a_unit()
                    beside_ = d_unit() if logits is not None and u == 0 else None
                    for j in range(4):
                        op = product(dst[:, j * D:(j + 1) * D],
                                     [(lhsT(k, tile_cols(4 * u + j)), rhs(k)) for k in chunks])
                        if beside_ is not None:
                            for jj in (2 * j, 2 * j + 1):
                                width = logits.shape[2]
                                last = product(beside_[:, jj * width:(jj + 1) * width],
                                               [(xnT[:, k, tile_cols(jj)], logits[:, k, :]) for k in range(DC)])
                    op.then_inc(a_filled, 1)
                    if beside_ is not None:
                        last.then_inc(d_filled, 1)

            def maxima_unit(i, j, h0, nh, w, part):
                dst = d_unit()
                rows = MLA if is_mla(i) else STACK
                for k in range(nh):
                    h = h0 + k
                    q = head_rows(Qs, i, h, rows, j * P, (j + 1) * P)
                    kk = key_rows(i, h, rows, part * HALF, part * HALF + w)
                    if is_mla(i):
                        q, kk = high(q), high(kk)
                    diagonal = part == (j >= NT // 2)
                    op = pe.matmul(dst[:, k * w:(k + 1) * w], q, kk, start=True, stop=not diagonal)
                    if diagonal:
                        op = pe.matmul(dst[:, (k + 1) * w - P:(k + 1) * w], identb[:], maskq[:], start=False, stop=True)
                op.then_inc(d_filled, 1)

            def maxima_transpose(i, heads):
                pe.wait_ge(max_ready, maxima_of(i))
                dst = d_unit()
                pe.transpose(dst[0:heads * NT, 0:P], mneg[:, 0:heads, :].rearrange("p h j -> p (h j)"),
                             identf[:]).then_inc(d_filled, 1)

            def scores_T(dst, base, k, q, kt, half, second=None, mask=False):
                lo = max(kt * P, half * HALF)
                diagonal = kt * P >= half * HALF
                out_ = dst[:, base + lo - half * HALF:base + HALF]
                if second is not None:
                    pe.matmul(out_, second[0], second[1](lo, (half + 1) * HALF), start=True, stop=False)
                op = pe.matmul(out_, k, q(lo, (half + 1) * HALF), start=second is None, stop=not (diagonal and mask))
                if diagonal and mask:
                    op = pe.matmul(out_[:, 0:P], identb[:], maskk[:], start=False, stop=True)
                return op

            def score_units(i, kt):
                rows = MLA_ONE + 1 if is_mla(i) else STACK + 1

                def one(heads):
                    dst = a_unit()
                    for b, h in enumerate(heads):
                        second = (Kr2[:, tile_cols(kt)], lambda lo, hi: Qr2[i % 2][:, h * T + lo:h * T + hi]) if is_mla(i) else None
                        k = key_rows(i, h, rows, kt * P, (kt + 1) * P)
                        q = lambda lo, hi: head_rows(Qs, i, h, rows, lo, hi)
                        if len(heads) == 1:
                            for half in range(2):
                                op = scores_T(dst, half * HALF, k, q, kt, half, second)
                        else:
                            op = scores_T(dst, b * HALF, k, q, kt, 1, second)
                    op.then_inc(a_filled, 1)
                step = 1 if kt < NT // 2 else 2
                return [list(range(h, h + step)) for h in range(0, GH, step)], one

            def values_product(i, kt, halves):
                s = NT * i + kt
                pe.wait_ge(masked, s + 1)
                if kt == 0 and i > 0:
                    pe.wait_ge(o_drained, i)
                for half in halves:
                    if kt * P >= (half + 1) * HALF:
                        continue
                    lo, hi = max(kt * P, half * HALF), (half + 1) * HALF
                    last_kt = hi // P - 1
                    for h in range(GH):
                        e = Pr[:, ((s % 2) * GH + h) * T + lo:((s % 2) * GH + h) * T + hi]
                        op = pe.matmul(psO[h * VW:(h + 1) * VW, lo:hi], values(i, kt, h), e,
                                       start=kt == 0, stop=kt == last_kt, tile_position=(0, h * VW),
                                       skip_group_check=True)
                if 1 in halves:
                    op.then_inc(pv_done, 1)

            def output_transposes(i):
                pe.wait_ge(o_drained, i + 1)
                for b in range(2):
                    dst = d_unit()
                    for j in range(4):
                        op = pe.transpose(dst[:, tile_cols(j)], OT[:, tile_cols(4 * b + j)], identf[:])
                    op.then_inc(d_filled, 1)

            def arrived(i):
                pe.wait_ge(stack_in[i % 4], stacks(i))
                if is_mla(i):
                    pe.wait_ge(kr_in, 16 * N_KR)
                elif i < 2 * NG:
                    pe.wait_ge(kg_in, 16 * N_KG)

            def attention(groups):
                if groups[0] > 0:
                    arrived(groups[0])
                    for j, part, h0, nh, w in MAX_UNITS:
                        maxima_unit(groups[0], j, h0, nh, w, part)
                    maxima_transpose(groups[0], GH)
                    expert_weights_transpose()
                behind = None
                for i in groups:
                    nxt = i + 1 if i + 1 in groups else None
                    if i == 2 * NG - 2:
                        pe.wait_ge(butterflies, 1)
                        for u in range(FC // 2):
                            pe.matmul(d_unit(), had[:], fT8[:, 2 * u:2 * u + 2, :].rearrange("p c d -> p (c d)"),
                                      start=True, stop=True).then_inc(d_filled, 1)
                    if i == 2 * NG - 1:
                        pe.wait_ge(d_drained, DU[f"o{NG - 1}"])
                        transposed(xn)
                    if is_mla(i):
                        pe.wait_ge(rest_in[i % 2], 16 * REST_DMAS * (i // 2 + 1))
                    pe.wait_ge(mrow_in, 16 * maxima_of(i))
                    for kt in range(NT):
                        heads, one = score_units(i, kt)
                        g, ahead = beside(groups, i, kt)
                        point, points = 0, len(heads) + (0 if behind is None else 1 + (len(heads) > 2))

                        def some_maxima(p):
                            for unit in ahead[p * len(ahead) // points:(p + 1) * len(ahead) // points]:
                                if unit == MAX_UNITS[0]:
                                    arrived(g)
                                j, part, h0, nh, w = unit
                                maxima_unit(g, j, h0, nh, w, part)

                        for k, hs in enumerate(heads):
                            one(hs)
                            if nxt is not None and kt == MAX_END:
                                if k == 1:
                                    maxima_transpose(nxt, GH)
                                    some_maxima(0)
                                    some_maxima(1)
                            else:
                                some_maxima(point)
                            point += 1
                            if behind is not None and k in (1, 2):
                                values_product(*behind, (0, 1) if len(heads) == 2 else (k - 1,))
                                some_maxima(point)
                                point += 1
                        assert point == points
                        behind = (i, kt)
                        if kt == 1 and i - 1 in groups:
                            output_transposes(i - 1)
                        if i == 2 * NG - 1 and kt in DOWN0_AT:
                            pe.wait_ge(a_drained, A["oT0"])
                            down(kt - DOWN0_AT[0], lambda t: [(fT[:, k, t], w_o0[:, k, :]) for k in range(DC)])
                values_product(*behind, (0, 1))
                output_transposes(groups[-1])

            def down(u, terms):
                dst = d_unit()
                for k in range(2):
                    op = product(dst[:, k * D:(k + 1) * D], terms(tile_cols(2 * u + k)))
                op.then_inc(d_filled, 1)

            def expert_weights_transpose():
                pe.wait_ge(comb_ready, 1)
                dst = a_unit()
                comb = lr[:, 6, :].rearrange("p (j e) -> p j e", e=E + 1)
                for j in range(NT):
                    op = pe.transpose(dst[0:E, tile_cols(j)], comb[:, j, 0:E], identf[:])
                op.then_inc(a_filled, 1)

            pe.wait_ge(ident_in, 16)
            transposed(xn, ready=0)
            at("xnT0", None)
            pe.wait_ge(a_drained, A["xnT0"])
            pe.wait_ge(w0_in, 16 * N_W0)
            features(cols(w_lat, 0, P), normed)
            pe.wait_ge(rotated, 2)
            features_half(cols(w_kr, 0, P), normed, 0)
            features_half(cols(w_kr, 0, P), normed, 1)
            pe.wait_ge(a_drained, A["lat"])
            ql = lambda k, c: lat[0:LAT, c]
            kvl = lambda k, c: lat[LAT:P, c]
            for m in range(2):
                features(lambda k: w_u[0:LAT, tile_cols(m)], ql, [0])
            for m in range(2):
                features(lambda k: w_u[LAT:P, tile_cols(m)], kvl, [0])
            value_units(kvl, lambda k: w_vu[LAT:P, :], [0])
            at("v0", "kr")
            pe.wait_ge(q_parts_ready, 2)
            pe.wait_ge(w0b_in, 16 * N_W0B)
            pe.wait_ge(consts_in, 16 * N_CONSTS)
            for item in PRE0:
                if item[0] == "rope":
                    for m in (item[1], H // 2 + item[1]):
                        for half in range(2):
                            c = slice(half * HALF, (half + 1) * HALF)
                            product(d_unit(), [(wq_high[:, tile_cols(m)], lat_parts[:, c]),
                                               (wq_low[0:LAT, tile_cols(m)], lat_parts[0:LAT, c])]).then_inc(d_filled, 1)
                elif item[0] == "router":
                    dst = d_unit()
                    for j in range(NT):
                        op = product(dst[:, j * H:(j + 1) * H],
                                     [(xnT[:, k, tile_cols(j)], w_g0[:, k, :]) for k in range(DC)])
                    op.then_inc(d_filled, 1)
                elif item[0] == "kv":
                    j = item[1]
                    product(d_unit(), [(xnT[:, k, tile_cols(j)], w_qkv0[:, k, D:3 * D]) for k in range(DC)]).then_inc(d_filled, 1)
                elif item[0] == "gq":
                    features(cols(w_qkv0, item[1] * P, (item[1] + 1) * P), normed)
                elif item[0] == "gk":
                    pe.wait_ge(ksel_ready, 1)
                    dst = a_unit()
                    for j in range(NT):
                        op = pe.transpose(dst[0:HD, tile_cols(j)], kvs[:, j, 0, :], identf[:])
                    op.then_inc(a_filled, 1)
                elif item[0] == "max":
                    if item[2] == MAX_UNITS[0]:
                        arrived(0)
                    j, part, h0, nh, w = item[2]
                    maxima_unit(0, j, h0, nh, w, part)
            maxima_transpose(0, GH)
            at("gk", "mrow0")
            attention(GROUPS[0])
            at(f"att{2 * NG - 1}", f"o{2 * NG - 1}")

            transposed(xn, ready=NT)
            pe.wait_ge(a_drained, A["xnT1"])
            pe.wait_ge(w1b_in, 16 * N_W1B)
            features(cols(w_sa, 0, 2 * RANK), normed)
            value_units(normed, lambda k: w_o1[:, k, :], range(DC))
            pe.wait_ge(a_drained, A["qk1"])
            for j, part, w in MAX1:
                dst = d_unit()
                diagonal = part == (j >= NT // 2)
                op = pe.matmul(dst[:, 0:w], high(Q1[0:RANK, tile_cols(j)]), high(K1[0:RANK, part * HALF:part * HALF + w]),
                               start=True, stop=not diagonal)
                if diagonal:
                    op = pe.matmul(dst[:, w - P:w], identb[:], maskq[:], start=False, stop=True)
                op.then_inc(d_filled, 1)
            pe.wait_ge(had_ready, 1)
            features(cols(h256, 0, P), normed)
            maxima_transpose("L1", 1)
            features(cols(h256, P, 2 * P), normed)
            pe.wait_ge(mrow_in, 16 * maxima_of("L1"))
            pe.wait_ge(ones1_ready, 1)
            pe.wait_ge(parts1_ready, 2)
            for kt in range(NT):
                dst = a_unit()
                for half in range(2):
                    if kt * P < (half + 1) * HALF:
                        op = scores_T(dst, half * HALF, K1[0:3 * RANK + 1, tile_cols(kt)],
                                      lambda lo, hi: Q1[0:3 * RANK + 1, lo:hi], kt, half, mask=True)
                op.then_inc(a_filled, 1)
            at("s1", "mrowL1")
            pe.wait_ge(a_drained, A["s1"])
            for j in range(NT):
                dst = d_unit()
                product(dst[:, 0:D + 1], [(slot(Pr, kt)[:, tile_cols(j)], V1[:, kt, :]) for kt in range(j + 1)]).then_inc(d_filled, 1)
            pe.wait_ge(xh_split, DC)
            pe.wait_ge(low1_ready, 2 * DC)
            hadamard = lambda k, c: (xh_high, xh_high, xh_low)[k % 3][:, k // 3, c]
            thrice = lambda h, l, m: (lambda k: (h, l, h)[k % 3][:, k // 3, tile_cols(m)])
            for m in range(FC):
                features(thrice(gt_high, gt_low, m), hadamard, range(3 * DC))
                for half in range(2):
                    features_half(thrice(up_high, up_low, m), hadamard, half, range(3 * DC))
            pe.wait_ge(dn_split, 1)
            for u in range(NT // 2):
                dst = d_unit()
                for k in range(2):
                    t = tile_cols(2 * u + k)
                    for m in range(FC):
                        if u == k == 0 and (m == 0 or m >= FC - 2):
                            pe.wait_ge(hid1_split, max(m + 1, FC - 2))
                        op = product(dst[:, k * D:(k + 1) * D],
                                     [(hid1_high[:, m, t], dn_high[:, m, :]), (hid1_high[:, m, t], dn_low[:, m, :]),
                                      (hid1_low[:, m, t], dn_high[:, m, :])], start=m == 0, stop=m == FC - 1)
                op.then_inc(d_filled, 1)
            at("gate1", "down1")

            transposed(xn, ready=2 * NT)
            pe.wait_ge(a_drained, A["xnT2"])
            pe.wait_ge(w2_in, 16 * N_W2)
            for m in (0, 2, 1, 3):
                features(cols(w_qkv2, m * P, (m + 1) * P), normed)
            value_units(normed, lambda k: w_qkv2[:, k, 2 * D:3 * D], range(DC), w_rt2)
            at("v2", "rt2")
            attention(GROUPS[2])
            pe.wait_ge(gsum_ready, 1)
            pe.matmul(d_unit()[:, 0:4], onesf[:], gam[:, 0:4], start=True, stop=True).then_inc(d_filled, 1)
            pe.wait_ge(d_drained, DU[f"o{LAST}"])
            transposed(xn)
            pe.wait_ge(x2_split, DC)
            parts2 = lambda k, c: (x2_high, x2_high, x2_low)[k % 3][:, k // 3, c]

            def weights2(m, g):
                low = egu_low[:, g] if m < E else (sg_low, su_low)[g][:]
                return lambda k: low[:, k // 3, tile_cols(m % E)] if k % 3 == 1 else piece(m)[:, g, k // 3, :]

            for m in range(E + DC):
                pe.wait_ge(piece_split, m + 1)
                features(weights2(m, 0), parts2, range(3 * DC))
                for half in range(2):
                    features_half(weights2(m, 1), parts2, half, range(3 * DC))
            pe.wait_ge(ed_split, 1)
            pe.wait_ge(ed_split2, 1)
            pe.wait_ge(hid2_split, E)
            pe.wait_ge(a_drained, A["oT2"])
            pe.wait_ge(d_drained, DU["up2"])
            for u in range(NT // 2):
                for terms in (
                        lambda t: [(fT[:, k, t], w_o2[:, k, :]) for k in range(DC)]
                        + [term for e in range(E) for w in (ed_high[e // (E // 2)][:, e % (E // 2), :],)
                           for term in ((hid2_high[:, e, t], w), (hid2_high[:, e, t], ed_low[:, e, :]),
                                        (hid2_low[:, e, t], w))],
                        lambda t: [(slot(Ks, m)[:, t], w_sd[:, m, :]) for m in range(DC)]):
                    dst = d_unit()
                    for k in range(2):
                        op = product(dst[:, k * D:(k + 1) * D], terms(tile_cols(2 * u + k)))
                    op.then_inc(d_filled, 1)

            transposed(xn, ready=3 * NT)
            pe.wait_ge(high3_ready, DC)
            pe.wait_ge(w3_in, 16 * N_W3)
            pe.wait_ge(w3m_in, 16 * N_W3M)
            pe.wait_ge(w3m_split, 1)
            parts3 = lambda k, c: (xn_high, xn_high, xn_low)[k % 3][:, k // 3, c]
            w3 = lambda n, c: (lambda k: (w3m_high, w3m_low, w3m_high)[k % 3][:, n * DC + k // 3, c * P:(c + 1) * P])
            for first, second in ((1, 2), (3, 0)):
                for c in range(DC):
                    if first == 1 and c == 0:
                        dst = a_unit()
                        for chunks in ((0, 1, 3, 4), (2, 5)):
                            if 2 in chunks:
                                pe.wait_ge(low3_ready, DC)
                            for half in range(2):
                                cs = slice(half * HALF, (half + 1) * HALF)
                                op = product(dst[:, cs], [(w3(first, c)(k), parts3(k, cs)) for k in chunks],
                                             start=0 in chunks, stop=2 in chunks)
                        op.then_inc(a_filled, 1)
                    else:
                        features(w3(first, c), parts3, range(3 * DC))
                    for half in range(2):
                        features_half(w3(second, c), parts3, half, range(3 * DC))
            pe.wait_ge(quantised, 1)
            cut = lambda k, c: (xn_high, xn_low)[k // DC][:, k % DC, c]
            twice = lambda w, a, b: (lambda k: w[:, k % DC, a:b])
            for m in range(F3C):
                a, b = m * P, m * P + f3_rows(m)
                features(twice(q31, a, b), cut, range(2 * DC))
                for half in range(2):
                    features_half(twice(q32, a, b), cut, half, range(2 * DC))
            pe.wait_ge(hid_split, F3C - 1)
            pe.wait_ge(y3_ready, DC)
            for u in range(NT // 2):
                dst = d_unit()
                for k in range(2):
                    t = tile_cols(2 * u + k)
                    hidden = lambda ms: [(slot(*h, f3_rows(m))[:, t], q33[0:f3_rows(m), m, :]) for m in ms
                                         for h in ((hid_high, HIGH_PLACES[m]), (hid_low, m))]
                    product(dst[:, k * D:(k + 1) * D], hidden(range(F3C - 1)), stop=False)
                    if u == k == 0:
                        pe.wait_ge(hid_split, F3C)
                    product(dst[:, k * D:(k + 1) * D], hidden((F3C - 1,)), start=False, stop=False)
                    for c in range(DC):
                        op = pe.matmul(dst[:, k * D + c * P:k * D + (c + 1) * P], slot(Qs, 4 + c)[:, t], identf[:],
                                       start=False, stop=c == DC - 1)
                op.then_inc(d_filled, 1)
            at("sig3", "down3")


def constants():
    def bf16(v):
        return (np.ascontiguousarray(v, np.float32).view(np.uint32) >> 16).astype(np.uint16)

    freqs = 1.0 / 10000.0 ** (np.arange(0, RD, 2, dtype=np.float32) / RD)
    ang = np.outer(np.arange(T, dtype=np.float32), freqs)
    table = lambda f: np.ascontiguousarray(np.tile(f(ang), (1, 4)).T.astype(np.float32))
    k = np.arange(D)
    parity = np.array([bin(v).count("1") & 1 for v in range(D)])
    hadamard = (1.0 - 2.0 * parity[k[:, None] & k[None, :]]).astype(np.float32)
    later = np.triu(np.ones((P, P), np.float32), 1) * np.float32(-1e30)
    return {
        "c_ident": np.eye(P, dtype=np.float32), "c_identb": bf16(np.eye(P)),
        "c_had": hadamard[:P, :P] / np.float32(np.sqrt(INTER)),
        "c_h256": hadamard / np.float32(np.sqrt(D)),
        "c_maskq": bf16(later), "c_maskk": bf16(later.T),
        "c_tie": np.tile(np.arange(H, 0, -1, dtype=np.float32), (P, 1)),
        "c_cos": table(np.cos), "c_sin": table(np.sin),
        "c_ones": np.ones((1, T), np.float32), "c_ones4b": bf16(np.ones((1, GH * T))),
    }


def kernel(**inputs):
    import concourse.bacc as bacc
    from concourse.bass_utils import run_bass_kernel_spmd

    a = {k: np.asarray(v) for k, v in inputs.items()}
    col = lambda v: v.reshape(-1, P).T
    flat = lambda v: v.reshape(-1, v.shape[-1])
    arrays = {
        "x": a["L0_attn_x"].reshape(T, D),
        "w_lat": np.concatenate([a["L0_attn_Wqd"], a["L0_attn_Wkvd"]], 1),
        "Wkr": a["L0_attn_Wkr"], "Wqr": a["L0_attn_Wqr"], "Wqu": a["L0_attn_Wqu"], "Wku": a["L0_attn_Wku"],
        "Wvu": a["L0_attn_Wvu"], "Wo0": a["L0_attn_Wo"], "Wg0T": a["L0_ffn_W_gate"].T,
        "Wqkv0T": a["L0_ffn_W_qkv"].T,
        "W_upT": a["L1_ffn_W_up"].T, "W_gateT": a["L1_ffn_W_gate"].T, "W_downT": a["L1_ffn_W_down"].T,
        "Wo1T": a["L1_attn_Wo"].T, "Wsa": np.concatenate([a["L1_attn_Ws"], a["L1_attn_Wa"]], 1),
        "ws_dp": a["L1_ffn_Wscale_dp"].reshape(1, D), "bo": a["L1_attn_bo"].reshape(1, D),
        "su": np.concatenate([col(a["L1_ffn_SU_ug"]), col(a["L1_ffn_SU_dp"]), col(a["L1_ffn_Wscale_ug"])], 1),
        "Wqkv2T": a["L2_attn_w_qkv"].T, "Wo2T": a["L2_attn_w_out"].T,
        "Wrt2T": np.concatenate([a["L2_ffn_gate_w"], a["L2_ffn_se_gate_w"]], 0).T,
        "WegT": flat(a["L2_ffn_w_gate"]).T, "WeuT": flat(a["L2_ffn_w_up"]).T,
        "WsgT": a["L2_ffn_sh_gate"].T, "WsuT": a["L2_ffn_sh_up"].T, "WsdT": a["L2_ffn_sh_down"].T,
        "WedT": flat(a["L2_ffn_w_down"].transpose(0, 2, 1)),
        "Wq3T": a["L3_attn_Wq"].T, "Wk3T": a["L3_attn_Wk"].T, "Wv3T": a["L3_attn_Wv"].T, "Wg3T": a["L3_attn_Wg"].T,
        "b3": np.concatenate([col(a[f"L3_attn_b{n}"]) for n in "qkvg"], 1),
        "w31T": a["L3_ffn_w1"].T, "w32T": a["L3_ffn_w2"].T, "w33T": a["L3_ffn_w3"].T,
        **constants(),
    }
    arrays = {k: np.ascontiguousarray(v) for k, v in arrays.items()}
    nc = bacc.Bacc("TRN2", target_bir_lowering=False, num_devices=1)
    ins = {k: nc.dram_tensor(f"in_{k}", v.shape, mybir.dt.from_np(v.dtype), kind="ExternalInput").ap() for k, v in arrays.items()}
    out = nc.dram_tensor("out", (T, D), F32, kind="ExternalOutput").ap()
    build(nc, ins, out)
    r = run_bass_kernel_spmd(nc, [{f"in_{k}": v for k, v in arrays.items()}], core_ids=[0])
    return np.asarray(r.results[0]["out"]).reshape(1, T, D)
```
